# Optimizing a Trainium2 kernel written in Bass

```python
import numpy as np
import jax
import jax.numpy as jnp

def _softmax(x, axis=-1):
    return jax.nn.softmax(x, axis=axis)

def _gelu(x):
    return jax.nn.gelu(x, approximate=True)

def _silu(x):
    return jax.nn.silu(x)

def _sigmoid(x):
    return jax.nn.sigmoid(x)

def _layernorm(x, axis=-1, eps=1e-05):
    m = jnp.mean(x, axis=axis, keepdims=True)
    v = jnp.var(x, axis=axis, keepdims=True)
    return (x - m) / jnp.sqrt(v + eps)

def _scatter_add(tgt, idx, src, axis=0):
    return tgt.at[idx].add(src)

def _segment_sum(src, seg, n):
    return jax.ops.segment_sum(src, seg, n)
kernel_name = 'mk_gnn_resnorm_d2_gnn_r32_d5edaa'

def setup_inputs(seed: int=0):
    np.random.seed(seed)
    _w = jnp.asarray

    def _rec_inputs():
        import jax
        import jax.numpy as jnp
        _gk = jax.random.key(seed)
        x = -8.776e-05 + 1 * jax.random.normal(jax.random.fold_in(_gk, 1), (3125, 256), jnp.float32)
        src = jax.random.randint(jax.random.fold_in(_gk, 2), (50000,), 0, 3125, jnp.int32)
        dst = jnp.minimum((3125 * jax.random.uniform(jax.random.fold_in(_gk, 3), (50000,)) ** 2.0).astype(jnp.int32), 99999)
        _o = jnp.argsort(dst, stable=True)
        src = src[_o]
        dst = dst[_o]
        edge_type_64 = jax.random.randint(jax.random.fold_in(_gk, 13), (50000,), 0, 64, jnp.int32)
        return (x, src, dst, edge_type_64)
    x, src, dst, edge_type_64 = _rec_inputs()

    def _L0_gnn_setup():
        import jax, jax.numpy as jnp
        import numpy as np
        N = 625
        E = 10000
        IN = 256
        HID = 256
        OUT = 256
        H1 = 8
        D1 = HID // H1
        H2 = 1

        def gat_conv(h, src, dst, fc_w, attn_l, attn_r, bias, heads, out_feats):
            n = h.shape[0]
            feat = (h @ fc_w.T).reshape(n, heads, out_feats)
            el = jnp.sum(feat * attn_l, axis=-1)
            er = jnp.sum(feat * attn_r, axis=-1)
            e = jax.nn.leaky_relu(el[src] + er[dst], 0.2)
            m = jax.ops.segment_max(e, dst, num_segments=n)
            m = jnp.where(jnp.isfinite(m), m, 0.0)
            ex = jnp.exp(e - m[dst])
            ssum = jax.ops.segment_sum(ex, dst, num_segments=n)
            a = ex / ssum[dst]
            rst = jax.ops.segment_sum(feat[src] * a[..., None], dst, num_segments=n)
            return rst + bias.reshape(heads, out_feats)
        key = jax.random.key(seed)
        ks = jax.random.split(key, 16)
        s = 0.05
        inputs = jax.random.normal(ks[0], (N, IN), jnp.float32)
        src = jax.random.randint(ks[1], (E,), 0, N, jnp.int32)
        dst = jax.random.randint(ks[2], (E,), 0, N, jnp.int32)
        return {'inputs': inputs, 'src': src, 'dst': dst, 'fc1_w': jax.random.normal(ks[3], (H1 * D1, IN), jnp.float32) * s, 'attn_l1': jax.random.normal(ks[4], (H1, D1), jnp.float32) * s, 'attn_r1': jax.random.normal(ks[5], (H1, D1), jnp.float32) * s, 'bias1': jax.random.normal(ks[6], (H1 * D1,), jnp.float32) * s, 'fc2_w': jax.random.normal(ks[7], (H2 * OUT, HID), jnp.float32) * s, 'attn_l2': jax.random.normal(ks[8], (H2, OUT), jnp.float32) * s, 'attn_r2': jax.random.normal(ks[9], (H2, OUT), jnp.float32) * s, 'bias2': jax.random.normal(ks[10], (H2 * OUT,), jnp.float32) * s, 'wb0': jax.random.normal(ks[11], (HID, IN), jnp.float32) * s, 'bb0': jax.random.normal(ks[12], (HID,), jnp.float32) * s, 'wb1': jax.random.normal(ks[13], (OUT, IN + HID), jnp.float32) * s, 'bb1': jax.random.normal(ks[14], (OUT,), jnp.float32) * s}
    _L0_gnn_all = _L0_gnn_setup()
    _L0_gnn_in = {k: v for k, v in _L0_gnn_all.items() if k in ('fc1_w', 'attn_l1', 'attn_r1', 'bias1', 'fc2_w', 'attn_l2', 'attn_r2', 'bias2', 'wb0', 'bb0', 'wb1', 'bb1')}
    del _L0_gnn_all

    def _L1_gnn_setup():
        import jax, jax.numpy as jnp
        import numpy as np
        N_NODES = 50000
        N_EDGES = 15625
        IN_DIM = 256
        HID = 64
        HEADS = 4
        N_REL = 64
        key = jax.random.key(seed)
        ks = jax.random.split(key, 16)
        s = 0.02
        return {'node_features': jax.random.normal(ks[0], (N_NODES, IN_DIM), jnp.float32), 'edge_index': jax.random.randint(ks[1], (2, N_EDGES), 0, N_NODES, jnp.int32), 'edge_relations': jax.random.randint(ks[2], (N_EDGES,), 0, N_REL, jnp.int32), 'query_emb': jax.random.normal(ks[3], (IN_DIM,), jnp.float32), 'Wq': jax.random.normal(ks[4], (IN_DIM, HID * HEADS), jnp.float32) * s, 'bq': jnp.zeros((HID * HEADS,), jnp.float32), 'Wk': jax.random.normal(ks[5], (IN_DIM, HID * HEADS), jnp.float32) * s, 'bk': jnp.zeros((HID * HEADS,), jnp.float32), 'Wv': jax.random.normal(ks[6], (IN_DIM, HID * HEADS), jnp.float32) * s, 'bv': jnp.zeros((HID * HEADS,), jnp.float32), 'rel_w': jax.random.normal(ks[7], (N_REL, HID), jnp.float32) * s, 'Wo': jax.random.normal(ks[8], (HID * HEADS, IN_DIM), jnp.float32) * s, 'bo': jnp.zeros((IN_DIM,), jnp.float32), 'gamma': jnp.ones((IN_DIM,), jnp.float32), 'beta': jnp.zeros((IN_DIM,), jnp.float32)}
    _L1_gnn_all = _L1_gnn_setup()
    _L1_gnn_in = {k: v for k, v in _L1_gnn_all.items() if k in ('query_emb', 'Wq', 'bq', 'Wk', 'bk', 'Wv', 'bv', 'rel_w', 'Wo', 'bo', 'gamma', 'beta')}
    del _L1_gnn_all
    return {'x': x, 'src': src, 'dst': dst, 'edge_type_64': edge_type_64, 'L0_gnn_fc1_w': _L0_gnn_in['fc1_w'], 'L0_gnn_attn_l1': _L0_gnn_in['attn_l1'], 'L0_gnn_attn_r1': _L0_gnn_in['attn_r1'], 'L0_gnn_bias1': _L0_gnn_in['bias1'], 'L0_gnn_fc2_w': _L0_gnn_in['fc2_w'], 'L0_gnn_attn_l2': _L0_gnn_in['attn_l2'], 'L0_gnn_attn_r2': _L0_gnn_in['attn_r2'], 'L0_gnn_bias2': _L0_gnn_in['bias2'], 'L0_gnn_wb0': _L0_gnn_in['wb0'], 'L0_gnn_bb0': _L0_gnn_in['bb0'], 'L0_gnn_wb1': _L0_gnn_in['wb1'], 'L0_gnn_bb1': _L0_gnn_in['bb1'], 'L1_gnn_query_emb': _L1_gnn_in['query_emb'], 'L1_gnn_Wq': _L1_gnn_in['Wq'], 'L1_gnn_bq': _L1_gnn_in['bq'], 'L1_gnn_Wk': _L1_gnn_in['Wk'], 'L1_gnn_bk': _L1_gnn_in['bk'], 'L1_gnn_Wv': _L1_gnn_in['Wv'], 'L1_gnn_bv': _L1_gnn_in['bv'], 'L1_gnn_rel_w': _L1_gnn_in['rel_w'], 'L1_gnn_Wo': _L1_gnn_in['Wo'], 'L1_gnn_bo': _L1_gnn_in['bo'], 'L1_gnn_gamma': _L1_gnn_in['gamma'], 'L1_gnn_beta': _L1_gnn_in['beta']}

def reference(x, src, dst, edge_type_64, L0_gnn_fc1_w, L0_gnn_attn_l1, L0_gnn_attn_r1, L0_gnn_bias1, L0_gnn_fc2_w, L0_gnn_attn_l2, L0_gnn_attn_r2, L0_gnn_bias2, L0_gnn_wb0, L0_gnn_bb0, L0_gnn_wb1, L0_gnn_bb1, L1_gnn_query_emb, L1_gnn_Wq, L1_gnn_bq, L1_gnn_Wk, L1_gnn_bk, L1_gnn_Wv, L1_gnn_bv, L1_gnn_rel_w, L1_gnn_Wo, L1_gnn_bo, L1_gnn_gamma, L1_gnn_beta):
    import jax
    import jax.numpy as jnp

    def _L0_gnn_ref(inputs, src, dst, fc1_w, attn_l1, attn_r1, bias1, fc2_w, attn_l2, attn_r2, bias2, wb0, bb0, wb1, bb1):
        import jax, jax.numpy as jnp
        import numpy as np
        N = 625
        E = 10000
        IN = 256
        HID = 256
        OUT = 256
        H1 = 8
        D1 = HID // H1
        H2 = 1

        def gat_conv(h, src, dst, fc_w, attn_l, attn_r, bias, heads, out_feats):
            n = h.shape[0]
            feat = (h @ fc_w.T).reshape(n, heads, out_feats)
            el = jnp.sum(feat * attn_l, axis=-1)
            er = jnp.sum(feat * attn_r, axis=-1)
            e = jax.nn.leaky_relu(el[src] + er[dst], 0.2)
            m = jax.ops.segment_max(e, dst, num_segments=n)
            m = jnp.where(jnp.isfinite(m), m, 0.0)
            ex = jnp.exp(e - m[dst])
            ssum = jax.ops.segment_sum(ex, dst, num_segments=n)
            a = ex / ssum[dst]
            rst = jax.ops.segment_sum(feat[src] * a[..., None], dst, num_segments=n)
            return rst + bias.reshape(heads, out_feats)
        n = inputs.shape[0]
        deg = jax.ops.segment_sum(jnp.ones_like(dst, jnp.float32), dst, num_segments=n)
        norm = (1.0 / jnp.clip(deg, 1.0, None))[:, None]
        h0 = gat_conv(inputs, src, dst, fc1_w, attn_l1, attn_r1, bias1, H1, D1)
        h0 = h0.reshape(n, H1 * D1)
        h1 = jax.nn.relu(h0 + norm * (inputs @ wb0.T + bb0))
        h2 = gat_conv(h1, src, dst, fc2_w, attn_l2, attn_r2, bias2, H2, OUT)
        h2 = h2.mean(axis=1)
        cat = jnp.concatenate([inputs, h1], axis=-1)
        return h2 + norm * (cat @ wb1.T + bb1)

    def _L1_gnn_ref(node_features, edge_index, edge_relations, query_emb, Wq, bq, Wk, bk, Wv, bv, rel_w, Wo, bo, gamma, beta):
        import jax, jax.numpy as jnp
        import numpy as np
        N_NODES = 50000
        N_EDGES = 15625
        IN_DIM = 256
        HID = 64
        HEADS = 4
        N_REL = 64
        N = node_features.shape[0]
        D = rel_w.shape[1]
        H = Wq.shape[1] // D
        enh = node_features + 0.1 * query_emb[None, :]
        Q = (enh @ Wq + bq).reshape(N, H, D)
        K = (enh @ Wk + bk).reshape(N, H, D)
        V = (enh @ Wv + bv).reshape(N, H, D)
        src, dst = (edge_index[0], edge_index[1])
        rel = rel_w[edge_relations]
        mod_k = K[src] + 0.2 * rel[:, None, :]
        scores = jnp.einsum('ehd,ehd->eh', Q[dst], mod_k) / D ** 0.5
        seg_max = jax.ops.segment_max(scores, dst, num_segments=N)
        ex = jnp.exp(scores - seg_max[dst])
        denom = jax.ops.segment_sum(ex, dst, num_segments=N)
        w = ex / denom[dst]
        agg = jax.ops.segment_sum(w[:, :, None] * V[src], dst, num_segments=N)
        deg = jax.ops.segment_sum(jnp.ones((src.shape[0],), jnp.float32), dst, num_segments=N)
        msgs = jnp.where(deg[:, None, None] > 0, agg, V)
        out = msgs.reshape(N, H * D) @ Wo + bo
        x = out + node_features
        mu = jnp.mean(x, axis=-1, keepdims=True)
        var = jnp.var(x, axis=-1, keepdims=True)
        return (x - mu) / jnp.sqrt(var + 1e-05) * gamma + beta
    edge_index = jnp.stack([src, dst])
    x = _layernorm(x + _L0_gnn_ref(x, src, dst, L0_gnn_fc1_w, L0_gnn_attn_l1, L0_gnn_attn_r1, L0_gnn_bias1, L0_gnn_fc2_w, L0_gnn_attn_l2, L0_gnn_attn_r2, L0_gnn_bias2, L0_gnn_wb0, L0_gnn_bb0, L0_gnn_wb1, L0_gnn_bb1), axis=-1)
    x = _layernorm(x + _L1_gnn_ref(x, edge_index, edge_type_64, L1_gnn_query_emb, L1_gnn_Wq, L1_gnn_bq, L1_gnn_Wk, L1_gnn_bk, L1_gnn_Wv, L1_gnn_bv, L1_gnn_rel_w, L1_gnn_Wo, L1_gnn_bo, L1_gnn_gamma, L1_gnn_beta), axis=-1)
    return x

_drawn_inputs = setup_inputs


def setup_inputs(seed=0):
    import zlib

    import numpy as np

    out = dict(_drawn_inputs(seed))
    spreads = {'L1_gnn_bq': (0.0, 0.8),
     'L1_gnn_bk': (0.0, 2.0),
     'L1_gnn_bv': (0.0, 0.509),
     'L1_gnn_bo': (0.0, 0.1),
     'L1_gnn_gamma': (1.0, 0.2),
     'L1_gnn_beta': (0.0, 0.1)}
    factors = {'L0_gnn_attn_l1': 5.464,
     'L0_gnn_attn_r1': 8.0,
     'L0_gnn_bias1': 2.768,
     'L0_gnn_attn_l2': 8.0,
     'L0_gnn_attn_r2': 8.0,
     'L0_gnn_wb0': 3.184,
     'L0_gnn_bb0': 8.0,
     'L0_gnn_bb1': 8.0,
     'L1_gnn_query_emb': 8.0,
     'L1_gnn_Wq': 8.0,
     'L1_gnn_Wk': 8.0,
     'L1_gnn_Wv': 3.175,
     'L1_gnn_rel_w': 64.0}
    for name, (base, spread) in spreads.items():
        noise = np.random.default_rng([zlib.crc32(name.encode()), seed]).standard_normal(out[name].shape)
        drawn = base * np.exp(spread * noise) if base else spread * noise
        out[name] = jnp.asarray(drawn.astype(out[name].dtype))
    for name, factor in factors.items():
        out[name] = (out[name] * factor).astype(out[name].dtype)
    return out
```

```python
import numpy as np
import concourse.bass as bass
from concourse import mybir
from contextlib import ExitStack

F32 = mybir.dt.float32
I32 = mybir.dt.int32
ALU = mybir.AluOpType
ACT = mybir.ActivationFunctionType
AX = mybir.AxisListType

P = 128
N, E, D, R = 3125, 50000, 256, 64
BLOCKS = -(-N // P)
NP = BLOCKS * P
TILES = -(-E // P)
TCH = -(-TILES // P)
GROUP = 8
SLOTS = 4
STEP = GROUP * SLOTS
ITEMS = -(-(TILES + BLOCKS - 1) // STEP) * STEP
GROUPS = ITEMS // GROUP
TURNS = ITEMS // STEP
ICH = -(-ITEMS // P)
LAST = ITEMS - (ICH - 1) * P
H1, H2, H3 = 8, 1, 4
UB = 5
BTURNS = BLOCKS // UB
BIG = 1.0e30
PAD_DST = NP - 1
DEG = D + H1
AW = DEG + 1
EPS = 1e-5


class Count:

    def __init__(self, sem):
        self.sem, self.n, self.turn, self.per, self.at = sem, 0, None, 0, 0

    def enter(self, turn, per):
        self.turn, self.per, self.at = turn, per, self.n

    def leave(self, turns):
        assert self.n - self.at == self.per, (self.n - self.at, self.per)
        self.n = self.at + self.per * turns
        self.turn = None

    def add(self, k=1):
        self.n += k

    def value(self):
        return self.n if self.turn is None else self.turn * self.per + self.n


def graph_layers(nc, a, out):
    ctx = ExitStack()
    with ctx:
        def sb(name, shape, dt=F32):
            return ctx.enter_context(nc.sbuf_tensor(name, shape, dt))

        def sem(name):
            return ctx.enter_context(nc.semaphore(name))

        def dram(name, shape, dt=F32):
            return nc.dram_tensor(name, shape, dt).ap()

        tab_feat1 = dram("tab_feat1", (NP, D))
        tab_feat2 = dram("tab_feat2", (NP, D))
        tab_k = dram("tab_k", (NP, D))
        tab_v = dram("tab_v", (NP, D))
        row_names = ["dst", "block_dst", "src_low", "type"]
        rows_d = {k: dram("rows_" + k, (ITEMS, P)) for k in row_names}

        ident = sb("ident", [P, P])
        below = sb("below", [P, P])
        ones = sb("ones", [P, P])
        iota_free = sb("iota_free", [P, ITEMS])
        neg_part = sb("neg_part", [P, 1])
        tile_no = sb("tile_no", [P, TCH])
        eps_col = sb("eps_col", [P, 1])
        src_i = sb("src_i", [P, ITEMS], I32)
        src_hi = sb("src_hi", [P, ITEMS])
        block_dst = sb("block_dst", [P, ITEMS])
        block_i = sb("block_i", [P, ITEMS], I32)
        el = sb("el", [P, BLOCKS * H1])
        er = sb("er", [P, BLOCKS, H1])
        deg = sb("deg", [P, BLOCKS])
        acc = sb("acc", [P, BLOCKS, AW])
        base = sb("base", [P, BLOCKS, D])
        queries = sb("queries", [P, BLOCKS, D])
        scores = sb("scores", [P, ITEMS * H1])

        def by_item(heads):
            return scores[:, 0:ITEMS * heads].rearrange("p (h i) -> p i h", h=heads)

        rows = sb("rows", [P, SLOTS, GROUP, D])
        index_slot = sb("index_slot", [P, SLOTS, GROUP], I32)
        w_a = sb("w_a", [P, 2, 3 * D])
        w_b = sb("w_b", [P, 2, D])
        w_el = sb("w_el", [P, 2, 2, H1])
        bias_row = sb("bias_row", [1, 3 * D])
        bias_all = sb("bias_all", [P, 2, D])
        rel_sb = sb("rel_sb", [R, R])
        query_col = sb("query_col", [P, 2])
        chunk_row = sb("chunk_row", [1, 12, P])
        chunk_col = sb("chunk_col", [P, 4])

        ARENA = 13900
        arena = sb("arena", [P, ARENA])

        def views(*sizes):
            got, at = [], 0
            for n in sizes:
                got.append(arena[:, at:at + n])
                at += n
            assert at <= ARENA
            return got

        ps = ctx.enter_context(nc.psum_tensor("ps", [P, 8, 512], F32))

        v = views(3 * TCH * P, 3 * TCH * P, TCH * ITEMS, TCH * ITEMS, ITEMS, 4 * ITEMS, 4 * TCH * P, 12 * TCH)
        tiles_i = v[0].bitcast(I32).rearrange("p (a c e) -> p a c e", a=3, c=TCH)
        tiles_f = v[1].rearrange("p (a c e) -> p a c e", a=3, c=TCH)
        sel = v[2].rearrange("p (c i) -> p c i", c=TCH)
        bsel = v[3].rearrange("p (c i) -> p c i", c=TCH)
        item_tmp = v[4]
        item_f = v[5].rearrange("p (a i) -> p a i", a=4)
        rows_t = v[6].rearrange("p (a c e) -> p a c e", a=4, c=TCH)
        tile_s = v[7].rearrange("p (k c) -> p k c", k=12)
        v = views(4 * GROUP * P, 4 * GROUP * P, 2 * GROUP * 32, 2 * GROUP * AW)
        bcast = v[0].rearrange("p (s a e) -> p s a e", s=2, a=2)
        onehot_t = v[1].rearrange("p (s a e) -> p s a e", s=2, a=2)
        hi_onehot = v[2].rearrange("p (s g d) -> p s g d", s=2, g=GROUP)
        product = v[3].rearrange("p (s g d) -> p s g d", s=2, g=GROUP)
        v = views(2 * GROUP * P, 2 * GROUP * AW)
        onehot = v[0].rearrange("p (s g d) -> p s g d", s=2, g=GROUP)
        weighted = v[1].rearrange("p (s g d) -> p s g d", s=2, g=GROUP)
        seg = views(*[ITEMS * H1 + 8] * 4)
        v = views(UB * 2 * P, UB * D, UB * 2 * P, UB * 2 * D, UB * D, UB * D, UB * 40, 2 * D)
        x_t = v[0].rearrange("p (j k n) -> p j k n", j=UB, k=2)
        x_n = v[1].rearrange("p (j d) -> p j d", j=UB)
        h_t = v[2].rearrange("p (j k n) -> p j k n", j=UB, k=2)
        stage = v[3].rearrange("p (j a d) -> p j a d", j=UB, a=2)
        h_n = v[4].rearrange("p (j d) -> p j d", j=UB)
        tmp_n = v[5].rearrange("p (j d) -> p j d", j=UB)
        small = v[6].rearrange("p (j k) -> p j k", j=UB)
        attn = v[7].rearrange("p (a d) -> p a d", a=2)

        edges_in = sem("edges_loaded")
        consts = sem("constants_made")
        weights_in = [sem(f"weights_loaded{k}") for k in range(4)]
        edge_pe = sem("edge_products")
        edge_dve = sem("edge_vectors")
        rows_stored = sem("item_rows_stored")
        phase = {k: sem("stage_done_" + k) for k in ["pe", "act", "dve", "sp"]}
        dve_step, act_step, pool_step = sem("dve_step"), sem("act_step"), sem("pool_step")
        x_loaded = [sem(f"node_inputs_loaded{j}") for j in range(UB)]
        h_made = sem("node_rows_made")
        t_made = sem("node_transposes_made")
        ht_copied = sem("node_transposes_copied")
        node_mm = sem("node_products_made")
        node_dve = sem("node_products_read_dve")
        node_act = sem("node_products_read_act")
        node_stored = [sem(f"node_rows_stored{j}") for j in range(UB)]
        variance, deviation = sem("variance_made"), sem("deviation_made")
        gathered = [sem(f"rows_gathered{s}") for s in range(SLOTS)]
        slot_claimed = sem("rows_slot_claimed")
        stats_made = sem("row_statistics_made")
        slot_used = [sem(f"rows_used{s}") for s in range(SLOTS)]
        bcast_in = [sem(f"item_rows_broadcast{s}") for s in range(2)]
        onehot_made = [sem(f"onehot_made{s}") for s in range(2)]
        score_mm = [sem(f"score_products_made{s}") for s in range(2)]
        score_read = [sem(f"score_products_read{s}") for s in range(2)]
        pair_mm = sem("pair_products_made")
        pair_read = sem("pair_products_read")
        seg_in = sem("segment_rows_loaded")
        seg_t = sem("score_transposes_made")
        seg_copied = sem("score_transposes_copied")
        seg_small = sem("chunk_rows_made")
        seg_dve = sem("chunk_rows_used")
        seg_exp = sem("numerators_made")
        seg_back = sem("numerators_transposed")
        weighted_made = sem("weighted_rows_made")
        sum_mm = sem("sums_made")
        sum_added = sem("sums_added")
        block = ctx.enter_context(nc.Block())

        STAGES = ["items", "node1", "score1", "soft1", "sum1", "node2", "score2", "soft2", "sum2",
                  "node3", "score3", "soft3", "sum3", "final"]

        def begin(eng, name, others):
            k = STAGES.index(name)
            for o in others:
                if k:
                    eng.wait_ge(phase[o], k)

        x_t_d = a["x_t"].rearrange("(k p) n -> p k n", k=2)

        def halves(w):
            return w.rearrange("(k p) n -> p k n", k=2)

        def nth(u, s):
            return u * (SLOTS // 2) + s // 2

        HALF = GROUPS // 2

        @block.sync
        def _(sp):
            def end():
                sp.sem_inc(phase["sp"], 1)

            sp.wait_ge(consts, 1)
            full, tail = E // P, E % P
            for k, name in enumerate(["src", "dst", "edge_type_64"]):
                v = a[name]
                w = v[0:(TCH - 1) * P * P].rearrange("(c p e) -> p c e", c=TCH - 1, e=P)
                sp.dma_start(tiles_i[:, k, 0:TCH - 1, :], w).then_inc(edges_in, 16)
                m = full - (TCH - 1) * P
                w = v[(TCH - 1) * P * P:full * P].rearrange("(p e) -> p e", e=P)
                sp.dma_start(tiles_i[0:m, k, TCH - 1, :], w).then_inc(edges_in, 16)
                w = v[full * P:E].rearrange("(p e) -> p e", p=1)
                sp.dma_start(tiles_i[m:m + 1, k, TCH - 1, 0:tail], w).then_inc(edges_in, 16)
            sp.dma_start(w_a[:, :, 0:D], halves(a["fc1_t"])).then_inc(weights_in[0], 16)
            sp.dma_start(w_a[:, :, D:2 * D], halves(a["wb0_t"])).then_inc(weights_in[0], 16)
            sp.dma_start(bias_row[:, D:2 * D], a["bb0"]).then_inc(weights_in[0], 16)
            sp.wait_ge(edge_dve, 4)
            for k, name in enumerate(row_names):
                w = rows_d[name][0:(ICH - 1) * P, :].rearrange("(c p) e -> p c e", p=P)
                sp.dma_start(w, rows_t[:, k, 0:ICH - 1, :]).then_inc(rows_stored, 16)
                sp.dma_start(rows_d[name][(ICH - 1) * P:ITEMS, :],
                             rows_t[0:LAST, k, ICH - 1, :]).then_inc(rows_stored, 16)
            sp.wait_ge(rows_stored, 2 * 4 * 16)
            end()

            def node(name, turns_before, loads, stores, last_rows=None):
                def turn(t, b0):
                    for j in range(UB):
                        if loads:
                            sp.wait_ge(node_mm, t + turns_before)
                            sp.wait_ge(node_dve, t + turns_before)
                            loads(j, b0 + j)
                    if stores:
                        sp.wait_ge(node_act, t + (turns_before + 1))
                        for j in range(UB):
                            stores(j, b0 + j)
                with nc.sync.Fori(0, BTURNS) as t:
                    turn(t, t * UB)

            begin(sp, "node1", ["dve", "pe", "act"])
            for k, name in enumerate(["attn_l1", "attn_r1"]):
                sp.dma_start(attn[:, k, :], a[name].broadcast_to([P, D])).then_inc(weights_in[0], 16)

            def load_xt(j, b):
                sp.dma_start(x_t[:, j], x_t_d[:, :, bass.ds(b * P, P)]).then_inc(x_loaded[j], 16)

            def load_x(j, b):
                sp.dma_start(x_n[:, j], a["x"][bass.ds(b * P, P), :]).then_inc(x_loaded[j], 16)

            def load_v(j, b):
                sp.dma_start(stage[:, j, 1], tab_v[bass.ds(b * P, P), :]).then_inc(x_loaded[j], 16)

            def store(table, part):
                def go(j, b):
                    sp.dma_start(table[bass.ds(b * P, P), :], stage[:, j, part]).then_inc(node_stored[j], 16)
                return go

            def store_kv(j, b):
                store(tab_k, 0)(j, b)
                store(tab_v, 1)(j, b)

            def stored(count):
                for j in range(UB):
                    sp.wait_ge(node_stored[j], 16 * count)

            node("node1", 0, load_xt, store(tab_feat1, 0))
            stored(BTURNS)
            end()

            def score_rows(layer, name, first):
                begin(sp, name, ["dve", "pe", "act"])
                flat = [rows_d[x].rearrange("i e -> (i e)") for x in (first, "block_dst")]
                with nc.sync.Fori(0, TURNS) as u:
                    for s in range(SLOTS):
                        sp.wait_ge(onehot_made[s % 2], nth(u, s) + layer * HALF)
                        for k in range(2):
                            row = flat[k][bass.ds(u * (STEP * P) + s * GROUP * P, GROUP * P)]
                            sp.dma_start(bcast[:, s % 2, k], row.partition_broadcast(P)).then_inc(bcast_in[s % 2], 16)
                end()

            def seg_rows(name, heads, chunks):
                begin(sp, name, ["dve", "pe", "act"])
                n = ITEMS // chunks * P
                row = rows_d["dst"].rearrange("(c j) e -> c (j e)", c=chunks)
                for h in range(heads):
                    sp.dma_start(seg[0][h * chunks:(h + 1) * chunks, 0:n], row).then_inc(seg_in, 16)
                end()

            score_rows(0, "score1", "src_low")
            seg_rows("soft1", H1, P // H1)
            begin(sp, "sum1", [])
            end()

            begin(sp, "node2", ["dve", "pe", "act"])
            sp.dma_start(w_a[:, :, 0:D], halves(a["fc2_t"])).then_inc(weights_in[1], 16)
            sp.dma_start(w_a[:, :, D:2 * D], halves(a["wb1_t"][D:2 * D, :])).then_inc(weights_in[1], 16)
            sp.dma_start(w_b[:], halves(a["wb1_t"][0:D, :])).then_inc(weights_in[1], 16)
            sp.dma_start(bias_row[:, D:2 * D], a["bb1"]).then_inc(weights_in[1], 16)
            sp.dma_start(bias_all[:, 0, :], a["bias1"].broadcast_to([P, D])).then_inc(weights_in[1], 16)
            for k, name in enumerate(["attn_l2", "attn_r2"]):
                sp.dma_start(attn[:, k, :], a[name].broadcast_to([P, D])).then_inc(weights_in[1], 16)
            node("node2", BTURNS, load_xt, store(tab_feat2, 0))
            stored(2 * BTURNS)
            end()
            score_rows(1, "score2", "src_low")
            seg_rows("soft2", H2, ITEMS // 4)
            begin(sp, "sum2", [])
            end()

            begin(sp, "node3", ["dve", "pe", "act"])
            for k, name in enumerate(["wq", "wk", "wv"]):
                sp.dma_start(w_a[:, :, k * D:(k + 1) * D], halves(a[name])).then_inc(weights_in[2], 16)
            for k, name in enumerate(["bq", "bk", "bv"]):
                sp.dma_start(bias_row[:, k * D:(k + 1) * D], a[name]).then_inc(weights_in[2], 16)
            sp.dma_start(bias_all[:, 0, :], a["bias2"].broadcast_to([P, D])).then_inc(weights_in[2], 16)
            sp.dma_start(query_col[:], a["query"]).then_inc(weights_in[2], 16)
            sp.dma_start(rel_sb[:], a["rel"]).then_inc(weights_in[2], 16)
            node("node3", 2 * BTURNS, load_x, store_kv)
            stored(4 * BTURNS)
            end()
            score_rows(2, "score3", "type")
            seg_rows("soft3", H3, P // H3)
            begin(sp, "sum3", [])
            end()

            begin(sp, "final", ["dve", "pe", "act"])
            sp.dma_start(w_b[:], halves(a["wo"])).then_inc(weights_in[3], 16)
            sp.dma_start(bias_row[:, 0:D], a["bo"]).then_inc(weights_in[3], 16)
            for k, name in enumerate(["gamma", "beta"]):
                sp.dma_start(bias_all[:, k, :], a[name].broadcast_to([P, D])).then_inc(weights_in[3], 16)

            def final_turn(t, b0, last):
                for j in range(UB):
                    sp.wait_ge(node_dve, t + 3 * BTURNS)
                    load_v(j, b0 + j)
                sp.wait_ge(node_dve, t + (3 * BTURNS + 1))
                for j in range(UB):
                    m = N - (BLOCKS - 1) * P if last and j == UB - 1 else P
                    sp.dma_start(out[bass.ds((b0 + j) * P, m), :], h_n[0:m, j]).then_inc(node_stored[j], 16)

            with nc.sync.Fori(0, BTURNS - 1) as t:
                final_turn(t, t * UB, False)
            final_turn(BTURNS - 1, (BTURNS - 1) * UB, True)
            stored(5 * BTURNS)

        @block.gpsimd
        def _(pool):
            step = Count(pool_step)

            def did(ins):
                ins.then_inc(pool_step, 1)
                step.add()
                pool.wait_ge(pool_step, step.value())

            did(nc.gpsimd.memset(tiles_i[:, :, TCH - 1, :], 0))
            did(nc.gpsimd.memset(tiles_i[:, 1, TCH - 1, :], PAD_DST))
            pool.sem_inc(consts, 1)
            nc.gpsimd.memset(ones[:], 1.0)
            nc.gpsimd.memset(eps_col[:], EPS)
            did(nc.gpsimd.memset(ident[:], 0.0))
            nc.gpsimd.affine_select(out=ident[:], in_=ident[:], compare_op=ALU.not_equal, fill=1.0, base=0,
                                    pattern=[[1, P]], channel_multiplier=-1)
            nc.gpsimd.affine_select(out=below[:], in_=ones[:], compare_op=ALU.is_gt, fill=0.0, base=0,
                                    pattern=[[1, P]], channel_multiplier=-1)
            nc.gpsimd.iota(iota_free[:], [[1, ITEMS]], base=0, channel_multiplier=0,
                           allow_small_or_imprecise_dtypes=True)
            nc.gpsimd.iota(neg_part[:], [[0, 1]], base=0, channel_multiplier=-1,
                           allow_small_or_imprecise_dtypes=True)
            did(nc.gpsimd.iota(tile_no[:], [[P, TCH]], base=0, channel_multiplier=1,
                               allow_small_or_imprecise_dtypes=True))
            pool.sem_inc(consts, 1)

            def gathers(nth_pass, table, name):
                k = STAGES.index(name)
                pool.wait_ge(phase["sp"], k + 1)
                with nc.gpsimd.Fori(0, TURNS) as u:
                    step.enter(u, SLOTS)
                    for s in range(SLOTS):
                        pool.wait_ge(gathered[s], (u + nth_pass * TURNS) * (16 * GROUP))
                        did(nc.gpsimd.tensor_copy(index_slot[:, s], src_i[:, bass.ds(u * STEP + s * GROUP, GROUP)]))
                        pool.wait_ge(slot_used[s], u + nth_pass * TURNS)
                        pool.sem_inc(slot_claimed, 1)
                        for g in range(GROUP):
                            nc.gpsimd.indirect_dma_start(
                                rows[:, s, g, :], None, table,
                                bass.IndirectOffsetOnAxis(ap=index_slot[:, s, g:g + 1], axis=0),
                            ).then_inc(gathered[s], 16)
                    step.leave(TURNS)

            gathers(0, tab_feat1, "node1")
            gathers(1, tab_feat2, "node2")
            gathers(2, tab_k, "node3")
            gathers(3, tab_v, "node3")

        @block.tensor
        def _(pe):
            def end():
                pe.sem_inc(phase["pe"], 1)

            pe.wait_ge(consts, 2)
            pe.wait_ge(edge_dve, 1)
            nc.tensor.matmul(ps[:, 0, 0:TCH], below[:], tile_s[:, 4, :], start=True, stop=True)
            nc.tensor.matmul(ps[:, 1, 0:TCH], ones[:], tile_s[:, 4, :], start=True, stop=True).then_inc(edge_pe, 1)
            pe.wait_ge(edge_dve, 2)
            for k in range(5):
                for c in range(TCH):
                    lhs = tiles_f[:, k, c, :] if k < 3 else ones[:]
                    rhs = bsel[:, c, :] if k == 3 else sel[:, c, :]
                    last = nc.tensor.matmul(ps[:, k, 0:ITEMS], lhs, rhs, start=c == 0, stop=c == TCH - 1)
            last.then_inc(edge_pe, 1)
            pe.wait_ge(edge_dve, 3)
            for k in range(4):
                w = item_f[:, k, :] if k != 1 else block_dst[:]
                for c in range(ICH):
                    m = P if c < ICH - 1 else LAST
                    last = nc.tensor.transpose(ps[0:m, k, c * P:(c + 1) * P], w[:, c * P:c * P + m], ident[:])
            last.then_inc(edge_pe, 1)
            pe.wait_ge(edge_pe, 3)
            end()

            begin(pe, "node1", ["dve", "act"])
            pe.wait_ge(weights_in[0], 5 * 16)
            pe.wait_ge(edge_dve, 5)
            with nc.tensor.Fori(0, BTURNS) as t:
                for j in range(UB):
                    pe.wait_ge(x_loaded[j], (t + 1) * 16)
                    if j == 0:
                        pe.wait_ge(node_dve, t)
                        pe.wait_ge(node_act, t)
                    for k in range(2):
                        nc.tensor.matmul(ps[:, j, :], x_t[:, j, k, :], w_a[:, k, 0:2 * D], start=k == 0, stop=False)
                    nc.tensor.matmul(ps[:, j, D:2 * D], ones[0:1, :], bias_row[:, D:2 * D], start=False, stop=True)
                    for k in range(2):
                        last = nc.tensor.matmul(ps[:, 7, 256 + 16 * j:272 + 16 * j], x_t[:, j, k, :],
                                                w_el[:, k].rearrange("p a h -> p (a h)"), start=k == 0, stop=k == 1)
                last.then_inc(node_mm, 1)
            pe.wait_ge(node_mm, BTURNS)
            end()

            regs = [pe.alloc_register(f"pe_block{g}") for g in range(GROUP)]

            def blocks(u, s):
                pe.load(regs, block_i[0:1, bass.ds(u * STEP + s * GROUP, GROUP)])
                return [pe.snap(r, min_val=0, max_val=BLOCKS - 1) for r in regs]

            def gat_scores(layer, name, heads):
                begin(pe, name, ["dve", "act", "sp"])
                w = BLOCKS * heads
                with nc.tensor.Fori(0, TURNS) as u:
                    for s in range(SLOTS):
                        bs = blocks(u, s)
                        pe.wait_ge(onehot_made[s % 2], nth(u, s) + (layer * HALF + 1))
                        pe.wait_ge(score_read[s % 2], nth(u, s) + layer * HALF)
                        for g in range(GROUP):
                            bank, at = s % 2 * 4 + g // 2, g % 2 * (w + heads)
                            e = slice(g * P, (g + 1) * P)
                            nc.tensor.matmul(ps[:, bank, at:at + w], onehot_t[:, s % 2, 0, e], el[:, 0:w],
                                             start=True, stop=True)
                            last = nc.tensor.matmul(ps[:, bank, at + w:at + w + heads], onehot_t[:, s % 2, 1, e],
                                                    er[:, bass.ds(bs[g], 1), 0:heads].rearrange("p a h -> p (a h)"),
                                                    start=True, stop=True)
                        last.then_inc(score_mm[s % 2], 1)
                for s in range(2):
                    pe.wait_ge(score_mm[s], (layer + 1) * HALF)
                end()

            def pair_scores(layer, name):
                begin(pe, name, ["dve", "act", "sp"])
                with nc.tensor.Fori(0, TURNS) as u:
                    for s in range(SLOTS):
                        bs = blocks(u, s)
                        pe.wait_ge(onehot_made[s % 2], nth(u, s) + (layer * HALF + 1))
                        for g in range(GROUP):
                            pe.wait_ge(pair_read, u * STEP + (s * GROUP + g + 1))
                            e = slice(g * P, (g + 1) * P)
                            nc.tensor.matmul(ps[:, g, 0:D], onehot_t[:, s % 2, 1, e],
                                             queries[:, bass.ds(bs[g], 1), :].rearrange("p a d -> p (a d)"),
                                             start=True, stop=True)
                            nc.tensor.matmul(ps[:, g, D:D + R], onehot_t[0:R, s % 2, 0, e], rel_sb[:],
                                             start=True, stop=True).then_inc(pair_mm, 1)
                pe.wait_ge(pair_mm, ITEMS)
                end()

            def soft(n, name, heads, chunks):
                begin(pe, name, ["dve", "act"])
                each = ITEMS // chunks
                m = heads * chunks
                for j in range(each):
                    last = nc.tensor.transpose(ps[0:m, j // 4, j % 4 * P:(j % 4 + 1) * P],
                                               scores[:, j:ITEMS * heads:each], ident[:])
                last.then_inc(seg_t, 1)
                pe.wait_ge(seg_dve, 3 * n + 1)
                for k in range(4):
                    last = nc.tensor.matmul(ps[0:1, 0, k * P:k * P + m], chunk_col[0:m, k:k + 1], ident[0:m, 0:m],
                                            start=True, stop=True)
                last.then_inc(seg_small, 1)
                pe.wait_ge(seg_dve, 3 * n + 2)
                for k in range(2):
                    last = nc.tensor.matmul(ps[0:m, 1, k:k + 1], chunk_row[:, 8 + k, 0:m], ones[0:1, 0:1],
                                            start=True, stop=True)
                last.then_inc(seg_small, 1)
                pe.wait_ge(seg_exp, n + 1)
                for j in range(each):
                    last = nc.tensor.transpose(ps[:, j // 4, j % 4 * m:(j % 4 + 1) * m],
                                               seg[1][0:m, j * P:(j + 1) * P], ident[0:m, 0:m])
                last.then_inc(seg_back, 1)
                pe.wait_ge(seg_back, n + 1)
                end()

            def sums(n, name, heads, width):
                begin(pe, name, ["dve", "act"])
                with nc.tensor.Fori(0, TURNS) as u:
                    for s in range(SLOTS):
                        pe.wait_ge(weighted_made, u * SLOTS + (s + 1 + n * GROUPS))
                        for g in range(GROUP):
                            pe.wait_ge(sum_added, u * STEP + (s * GROUP + g + 1 + n * (ITEMS + GROUP)))
                            nc.tensor.matmul(ps[:, g, 0:width], onehot[:, s % 2, g, :], weighted[:, s % 2, g, 0:width],
                                             start=True, stop=True).then_inc(sum_mm, 1)
                pe.wait_ge(sum_mm, (n + 1) * ITEMS)
                end()

            def transposes(turn):
                pe.wait_ge(h_made, turn + 1)
                for j in range(UB):
                    for k in range(2):
                        q = 2 * j + k
                        last = nc.tensor.transpose(ps[:, 5 + q // 4, q % 4 * P:(q % 4 + 1) * P],
                                                   h_n[:, j, k * P:(k + 1) * P], ident[:])
                last.then_inc(t_made, 1)

            gat_scores(0, "score1", H1)
            soft(0, "soft1", H1, P // H1)
            sums(0, "sum1", H1, AW)

            begin(pe, "node2", ["dve", "act"])
            pe.wait_ge(weights_in[1], 7 * 16)
            pe.wait_ge(edge_dve, 6)
            with nc.tensor.Fori(0, BTURNS) as t:
                pe.wait_ge(node_dve, t + BTURNS)
                pe.wait_ge(node_act, t + BTURNS)
                transposes(t)
                pe.wait_ge(ht_copied, t + 1)
                for j in range(UB):
                    pe.wait_ge(x_loaded[j], (t + (BTURNS + 1)) * 16)
                    for k in range(2):
                        nc.tensor.matmul(ps[:, j, :], h_t[:, j, k, :], w_a[:, k, 0:2 * D], start=k == 0, stop=False)
                    nc.tensor.matmul(ps[:, j, D:2 * D], ones[0:1, :], bias_row[:, D:2 * D], start=False, stop=False)
                    for k in range(2):
                        nc.tensor.matmul(ps[:, j, D:2 * D], x_t[:, j, k, :], w_b[:, k, :], start=False, stop=k == 1)
                    for k in range(2):
                        last = nc.tensor.matmul(ps[:, 7, 256 + 16 * j:272 + 16 * j], h_t[:, j, k, :],
                                                w_el[:, k].rearrange("p a h -> p (a h)"), start=k == 0, stop=k == 1)
                last.then_inc(node_mm, 1)
            pe.wait_ge(node_mm, 2 * BTURNS)
            end()

            gat_scores(1, "score2", H2)
            soft(1, "soft2", H2, ITEMS // 4)
            sums(1, "sum2", H2, D + H2)

            begin(pe, "node3", ["dve", "act"])
            pe.wait_ge(weights_in[2], 9 * 16)
            with nc.tensor.Fori(0, BTURNS) as t:
                pe.wait_ge(node_dve, t + 2 * BTURNS)
                pe.wait_ge(node_act, t + 2 * BTURNS)
                transposes(t + BTURNS)
                pe.wait_ge(ht_copied, t + (BTURNS + 1))
                for j in range(UB):
                    v_at = ps[:, 5 + j // 2, j % 2 * D:(j % 2 + 1) * D]
                    for at, w0, w1 in ((ps[:, j, :], 0, 2 * D), (v_at, 2 * D, 3 * D)):
                        for k in range(2):
                            nc.tensor.matmul(at, h_t[:, j, k, :], w_a[:, k, w0:w1], start=k == 0, stop=False)
                        last = nc.tensor.matmul(at, ones[0:1, :], bias_row[:, w0:w1], start=False, stop=True)
                last.then_inc(node_mm, 1)
            pe.wait_ge(node_mm, 3 * BTURNS)
            end()

            pair_scores(2, "score3")
            soft(2, "soft3", H3, P // H3)
            sums(2, "sum3", H3, D + H3)

            begin(pe, "final", ["dve", "act"])
            pe.wait_ge(weights_in[3], 4 * 16)
            with nc.tensor.Fori(0, BTURNS) as t:
                transposes(t + 2 * BTURNS)
                pe.wait_ge(ht_copied, t + (2 * BTURNS + 1))
                pe.wait_ge(node_dve, t + 3 * BTURNS)
                for j in range(UB):
                    for k in range(2):
                        nc.tensor.matmul(ps[:, j, 0:D], h_t[:, j, k, :], w_b[:, k, :], start=k == 0, stop=False)
                    last = nc.tensor.matmul(ps[:, j, 0:D], ones[0:1, :], bias_row[:, 0:D], start=False, stop=True)
                last.then_inc(node_mm, 1)

        @block.scalar
        def _(act):
            step = Count(act_step)

            def did(ins):
                ins.then_inc(act_step, 1)
                step.add()
                act.wait_ge(act_step, step.value())

            def end():
                act.sem_inc(phase["act"], 1)

            def idle(name):
                begin(act, name, ["act"])
                end()

            idle("items")

            def copy_transposes(t, before, bias=None):
                act.wait_ge(t_made, t + (before + 1))
                for bank in range(3):
                    n = 2 if bank < 2 else 1
                    src = ps[:, 5 + bank, 0:2 * n * P].rearrange("p (j k n) -> p j k n", k=2, n=P)
                    dst = h_t[:, 2 * bank:2 * bank + n]
                    if bias is None:
                        last = nc.scalar.copy(dst, src)
                    else:
                        for k in range(2):
                            last = nc.scalar.activation(dst[:, :, k], src[:, :, k], ACT.Identity, bias=bias[:, k:k + 1])
                last.then_inc(ht_copied, 1)

            def products(t, before, stores_each, stores_before):
                act.wait_ge(node_mm, t + (before + 1))
                for j in range(UB):
                    act.wait_ge(node_stored[j], t * (16 * stores_each) + 16 * stores_before)

            def gat_copies(t, before, heads):
                products(t, before, 1, before)
                nc.scalar.copy(stage[:, :, 0, :], ps[:, 0:UB, 0:D])
                terms = ps[:, 7, 256:256 + 16 * UB].rearrange("p (j a h) -> p j a h", j=UB, a=2)
                el_v = el[:, 0:BLOCKS * heads].rearrange("p (b h) -> p b h", h=heads)
                nc.scalar.copy(el_v[:, bass.ds(t * UB, UB), :], terms[:, :, 0, 0:heads])
                nc.scalar.copy(er[:, bass.ds(t * UB, UB), 0:heads], terms[:, :, 1, 0:heads]).then_inc(node_act, 1)

            def onehots(layer, name):
                begin(act, name, ["dve", "pe"])
                with nc.scalar.Fori(0, TURNS) as u:
                    step.enter(u, SLOTS)
                    for s in range(SLOTS):
                        act.wait_ge(bcast_in[s % 2], nth(u, s) * 32 + 32 * (layer * HALF + 1))
                        did(nc.scalar.activation(bcast[:, s % 2], bcast[:, s % 2], ACT.Abs, bias=neg_part[:]))
                        act.wait_ge(score_mm[s % 2], nth(u, s) + layer * HALF)
                        nc.scalar.activation(onehot_t[:, s % 2], bcast[:, s % 2], ACT.Relu, bias=ones[:, 0:1],
                                             scale=-1.0).then_inc(onehot_made[s % 2], 1)
                    step.leave(TURNS)
                for s in range(2):
                    act.wait_ge(onehot_made[s], (layer + 1) * HALF)
                end()

            def soft(n, name, heads, chunks):
                begin(act, name, ["dve", "pe"])
                each, m = ITEMS // chunks, heads * chunks
                act.wait_ge(seg_t, n + 1)
                for bank in range(-(-each // 4)):
                    k = min(4, each - 4 * bank) * P
                    last = nc.scalar.copy(seg[1][0:m, 4 * bank * P:4 * bank * P + k], ps[0:m, bank, 0:k])
                last.then_inc(seg_copied, 1)
                act.wait_ge(seg_dve, 3 * n + 3)
                nc.scalar.activation(seg[1][0:m, 0:each * P], seg[1][0:m, 0:each * P], ACT.Exp).then_inc(seg_exp, 1)
                act.wait_ge(seg_back, n + 1)
                view = scores[:, 0:ITEMS * heads].rearrange("p (m j) -> p j m", j=each)
                for bank in range(-(-each // 4)):
                    k = min(4, each - 4 * bank)
                    last = nc.scalar.copy(view[:, 4 * bank:4 * bank + k],
                                          ps[:, bank, 0:k * m].rearrange("p (j m) -> p j m", j=k))
                did(last)
                end()

            def deviations(k):
                act.wait_ge(variance, k)
                nc.scalar.activation(small[:, :, 8:9], small[:, :, 7:8], ACT.Sqrt, bias=eps_col[:]).then_inc(deviation, 1)

            begin(act, "node1", ["dve", "pe"])
            with nc.scalar.Fori(0, BTURNS) as t:
                gat_copies(t, 0, H1)
            act.wait_ge(node_act, BTURNS)
            end()
            onehots(0, "score1")
            soft(0, "soft1", H1, P // H1)
            idle("sum1")

            begin(act, "node2", ["dve", "pe"])
            with nc.scalar.Fori(0, BTURNS) as t:
                copy_transposes(t, 0)
                gat_copies(t, BTURNS, H2)
            act.wait_ge(node_act, 2 * BTURNS)
            end()
            onehots(1, "score2")
            soft(1, "soft2", H2, ITEMS // 4)
            idle("sum2")

            begin(act, "node3", ["dve", "pe"])
            act.wait_ge(weights_in[2], 9 * 16)
            did(nc.scalar.mul(query_col[:], query_col[:], 0.1))
            did(nc.scalar.mul(rel_sb[:], rel_sb[:], 0.2))
            with nc.scalar.Fori(0, BTURNS) as t:
                deviations(t + 1)
                copy_transposes(t, BTURNS, query_col)
                products(t, 2 * BTURNS, 2, 2 * BTURNS)
                nc.scalar.copy(stage[:, :, 0, :], ps[:, 0:UB, D:2 * D])
                for bank in range(3):
                    n = 2 if bank < 2 else 1
                    last = nc.scalar.copy(stage[:, 2 * bank:2 * bank + n, 1, :],
                                          ps[:, 5 + bank, 0:n * D].rearrange("p (j d) -> p j d", j=n))
                last.then_inc(node_act, 1)
            act.wait_ge(node_act, 3 * BTURNS)
            end()
            onehots(2, "score3")
            soft(2, "soft3", H3, P // H3)
            idle("sum3")

            begin(act, "final", ["dve", "pe"])
            with nc.scalar.Fori(0, BTURNS) as t:
                copy_transposes(t, 2 * BTURNS)
                deviations(t * 2 + (BTURNS + 1))
                deviations(t * 2 + (BTURNS + 2))

        @block.vector
        def _(dve):
            step = Count(dve_step)
            vec = nc.vector

            def did(ins):
                ins.then_inc(dve_step, 1)
                step.add()
                dve.wait_ge(dve_step, step.value())

            def end():
                dve.sem_inc(phase["dve"], 1)

            def signal(sem):
                dve.sem_inc(sem, 1)

            dve.wait_ge(consts, 2)
            dve.wait_ge(edges_in, 9 * 16)
            did(vec.tensor_copy(tiles_f, tiles_i))
            tile_si = tile_s.bitcast(I32)
            lo, hi, many, start, stop, shift, total = (tile_s[:, k, :] for k in range(2, 9))
            did(vec.tensor_scalar(tile_si[:, 0, :], tiles_i[:, 1, :, 0], 7, None, ALU.arith_shift_right))
            did(vec.tensor_scalar(tile_si[:, 1, :], tiles_i[:, 1, :, P - 1], 7, None, ALU.arith_shift_right))
            did(vec.tensor_copy(tile_s[:, 2:4, :], tile_si[:, 0:2, :]))
            did(vec.tensor_tensor(many, hi, lo, ALU.subtract))
            did(vec.tensor_scalar(many, many, 1.0, None, ALU.add))
            did(vec.scalar_tensor_tensor(many, tile_no[:], float(TILES), many, ALU.is_lt, ALU.mult))
            signal(edge_dve)
            dve.wait_ge(edge_pe, 1)
            did(vec.memset(total[:, 0:1], 0.0))
            for c in range(1, TCH):
                did(vec.tensor_tensor(total[:, c:c + 1], total[:, c - 1:c], ps[:, 1, c - 1:c], ALU.add))
            did(vec.tensor_tensor(start, total, ps[:, 0, 0:TCH], ALU.add))
            did(vec.tensor_tensor(stop, start, many, ALU.add))
            did(vec.tensor_tensor(shift, lo, start, ALU.subtract))
            for c in range(TCH):
                did(vec.tensor_scalar(item_tmp, iota_free[:], start[:, c:c + 1], None, ALU.is_ge))
                did(vec.scalar_tensor_tensor(sel[:, c, :], iota_free[:], stop[:, c:c + 1], item_tmp,
                                             ALU.is_lt, ALU.mult))
                did(vec.scalar_tensor_tensor(bsel[:, c, :], iota_free[:], shift[:, c:c + 1], sel[:, c, :],
                                             ALU.add, ALU.mult))
            signal(edge_dve)
            dve.wait_ge(edge_pe, 2)
            tmp_i = item_tmp.bitcast(I32)
            did(vec.tensor_copy(src_i[:], ps[:, 0, 0:ITEMS]))
            did(vec.tensor_copy(item_f[:, 0, :], ps[:, 1, 0:ITEMS]))
            did(vec.tensor_copy(item_f[:, 3, :], ps[:, 2, 0:ITEMS]))
            did(vec.tensor_copy(block_i[:], ps[:, 3, 0:ITEMS]))
            did(vec.scalar_tensor_tensor(block_dst[:], ps[:, 3, 0:ITEMS], -float(P), item_f[:, 0, :],
                                         ALU.mult, ALU.add))
            did(vec.tensor_tensor(block_dst[:], block_dst[:], ps[:, 4, 0:ITEMS], ALU.add))
            did(vec.tensor_scalar(block_dst[:], block_dst[:], -1.0, None, ALU.add))
            did(vec.tensor_scalar(tmp_i, src_i[:], 7, None, ALU.arith_shift_right))
            did(vec.tensor_copy(src_hi[:], tmp_i))
            did(vec.tensor_scalar(tmp_i, src_i[:], P - 1, None, ALU.bitwise_and))
            did(vec.tensor_copy(item_f[:, 2, :], tmp_i))
            signal(edge_dve)
            dve.wait_ge(edge_pe, 3)
            for k in range(4):
                did(vec.tensor_copy(rows_t[:, k, 0:ICH - 1, :],
                                    ps[:, k, 0:(ICH - 1) * P].rearrange("p (c e) -> p c e", e=P)))
                did(vec.tensor_copy(rows_t[0:LAST, k, ICH - 1, :], ps[0:LAST, k, (ICH - 1) * P:ICH * P]))
            signal(edge_dve)
            end()

            def attention_columns(k, count, heads):
                dve.wait_ge(weights_in[k], 16 * count)
                for side in range(2):
                    did(vec.tensor_tensor(tmp_n[:, 0:2, :], w_a[:, :, 0:D],
                                          attn[:, side:side + 1, :].broadcast_to([P, 2, D]), ALU.mult))
                    did(vec.tensor_reduce(w_el[:, :, side, 0:heads],
                                          tmp_n[:, 0:2, :].rearrange("p k (h d) -> p k h d", h=heads), AX.X, ALU.add))
                signal(edge_dve)

            begin(dve, "node1", ["pe", "act", "sp"])
            attention_columns(0, 5, H1)
            did(vec.memset(acc[:], 0.0))
            with vec.Fori(0, BTURNS) as t:
                dve.wait_ge(node_act, t + 1)
                vec.tensor_copy(base[:, bass.ds(t * UB, UB), :], ps[:, 0:UB, D:2 * D]).then_inc(node_dve, 1)
            dve.wait_ge(node_dve, BTURNS)
            end()

            def gat_scores(layer, name, heads):
                begin(dve, name, ["pe", "act"])
                w = BLOCKS * heads
                with vec.Fori(0, TURNS) as u:
                    step.enter(u, SLOTS * 7)
                    for s in range(SLOTS):
                        z = s % 2
                        first = u * STEP + s * GROUP
                        hot = hi_onehot[:, z, :, 0:BLOCKS]
                        did(vec.tensor_tensor(
                            hot, iota_free[:, 0:BLOCKS].unsqueeze(1).broadcast_to([P, GROUP, BLOCKS]),
                            src_hi[:, bass.ds(first, GROUP)].unsqueeze(2).broadcast_to([P, GROUP, BLOCKS]), ALU.is_equal))
                        dve.wait_ge(score_mm[z], nth(u, s) + (layer * HALF + 1))
                        for q in range(GROUP // 2):
                            got = ps[:, z * 4 + q, 0:2 * (w + heads)].rearrange("p (i x) -> p i x", i=2)
                            last = vec.tensor_tensor(
                                product[:, z, 2 * q:2 * q + 2, 0:w].rearrange("p i (h b) -> p i h b", h=heads),
                                got[:, :, 0:w].rearrange("p i (b h) -> p i h b", h=heads),
                                hot[:, 2 * q:2 * q + 2, :].unsqueeze(2).broadcast_to([P, 2, heads, BLOCKS]), ALU.mult)
                            did(last)
                        source = product[:, z, :, w:w + heads]
                        did(vec.tensor_reduce(source, product[:, z, :, 0:w].rearrange("p i (h b) -> p i h b", h=heads),
                                              AX.X, ALU.add))
                        four = ps[:, z * 4:z * 4 + 4, 0:2 * (w + heads)].rearrange("p q (i x) -> p q i x", i=2)
                        pairs = source.rearrange("p (q i) h -> p q i h", i=2)
                        did(vec.tensor_tensor(pairs, pairs, four[:, :, :, w:w + heads], ALU.add))
                        signal(score_read[z])
                        vec.scalar_tensor_tensor(by_item(heads)[:, bass.ds(first, GROUP), :], source, 0.2, source, ALU.mult, ALU.max)
                    step.leave(TURNS)
                did(vec.memset(chunk_col[:, 0:1], 0.0))
                end()

            def pair_scores(layer, name):
                begin(dve, name, ["pe", "act"])
                dve.sem_inc(pair_read, GROUP)
                with vec.Fori(0, TURNS) as u:
                    step.enter(u, SLOTS * (GROUP + 1))
                    for s in range(SLOTS):
                        z = s % 2
                        dve.wait_ge(gathered[s], (u + (2 * TURNS + 1)) * (16 * GROUP))
                        for g in range(GROUP):
                            dve.wait_ge(pair_mm, u * STEP + (s * GROUP + g + 1))
                            key = product[:, z, g, 0:D].rearrange("p (h d) -> p h d", h=H3)
                            did(vec.tensor_tensor(key, rows[:, s, g, :].rearrange("p (h d) -> p h d", h=H3),
                                                  ps[:, g, D:D + R].unsqueeze(1).broadcast_to([P, H3, R]), ALU.add))
                            vec.tensor_tensor(product[:, z, g, 0:D], product[:, z, g, 0:D],
                                              ps[:, g, 0:D], ALU.mult).then_inc(pair_read, 1)
                        dve.wait_ge(pair_read, u * STEP + (s + 2) * GROUP)
                        signal(slot_used[s])
                        signal(score_mm[z])
                        did(vec.tensor_reduce(by_item(H3)[:, bass.ds(u * STEP + s * GROUP, GROUP), :],
                                              product[:, z, :, 0:D].rearrange("p i (h d) -> p i h d", h=H3),
                                              AX.X, ALU.add))
                    step.leave(TURNS)
                end()

            def soft(n, name, heads, chunks, rows_before):
                begin(dve, name, ["pe", "act"])
                each, m = ITEMS // chunks, heads * chunks
                L = each * P
                dst, score, gap, top = (b[0:m] for b in seg)
                dve.wait_ge(seg_in, 16 * (rows_before + heads))
                did(vec.memset(gap[:, 0:1], -BIG))
                did(vec.memset(gap[:, L:L + 1], -BIG))
                did(vec.tensor_tensor(gap[:, 1:L], dst[:, 1:L], dst[:, 0:L - 1], ALU.not_equal))
                did(vec.tensor_scalar(gap[:, 1:L], gap[:, 1:L], -BIG, None, ALU.mult))
                dve.wait_ge(seg_copied, n + 1)
                did(vec.tensor_tensor_scan(top[:, 0:L], gap[:, 0:L], score[:, 0:L], -BIG, ALU.add, ALU.max))
                did(vec.tensor_tensor_scan(top[:, 0:L][:, ::-1], gap[:, 1:L + 1][:, ::-1], top[:, 0:L][:, ::-1],
                                           -BIG, ALU.add, ALU.max))
                for k, end_v in enumerate([top[:, 0:1], top[:, L - 1:L], dst[:, 0:1], dst[:, L - 1:L]]):
                    did(vec.tensor_copy(chunk_col[0:m, k:k + 1], end_v))
                signal(seg_dve)
                dve.wait_ge(seg_small, 2 * n + 1)
                did(vec.tensor_copy(chunk_row[:, 0:4, 0:m], ps[0:1, 0, :].rearrange("p (k c) -> p k c", k=4)[:, :, 0:m]))
                head_top, tail_top, head_dst, tail_dst, whole, joint, a0, b0, before, after, a1, b1 = (
                    chunk_row[:, k, 0:m] for k in range(12))
                did(vec.tensor_tensor(whole, head_dst, tail_dst, ALU.not_equal))
                did(vec.tensor_scalar(whole, whole, -BIG, None, ALU.mult))
                did(vec.tensor_tensor(joint[:, 1:m], head_dst[:, 1:m], tail_dst[:, 0:m - 1], ALU.not_equal))
                did(vec.tensor_scalar(joint[:, 1:m], joint[:, 1:m], -BIG, None, ALU.mult))
                did(vec.memset(joint.rearrange("p (h c) -> p h c", h=heads)[:, :, 0:1], -BIG))
                for row, col in ((a0, 0), (b0, 0), (a1, m - 1), (b1, m - 1)):
                    did(vec.memset(row[:, col:col + 1], -BIG))
                did(vec.tensor_tensor(a0[:, 1:m], whole[:, 0:m - 1], joint[:, 1:m], ALU.add))
                did(vec.tensor_tensor(b0[:, 1:m], tail_top[:, 0:m - 1], joint[:, 1:m], ALU.add))
                did(vec.tensor_tensor(a1[:, 0:m - 1], whole[:, 1:m], joint[:, 1:m], ALU.add))
                did(vec.tensor_tensor(b1[:, 0:m - 1], head_top[:, 1:m], joint[:, 1:m], ALU.add))
                did(vec.tensor_tensor_scan(before, a0, b0, -BIG, ALU.add, ALU.max))
                did(vec.tensor_tensor_scan(after[:, ::-1], a1[:, ::-1], b1[:, ::-1], -BIG, ALU.add, ALU.max))
                signal(seg_dve)
                dve.wait_ge(seg_small, 2 * n + 2)
                did(vec.tensor_copy(chunk_col[0:m, 0:2], ps[0:m, 1, 0:2]))
                for k in range(2):
                    did(vec.tensor_scalar(gap[:, 0:L], dst[:, 0:L], chunk_col[0:m, 2 + k:3 + k], -BIG,
                                          ALU.not_equal, ALU.mult))
                    did(vec.scalar_tensor_tensor(top[:, 0:L], gap[:, 0:L], chunk_col[0:m, k:k + 1], top[:, 0:L],
                                                 ALU.add, ALU.max))
                did(vec.tensor_tensor(score[:, 0:L], score[:, 0:L], top[:, 0:L], ALU.subtract))
                signal(seg_dve)
                end()

            regs = [dve.alloc_register(f"dve_block{g}") for g in range(GROUP)]

            def sums(n, name, heads, width, nth_pass):
                begin(dve, name, ["pe", "act"])
                did(vec.memset(weighted[:, :, :, DEG:AW], 1.0))
                dve.sem_inc(sum_added, GROUP)

                def build(u, s, peeled=False):
                    z = s % 2
                    first = u * STEP + s * GROUP
                    dve.wait_ge(gathered[s], (u + (nth_pass * TURNS + 1)) * (16 * GROUP))
                    if not peeled:
                        dve.wait_ge(sum_mm, u * STEP + (s * GROUP - GROUP + n * ITEMS))
                    vec.tensor_tensor(onehot[:, z], iota_free[:, 0:P].unsqueeze(1).broadcast_to([P, GROUP, P]),
                                      block_dst[:, bass.ds(first, GROUP)].unsqueeze(2).broadcast_to([P, GROUP, P]),
                                      ALU.is_equal)
                    share = by_item(heads)[:, bass.ds(first, GROUP), :]
                    vec.tensor_copy(weighted[:, z, :, D:D + heads], share)
                    vec.tensor_tensor(weighted[:, z, :, 0:D].rearrange("p i (h d) -> p i h d", h=heads),
                                      rows[:, s].rearrange("p i (h d) -> p i h d", h=heads),
                                      share.unsqueeze(3).broadcast_to([P, GROUP, heads, D // heads]),
                                      ALU.mult).then_inc(weighted_made, 1)

                def add(u, s):
                    dve.load(regs, block_i[0:1, bass.ds(u * STEP + s * GROUP, GROUP)])
                    bs = [dve.snap(r, min_val=0, max_val=BLOCKS - 1) for r in regs]
                    dve.wait_ge(weighted_made, u * SLOTS + (s + 1 + n * GROUPS))
                    dve.sem_inc(slot_used[s], 1)
                    for g in range(GROUP):
                        i = s * GROUP + g
                        dve.wait_ge(sum_mm, u * STEP + (i + 1 + n * ITEMS))
                        dve.wait_ge(sum_added, u * STEP + (i + GROUP + n * (ITEMS + GROUP)))
                        to = acc[:, bass.ds(bs[g], 1), 0:width].rearrange("p a d -> p (a d)")
                        vec.tensor_tensor(to, to, ps[:, g, 0:width], ALU.add).then_inc(sum_added, 1)

                build(0, 0, peeled=True)
                with vec.Fori(0, TURNS - 1) as u:
                    for s in range(SLOTS):
                        build(u + (s + 1) // SLOTS, (s + 1) % SLOTS)
                        add(u, s)
                for s in range(SLOTS):
                    if s + 1 < SLOTS:
                        build(TURNS - 1, s + 1)
                    add(TURNS - 1, s)
                dve.wait_ge(sum_added, (n + 1) * (ITEMS + GROUP))
                end()

            def turn_of(buf, t):
                return buf[:, bass.ds(t * UB, UB), :]

            def mean_rows(t, heads):
                sums_t = turn_of(acc, t)
                did(vec.tensor_scalar(small[:, :, 16:16 + heads], sums_t[:, :, D:D + heads], 0.5, None, ALU.max))
                did(vec.reciprocal(small[:, :, 24:24 + heads], small[:, :, 16:16 + heads]))
                did(vec.tensor_tensor(h_n.rearrange("p j (h d) -> p j h d", h=heads),
                                      sums_t[:, :, 0:D].rearrange("p j (h d) -> p j h d", h=heads),
                                      small[:, :, 24:24 + heads].unsqueeze(3).broadcast_to([P, UB, heads, D // heads]),
                                      ALU.mult))

            def add_residual(t):
                did(vec.tensor_scalar(small[:, :, 10:11], deg[:, bass.ds(t * UB, UB)].unsqueeze(2), 1.0, None, ALU.max))
                did(vec.reciprocal(small[:, :, 11:12], small[:, :, 10:11]))
                did(vec.tensor_tensor(tmp_n, turn_of(base, t), small[:, :, 11:12].broadcast_to([P, UB, D]), ALU.mult))
                did(vec.tensor_tensor(h_n, h_n, tmp_n, ALU.add))
                did(vec.tensor_tensor(h_n, h_n, bias_all[:, 0:1, :].broadcast_to([P, UB, D]), ALU.add))

            def norm(k):
                for j in range(UB):
                    last = vec.bn_stats(small[:, j, 0:6], h_n[:, j])
                did(last)
                signal(stats_made)
                for j in range(UB):
                    last = vec.bn_aggr(small[:, j, 6:8], small[:, j, 0:6])
                last.then_inc(variance, 1)
                dve.wait_ge(deviation, k)
                did(vec.reciprocal(small[:, :, 9:10], small[:, :, 8:9]))
                for j in range(UB):
                    last = vec.tensor_scalar(h_n[:, j], h_n[:, j], small[:, j, 6:7], small[:, j, 9:10],
                                             ALU.subtract, ALU.mult)
                did(last)

            NORM = 3

            gat_scores(0, "score1", H1)
            soft(0, "soft1", H1, P // H1, 0)
            sums(0, "sum1", H1, AW, 0)

            begin(dve, "node2", ["pe", "act"])
            attention_columns(1, 7, H2)
            did(vec.tensor_copy(deg[:].unsqueeze(2), acc[:, :, DEG:AW]))
            with vec.Fori(0, BTURNS) as t:
                step.enter(t, 9)
                mean_rows(t, H1)
                add_residual(t)
                did(vec.tensor_scalar(h_n, h_n, 0.0, None, ALU.max))
                signal(h_made)
                dve.wait_ge(node_act, t + (BTURNS + 1))
                vec.tensor_scalar(turn_of(base, t), ps[:, 0:UB, D:2 * D], 1.0, None, ALU.mult).then_inc(node_dve, 1)
                step.leave(BTURNS)
            dve.wait_ge(node_dve, 2 * BTURNS)
            did(vec.memset(acc[:], 0.0))
            end()

            gat_scores(1, "score2", H2)
            soft(1, "soft2", H2, ITEMS // 4, H1)
            sums(1, "sum2", H2, D + H2, 1)

            begin(dve, "node3", ["pe", "act"])
            dve.wait_ge(weights_in[2], 9 * 16)
            with vec.Fori(0, BTURNS) as t:
                step.enter(t, 8 + 1 + NORM + 1)
                mean_rows(t, H2)
                add_residual(t)
                for j in range(UB):
                    dve.wait_ge(x_loaded[j], (t + (2 * BTURNS + 1)) * 16)
                did(vec.tensor_tensor(h_n, h_n, x_n, ALU.add))
                norm(t + 1)
                did(vec.tensor_scalar(turn_of(base, t), h_n, 1.0, None, ALU.mult))
                signal(h_made)
                dve.wait_ge(node_act, t + (2 * BTURNS + 1))
                vec.tensor_scalar(turn_of(queries, t), ps[:, 0:UB, 0:D], float(R) ** -0.5, None,
                                  ALU.mult).then_inc(node_dve, 1)
                step.leave(BTURNS)
            dve.wait_ge(node_dve, 3 * BTURNS)
            did(vec.memset(acc[:], 0.0))
            end()

            pair_scores(2, "score3")
            soft(2, "soft3", H3, P // H3, H1 + H2)
            sums(2, "sum3", H3, D + H3, 3)

            begin(dve, "final", ["pe", "act"])
            dve.wait_ge(weights_in[3], 4 * 16)
            with vec.Fori(0, BTURNS) as t:
                step.enter(t, 6 + 1 + 2 * NORM + 3)
                for j in range(UB):
                    dve.wait_ge(node_stored[j], t * 16 + 16 * 4 * BTURNS)
                mean_rows(t, H3)
                did(vec.tensor_scalar(small[:, :, 10:11], deg[:, bass.ds(t * UB, UB)].unsqueeze(2), 0.5, None, ALU.is_lt))
                for j in range(UB):
                    dve.wait_ge(x_loaded[j], (t + (3 * BTURNS + 1)) * 16)
                did(vec.tensor_tensor(tmp_n, stage[:, :, 1, :], small[:, :, 10:11].broadcast_to([P, UB, D]), ALU.mult))
                did(vec.tensor_tensor(h_n, h_n, tmp_n, ALU.add))
                signal(h_made)
                dve.wait_ge(node_mm, t + (3 * BTURNS + 1))
                did(vec.tensor_tensor(h_n, ps[:, 0:UB, 0:D], turn_of(base, t), ALU.add))
                norm(t * 2 + (BTURNS + 1))
                did(vec.tensor_tensor(h_n, h_n, bias_all[:, 0:1, :].broadcast_to([P, UB, D]), ALU.mult))
                did(vec.tensor_tensor(h_n, h_n, bias_all[:, 1:2, :].broadcast_to([P, UB, D]), ALU.add))
                did(vec.tensor_tensor(h_n, h_n, turn_of(base, t), ALU.add))
                norm(t * 2 + (BTURNS + 2))
                signal(node_dve)
                step.leave(BTURNS)


def kernel(**inputs):
    import concourse.bacc as bacc
    from concourse.bass_utils import run_bass_kernel_spmd

    def rows_of(v):
        return np.ascontiguousarray(v).reshape(1, -1)

    x = np.zeros((NP, D), inputs["x"].dtype)
    x[0:N] = inputs["x"]
    arrays = {"x": x, "x_t": np.ascontiguousarray(x.T)}
    for k in ("src", "dst", "edge_type_64"):
        arrays[k] = np.ascontiguousarray(inputs[k])
    for k in ("fc1_w", "fc2_w", "wb0", "wb1"):
        arrays[k.replace("_w", "") + "_t"] = np.ascontiguousarray(np.transpose(inputs["L0_gnn_" + k]))
    for k in ("attn_l1", "attn_r1", "attn_l2", "attn_r2", "bias1", "bias2", "bb0", "bb1"):
        arrays[k] = rows_of(inputs["L0_gnn_" + k])
    for k in ("Wq", "Wk", "Wv", "Wo"):
        arrays[k.lower()] = np.ascontiguousarray(inputs["L1_gnn_" + k])
    for k in ("bq", "bk", "bv", "bo", "gamma", "beta"):
        arrays[k] = rows_of(inputs["L1_gnn_" + k])
    arrays["query"] = np.ascontiguousarray(np.reshape(inputs["L1_gnn_query_emb"], (2, P)).T)
    arrays["rel"] = np.ascontiguousarray(inputs["L1_gnn_rel_w"])

    nc = bacc.Bacc("TRN2", target_bir_lowering=False, num_devices=1)
    a = {k: nc.dram_tensor("in_" + k, v.shape, mybir.dt.from_np(v.dtype), kind="ExternalInput").ap()
         for k, v in arrays.items()}
    out = nc.dram_tensor("out", (N, D), F32, kind="ExternalOutput").ap()
    graph_layers(nc, a, out)
    r = run_bass_kernel_spmd(nc, [{"in_" + k: v for k, v in arrays.items()}], core_ids=[0])
    return r.results[0]["out"]
```

```python
import numpy as np
import concourse.bass as bass
from concourse import mybir
from contextlib import ExitStack

F32 = mybir.dt.float32
I32 = mybir.dt.int32
I16 = mybir.dt.int16
BF16 = mybir.dt.bfloat16
ALU = mybir.AluOpType
ACT = mybir.ActivationFunctionType
AX = mybir.AxisListType

P = 128
N, E, D, R = 3125, 50000, 256, 64
BLOCKS = -(-N // P)
NP = BLOCKS * P
TILES = -(-E // P)
TCH = -(-TILES // P)
GROUP = 8
SLOTS = 4
STEP = GROUP * SLOTS
ITEMS = -(-(TILES + BLOCKS - 1) // STEP) * STEP
GROUPS = ITEMS // GROUP
TURNS = ITEMS // STEP
ICH = -(-ITEMS // P)
LAST = ITEMS - (ICH - 1) * P
H1, H2, H3 = 8, 1, 4
UB = 5
PIECE = 23
ROW = 16
RINGS = [2 * SLOTS, 2 * SLOTS, SLOTS, SLOTS]
BTURNS = BLOCKS // UB
PICKS = BLOCKS + 3
BIG = 1.0e30
PAD_DST = NP - 1
DEG = D + H1
AW = DEG + 1
EPS = 1e-5


class Count:

    def __init__(self, sem):
        self.sem, self.n, self.turn, self.per, self.at = sem, 0, None, 0, 0

    def enter(self, turn, per):
        self.turn, self.per, self.at = turn, per, self.n

    def leave(self, turns):
        assert self.n - self.at == self.per, (self.n - self.at, self.per)
        self.n = self.at + self.per * turns
        self.turn = None

    def add(self, k=1):
        self.n += k

    def value(self):
        return self.n if self.turn is None else self.turn * self.per + self.n


def graph_layers(nc, a, out):
    ctx = ExitStack()
    with ctx:
        def sb(name, shape, dt=F32):
            return ctx.enter_context(nc.sbuf_tensor(name, shape, dt))

        def sem(name):
            return ctx.enter_context(nc.semaphore(name))

        def dram(name, shape, dt=F32):
            return nc.dram_tensor(name, shape, dt).ap()

        tab_feat1 = dram("tab_feat1", (NP, D))
        tab_feat2 = dram("tab_feat2", (NP, D))
        tab_k = dram("tab_k", (NP, D))
        tab_v = dram("tab_v", (NP, D))
        row_names = ["dst", "block_dst", "src_low", "type"]
        sorted_d = dram("sorted_edges", (TILES * P, ROW), I32)
        rows_d = {k: dram("rows_" + k, (ITEMS, P), I16 if k == "dst" else BF16) for k in row_names}

        ident = sb("ident", [P, P])
        below = sb("below", [P, P])
        before_edge = sb("before_edge", [P, P])
        ones = sb("ones", [P, P])
        iota_free = sb("iota_free", [P, ITEMS])
        part_no = sb("part_no", [P, 1])
        tile_no = sb("tile_no", [P, TCH])
        eps_col = sb("eps_col", [P, 1])
        src_i = sb("src_i", [P, ITEMS], I32)
        src_hi = sb("src_hi", [P, ITEMS])
        block_dst = sb("block_dst", [P, ITEMS])
        block_i = sb("block_i", [P, ITEMS], I32)
        el = sb("el", [P, BLOCKS * H1])
        er = sb("er", [P, BLOCKS, H1])
        deg = sb("deg", [P, BLOCKS])
        acc = sb("acc", [P, BLOCKS, AW])
        base = sb("base", [P, BLOCKS, D])
        el_parts = sb("el_parts", [P, 3, BLOCKS * H1], BF16)
        er_parts = sb("er_parts", [P, BLOCKS * 3 * H1], BF16)
        rel_parts = sb("rel_parts", [R, 3, R], BF16)
        query_parts = sb("query_parts", [P, 3, BLOCKS, D], BF16)
        scores = sb("scores", [P, ITEMS * H1])

        def by_item(heads):
            return scores[:, 0:ITEMS * heads].rearrange("p (h i) -> p i h", h=heads)

        rows = sb("rows", [P, SLOTS, GROUP, D])
        bias_split = rows[0:1, 0].rearrange("p g d -> p (g d)").bitcast(BF16)[:, 0:3 * 3 * D].rearrange(
            "p (k d) -> p k d", k=3)
        more_rows = query_parts[:].rearrange("p k b d -> p (k b d)").bitcast(F32)[:, 0:SLOTS * GROUP * D].rearrange(
            "p (s g d) -> p s g d", s=SLOTS, g=GROUP)
        row_slots = [rows[:, s] for s in range(SLOTS)] + [more_rows[:, s] for s in range(SLOTS)]
        index_slot = sb("index_slot", [P, 2 * SLOTS, GROUP], I32)
        w_a = sb("w_a", [P, 2, 3 * D])
        w_b = sb("w_b", [P, 2, D])
        w_el = sb("w_el", [P, 2, 2, H1])
        bias_row = sb("bias_row", [1, 3 * D])
        bias_parts = sb("bias_parts", [3, 3 * D], BF16)
        ones_parts = sb("ones_parts", [3, P], BF16)
        bias_all = sb("bias_all", [P, 2, D])
        rel_sb = sb("rel_sb", [R, R])
        bias1_col = sb("bias1_col", [P, 2])
        query_col = sb("query_col", [P, 2])
        chunk_row = w_a[0:1].rearrange("p k n -> p (k n)").rearrange("p (r c) -> p r c", r=12)
        chunk_col = sb("chunk_col", [P, 4])

        ARENA = 10900
        arena = sb("arena", [P, ARENA])

        def views(*sizes):
            got, at = [], 0
            for n in sizes:
                got.append(arena[:, at:at + n])
                at += n
            assert at <= ARENA
            return got

        ps = ctx.enter_context(nc.psum_tensor("ps", [P, 8, 512], F32))

        v = views(3 * TCH * P, 3 * TCH * P, TCH * ITEMS, TCH * ITEMS, ITEMS, 4 * ITEMS, 4 * TCH * P, 12 * TCH)
        tiles_i = v[0].bitcast(I32).rearrange("p (a c e) -> p a c e", a=3, c=TCH)
        tiles_f = v[1].rearrange("p (a c e) -> p a c e", a=3, c=TCH)
        sel = v[2].rearrange("p (c i) -> p c i", c=TCH)
        bsel = v[3].rearrange("p (c i) -> p c i", c=TCH)
        item_tmp = v[4]
        item_f = v[5].rearrange("p (a i) -> p a i", a=4)
        rows_t = [v[6][:, k * TCH * P // 2:(k + 1) * TCH * P // 2].bitcast(I16 if k == 0 else BF16).rearrange(
            "p (c e) -> p c e", c=TCH) for k in range(4)]
        tile_s = v[7].rearrange("p (k c) -> p k c", k=12)
        v = views(3 * TCH * P, TCH * P, TCH * P, 4 * TILES, 3 * TILES, PIECE * P, 4 * P, ROW * P, ROW, 4 + PIECE)
        next_i = v[1].bitcast(I32).rearrange("p (c e) -> p c e", c=TCH)
        falls = v[2].rearrange("p (c e) -> p c e", c=TCH)
        sort_cols = v[3].bitcast(I32).rearrange("p (k t) -> p k t", k=4)
        sort_dst, sort_level, sort_rank = (v[4][:, k * TILES:(k + 1) * TILES] for k in range(3))
        sort_less = v[5].rearrange("p (t e) -> p t e", e=P)
        sort_row_i = v[6][:, 0:2 * P].bitcast(I32).rearrange("p (s e) -> p s e", s=2)
        sort_row, sort_same = v[6][:, 2 * P:3 * P], v[6][:, 3 * P:4 * P]
        sort_back = v[7].bitcast(I32)
        sort_record = v[8].bitcast(I32)
        order_col = v[9][:, 0:4]
        sort_dst_sum = v[9][:, 4:4 + PIECE]
        v = views(2 * GROUP * P, 2 * GROUP * P, 2 * GROUP * 32, 2 * GROUP * AW)
        bcast = v[0].bitcast(BF16).rearrange("p (s a e) -> p s a e", s=2, a=2)
        onehot_t = v[1].bitcast(BF16).rearrange("p (s a e) -> p s a e", s=2, a=2)
        hi_onehot = v[2].rearrange("p (s g d) -> p s g d", s=2, g=GROUP)
        product = v[3].rearrange("p (s g d) -> p s g d", s=2, g=GROUP)
        v = views(2 * GROUP * P, 2 * GROUP * AW)
        onehot = v[0].rearrange("p (s g d) -> p s g d", s=2, g=GROUP)
        weighted = v[1].rearrange("p (s g d) -> p s g d", s=2, g=GROUP)
        SEG = ITEMS * H1
        v = views(SEG // 2, SEG, SEG // 2 + 8, SEG)
        seg = [v[0].bitcast(I16), v[1], v[2].bitcast(BF16), v[3]]
        v = views(UB * 2 * P, UB * D, UB * 2 * P, UB * 2 * D, UB * D, UB * D, UB * 40, 2 * D, BLOCKS * H1, BLOCKS)
        x_t = v[0].rearrange("p (j k n) -> p j k n", j=UB, k=2)
        x_n = v[1].rearrange("p (j d) -> p j d", j=UB)
        h_t = v[2].rearrange("p (j k n) -> p j k n", j=UB, k=2)
        stage = v[3].rearrange("p (j a d) -> p j a d", j=UB, a=2)
        h_n = v[4].rearrange("p (j d) -> p j d", j=UB)
        tmp_n = v[5].rearrange("p (j d) -> p j d", j=UB)
        small = v[6].rearrange("p (j k) -> p j k", j=UB)
        inv_sum = v[8].rearrange("p (b h) -> p b h", b=BLOCKS)
        inv_deg = v[9]
        attn = v[7].rearrange("p (a d) -> p a d", a=2)

        edges_in = sem("edges_loaded")
        consts = sem("constants_made")
        weights_in = [sem(f"weights_loaded{k}") for k in range(4)]
        order_dve, order_pe, order_known = (
            sem("falls_counted"), sem("falls_summed"), sem("order_known"))
        order_flag = sb("order_flag", [1, 1], I32)
        sort_cols_in = sem("sort_columns_loaded")
        sort_row_in = [sem(f"sort_row_loaded{k}") for k in range(2)]
        sort_row_used = [sem(f"sort_row_used{k}") for k in range(2)]
        sort_ranked, sort_scattered, sort_back_in, sort_back_used, sort_done = (
            sem("sort_ranks_made"), sem("sort_records_stored"), sem("sorted_records_loaded"),
            sem("sorted_records_used"), sem("edges_sorted"))
        sort_step = sem("sort_step")
        sort_copied, sort_ready = sem("sort_record_copied"), sem("sort_record_ready")
        edge_pe = sem("edge_products")
        edge_dve = sem("edge_vectors")
        rows_stored = sem("item_rows_stored")
        phase = {k: sem("stage_done_" + k) for k in ["pe", "act", "dve", "sp"]}
        dve_step, act_step, pool_step = sem("dve_step"), sem("act_step"), sem("pool_step")
        x_loaded = [sem(f"node_inputs_loaded{j}") for j in range(UB)]
        h_made = sem("node_rows_made")
        t_made = sem("node_transposes_made")
        ht_copied = sem("node_transposes_copied")
        bias_made, bias_in = sem("bias_parts_made"), sem("bias_parts_loaded")
        x_used = sem("node_inputs_used")
        out_made = sem("output_rows_made")
        node_mm = sem("node_products_made")
        node_dve = sem("node_products_read_dve")
        node_act = sem("node_products_read_act")
        node_stored = [sem(f"node_rows_stored{j}") for j in range(UB)]
        variance = [sem(f"variance_made{k}") for k in range(2)]
        deviated = [sem(f"deviation_made{k}") for k in range(2)]
        gathered = [sem(f"rows_gathered{s}") for s in range(2 * SLOTS)]
        slot_claimed = sem("rows_slot_claimed")
        stats_made = sem("row_statistics_made")
        slot_used = [sem(f"rows_used{s}") for s in range(2 * SLOTS)]
        bcast_in = [sem(f"item_rows_broadcast{s}") for s in range(2)]
        onehot_made = [sem(f"onehot_made{s}") for s in range(2)]
        score_mm = [sem(f"score_products_made{s}") for s in range(2)]
        score_read = [sem(f"score_products_read{s}") for s in range(2)]
        pair_mm = sem("pair_products_made")
        pair_read = sem("pair_products_read")
        seg_in = sem("segment_rows_loaded")
        seg_t = sem("score_transposes_made")
        seg_copied = sem("score_transposes_copied")
        seg_small = sem("chunk_rows_made")
        seg_dve = sem("chunk_rows_used")
        seg_exp = sem("numerators_made")
        seg_back = sem("numerators_transposed")
        weighted_made = sem("weighted_rows_made")
        sum_mm = sem("sums_made")
        sum_added = sem("sums_added")
        block = ctx.enter_context(nc.Block())

        STAGES = ["items", "node1", "score1", "soft1", "sum1", "node2", "score2", "soft2", "sum2",
                  "node3", "score3", "soft3", "sum3", "final"]

        def begin(eng, name, others):
            k = STAGES.index(name)
            for o in others:
                if k:
                    eng.wait_ge(phase[o], k)

        def pipeline(fori, steps, chain=None, per_block=0):
            lags = max(lag for lag, _ in steps)
            assert lags <= UB

            def iteration(t, j, fixed):
                for lag, work in steps:
                    b = t * UB + j - lag if fixed else None
                    if fixed and not 0 <= b < BLOCKS:
                        continue
                    if fixed:
                        work(b // UB, b % UB)
                    else:
                        work(t + (j - lag) // UB, (j - lag) % UB)

            for j in range(UB):
                iteration(0, j, True)
            with fori(0, BTURNS - 1) as t:
                if chain:
                    chain.enter(t, UB * per_block)
                for j in range(UB):
                    iteration(t + 1, j, False)
                if chain:
                    chain.leave(BTURNS - 1)
            for j in range(lags):
                iteration(BTURNS, j, True)

        def early(t, j, k):
            return isinstance(t, int) and t * UB + j < k

        def nth_block(t, j, stage_no, off):
            return t * UB + (j + off + stage_no * BLOCKS)

        def product_bank(j):
            return (0, 1, 2, 0, 1)[j]

        def block_of(buf, t, j):
            return buf[:, bass.ds(t * UB + j, 1)]

        def uses(n, s):
            return sum((GROUPS - 1 - s) // ring + 1 for ring in RINGS[0:n] if s < ring)

        x_t_d = a["x_t"].rearrange("(k p) n -> p k n", k=2)

        def halves(w):
            return w.rearrange("(k p) n -> p k n", k=2)

        def nth(u, s):
            return u * (SLOTS // 2) + s // 2

        HALF = GROUPS // 2

        @block.sync
        def _(sp):
            def end():
                sp.sem_inc(phase["sp"], 1)

            sp.wait_ge(consts, 1)
            full, tail = E // P, E % P
            for k, name in enumerate(["src", "dst", "edge_type_64"]):
                v = a[name]
                w = v[0:(TCH - 1) * P * P].rearrange("(c p e) -> p c e", c=TCH - 1, e=P)
                sp.dma_start(tiles_i[:, k, 0:TCH - 1, :], w).then_inc(edges_in, 16)
                m = full - (TCH - 1) * P
                w = v[(TCH - 1) * P * P:full * P].rearrange("(p e) -> p e", e=P)
                sp.dma_start(tiles_i[0:m, k, TCH - 1, :], w).then_inc(edges_in, 16)
                w = v[full * P:E].rearrange("(p e) -> p e", p=1)
                sp.dma_start(tiles_i[m:m + 1, k, TCH - 1, 0:tail], w).then_inc(edges_in, 16)
            after = a["dst"][1:E]
            m = full - (TCH - 1) * P
            w = after[0:(TCH - 1) * P * P].rearrange("(c p e) -> p c e", c=TCH - 1, e=P)
            sp.dma_start(next_i[:, 0:TCH - 1, :], w).then_inc(edges_in, 16)
            w = after[(TCH - 1) * P * P:full * P].rearrange("(p e) -> p e", e=P)
            sp.dma_start(next_i[0:m, TCH - 1, :], w).then_inc(edges_in, 16)
            w = after[full * P:E - 1].rearrange("(p e) -> p e", p=1)
            sp.dma_start(next_i[m:m + 1, TCH - 1, 0:tail - 1], w).then_inc(edges_in, 16)
            sp.wait_ge(order_known, 1)
            unsorted = sp.value_load(order_flag[0:1, 0:1], min_val=0, max_val=1)
            with sp.If(unsorted != 0):
                sp.wait_ge(sort_done, 1)
                with nc.allow_non_contiguous_dma(reason="only for edges out of order"):
                    for k, name in enumerate(["src", "dst", "edge_type_64"]):
                        w = a[name][0:full * P].rearrange("(t e) -> e t", e=P)
                        sp.dma_start(sort_cols[:, k, 0:full], w).then_inc(sort_cols_in, 16)
                        w = a[name][full * P:E].rearrange("(e t) -> e t", t=1)
                        sp.dma_start(sort_cols[0:tail, k, full:full + 1], w).then_inc(sort_cols_in, 16)
                with nc.sync.Fori(0, full // 2) as t:
                    for k in range(2):
                        sp.wait_ge(sort_row_used[k], t + 1)
                        row = a["dst"][bass.ds(t * (2 * P) + k * P, P)]
                        sp.dma_start(sort_row_i[:, k], row.partition_broadcast(P)).then_inc(sort_row_in[k], 16)
                sp.wait_ge(sort_done, 2)
                row = a["dst"][full * P:E]
                sp.dma_start(sort_row_i[:, 0, 0:tail], row.partition_broadcast(P)).then_inc(sort_row_in[0], 16)
                sp.wait_ge(sort_done, 3)
                for c in range(TCH):
                    k = min(P, TILES - c * P)
                    sp.wait_ge(sort_back_used, c)
                    w = sorted_d[c * P * P:(c * P + k) * P, :].rearrange("(p e) k -> p (e k)", e=P)
                    sp.dma_start(sort_back[0:k, :], w).then_inc(sort_back_in, 16)
                sp.wait_ge(sort_back_used, TCH)
            sp.dma_start(w_a[:, :, 0:D], halves(a["fc1_t"])).then_inc(weights_in[0], 16)
            sp.dma_start(w_a[:, :, D:2 * D], halves(a["wb0_t"])).then_inc(weights_in[0], 16)
            sp.dma_start(bias_all[:, 1, :], a["bb0"].broadcast_to([P, D])).then_inc(weights_in[0], 16)
            sp.wait_ge(edge_dve, 4)
            for k, name in enumerate(row_names):
                w = rows_d[name][0:(ICH - 1) * P, :].rearrange("(c p) e -> p c e", p=P)
                sp.dma_start(w, rows_t[k][:, 0:ICH - 1, :]).then_inc(rows_stored, 16)
                sp.dma_start(rows_d[name][(ICH - 1) * P:ITEMS, :],
                             rows_t[k][0:LAST, ICH - 1, :]).then_inc(rows_stored, 16)
            sp.wait_ge(rows_stored, 2 * 4 * 16)
            end()

            def load_xt(stage_no):
                def go(t, j):
                    if not early(t, j, UB):
                        sp.wait_ge(node_mm, nth_block(t, j, stage_no, 1 - UB))
                    sp.dma_start(x_t[:, j], x_t_d[:, :, bass.ds((t * UB + j) * P, P)]).then_inc(x_loaded[j], 16)
                return go

            def load_x(t, j):
                if not early(t, j, UB):
                    sp.wait_ge(x_used, nth_block(t, j, 0, 1 - UB))
                sp.dma_start(x_n[:, j], a["x"][bass.ds((t * UB + j) * P, P), :]).then_inc(x_loaded[j], 16)

            def load_v(t, j):
                if not early(t, j, UB):
                    sp.wait_ge(x_used, nth_block(t, j, 1, 1 - UB))
                sp.dma_start(stage[:, j, 1], tab_v[bass.ds((t * UB + j) * P, P), :]).then_inc(x_loaded[j], 16)

            def store(stage_no, *tables):
                def go(t, j):
                    sp.wait_ge(node_act, nth_block(t, j, stage_no, 1))
                    for k, table in enumerate(tables):
                        sp.dma_start(table[bass.ds((t * UB + j) * P, P), :], stage[:, j, k]).then_inc(node_stored[j], 16)
                return go

            def stored(count):
                for j in range(UB):
                    sp.wait_ge(node_stored[j], 16 * count)

            begin(sp, "node1", ["dve", "pe", "act"])
            for k, name in enumerate(["attn_l1", "attn_r1"]):
                sp.dma_start(attn[:, k, :], a[name].broadcast_to([P, D])).then_inc(weights_in[0], 16)
            pipeline(nc.sync.Fori, [(0, load_xt(0)), (4, store(0, tab_feat1))])
            stored(BTURNS)
            end()

            def score_rows(layer, name, first):
                begin(sp, name, ["dve", "pe", "act"])
                flat = [rows_d[x].rearrange("i e -> (i e)") for x in (first, "block_dst")]
                with nc.sync.Fori(0, TURNS) as u:
                    for s in range(SLOTS):
                        sp.wait_ge(onehot_made[s % 2], nth(u, s) + (layer * HALF + 1))
                        for k in range(2):
                            row = flat[k][bass.ds(u * (STEP * P) + s * GROUP * P, GROUP * P)]
                            sp.dma_start(bcast[:, s % 2, k], row.partition_broadcast(P)).then_inc(bcast_in[s % 2], 16)
                end()

            def seg_rows(name, heads, chunks):
                begin(sp, name, ["dve", "pe", "act"])
                n = ITEMS // chunks * P
                row = rows_d["dst"].rearrange("(c j) e -> c (j e)", c=chunks)
                for h in range(heads):
                    sp.dma_start(seg[0][h * chunks:(h + 1) * chunks, 0:n], row).then_inc(seg_in, 16)
                end()

            score_rows(0, "score1", "src_low")
            seg_rows("soft1", H1, P // H1)
            begin(sp, "sum1", [])
            end()

            begin(sp, "node2", ["dve", "pe", "act"])
            sp.dma_start(w_a[:, :, 0:D], halves(a["fc2_t"])).then_inc(weights_in[1], 16)
            sp.dma_start(w_a[:, :, D:2 * D], halves(a["wb1_t"][D:2 * D, :])).then_inc(weights_in[1], 16)
            sp.dma_start(w_b[:], halves(a["wb1_t"][0:D, :])).then_inc(weights_in[1], 16)
            sp.dma_start(bias_all[:, 1, :], a["bb1"].broadcast_to([P, D])).then_inc(weights_in[1], 16)
            sp.dma_start(bias1_col[:], a["bias1"]).then_inc(weights_in[1], 16)
            for k, name in enumerate(["attn_l2", "attn_r2"]):
                sp.dma_start(attn[:, k, :], a[name].broadcast_to([P, D])).then_inc(weights_in[1], 16)
            pipeline(nc.sync.Fori, [(0, load_xt(1)), (4, store(1, tab_feat2))])
            stored(2 * BTURNS)
            end()
            score_rows(1, "score2", "src_low")
            seg_rows("soft2", H2, ITEMS // 4)
            begin(sp, "sum2", [])
            end()

            begin(sp, "node3", ["dve", "pe", "act"])
            for k, name in enumerate(["wq", "wk", "wv"]):
                sp.dma_start(w_a[:, :, k * D:(k + 1) * D], halves(a[name])).then_inc(weights_in[2], 16)
            for k, name in enumerate(["bq", "bk", "bv"]):
                sp.dma_start(bias_row[:, k * D:(k + 1) * D], a[name]).then_inc(weights_in[2], 16)
            sp.dma_start(bias_all[:, 0, :], a["bias2"].broadcast_to([P, D])).then_inc(weights_in[2], 16)
            sp.dma_start(query_col[:], a["query"]).then_inc(weights_in[2], 16)
            sp.dma_start(rel_sb[:], a["rel"]).then_inc(weights_in[2], 16)
            sp.wait_ge(bias_made, 1)
            for k in range(3):
                sp.dma_start(bias_parts[k:k + 1, :], bias_split[:, k]).then_inc(bias_in, 16)
            pipeline(nc.sync.Fori, [(0, load_x), (4, store(2, tab_k, tab_v))])
            stored(4 * BTURNS)
            end()
            score_rows(2, "score3", "type")
            seg_rows("soft3", H3, P // H3)
            begin(sp, "sum3", [])
            end()

            begin(sp, "final", ["dve", "pe", "act"])
            sp.dma_start(w_b[:], halves(a["wo"])).then_inc(weights_in[3], 16)
            sp.dma_start(bias_row[:, 0:D], a["bo"]).then_inc(weights_in[3], 16)
            for k, name in enumerate(["gamma", "beta"]):
                sp.dma_start(bias_all[:, k, :], a[name].broadcast_to([P, D])).then_inc(weights_in[3], 16)

            sp.wait_ge(bias_made, 2)
            for k in range(3):
                sp.dma_start(bias_parts[k:k + 1, 0:D], bias_split[:, k, 0:D]).then_inc(bias_in, 16)

            def store_out(t, j):
                sp.wait_ge(out_made, nth_block(t, j, 0, 1))
                last = isinstance(t, int) and t * UB + j == BLOCKS - 1
                m = N - (BLOCKS - 1) * P if last else P
                sp.dma_start(out[bass.ds((t * UB + j) * P, m), :], stage[0:m, j, 0]).then_inc(node_stored[j], 16)

            pipeline(nc.sync.Fori, [(0, load_v), (5, store_out)])
            stored(5 * BTURNS)

        @block.gpsimd
        def _(pool):
            step = Count(pool_step)

            def did(ins):
                ins.then_inc(pool_step, 1)
                step.add()
                pool.wait_ge(pool_step, step.value())

            did(nc.gpsimd.memset(tiles_i[:, :, TCH - 1, :], 0))
            did(nc.gpsimd.memset(tiles_i[:, 1, TCH - 1, :], PAD_DST))
            did(nc.gpsimd.memset(next_i[:, TCH - 1, :], PAD_DST))
            pool.sem_inc(consts, 1)
            for credit in slot_used + onehot_made + score_read + sort_row_used:
                pool.sem_inc(credit, 1)
            nc.gpsimd.memset(ones[:], 1.0)
            nc.gpsimd.memset(eps_col[:], EPS)
            nc.gpsimd.memset(ones_parts[:], 1.0)
            did(nc.gpsimd.memset(ident[:], 0.0))
            nc.gpsimd.affine_select(out=ident[:], in_=ident[:], compare_op=ALU.not_equal, fill=1.0, base=0,
                                    pattern=[[1, P]], channel_multiplier=-1)
            nc.gpsimd.affine_select(out=below[:], in_=ones[:], compare_op=ALU.is_gt, fill=0.0, base=0,
                                    pattern=[[1, P]], channel_multiplier=-1)
            nc.gpsimd.affine_select(out=before_edge[:], in_=ones[:], compare_op=ALU.is_gt, fill=0.0, base=0,
                                    pattern=[[-1, P]], channel_multiplier=1)
            nc.gpsimd.iota(iota_free[:], [[1, ITEMS]], base=0, channel_multiplier=0,
                           allow_small_or_imprecise_dtypes=True)
            nc.gpsimd.iota(part_no[:], [[0, 1]], base=0, channel_multiplier=1,
                           allow_small_or_imprecise_dtypes=True)
            did(nc.gpsimd.iota(tile_no[:], [[P, TCH]], base=0, channel_multiplier=1,
                               allow_small_or_imprecise_dtypes=True))
            pool.sem_inc(consts, 1)

            pool.wait_ge(order_known, 1)
            unsorted = pool.value_load(order_flag[0:1, 0:1], min_val=0, max_val=1)
            with pool.If(unsorted != 0):
                pool.wait_ge(sort_ranked, 1)
                nc.gpsimd.memset(sort_record, 0).then_inc(sort_copied, 1)
                pool.wait_ge(sort_copied, 1)
                with nc.gpsimd.Fori(0, TILES) as t:
                    pool.wait_ge(sort_scattered, t * 16)
                    nc.gpsimd.tensor_copy(sort_record[:, 0:4], sort_cols[:, :, bass.ds(t, 1)]).then_inc(sort_copied, 1)
                    pool.wait_ge(sort_copied, t + 2)
                    pool.sem_inc(sort_ready, 1)
                    nc.gpsimd.indirect_dma_start(
                        sorted_d, bass.IndirectOffsetOnAxis(ap=sort_record[:, 3:4], axis=0), sort_record, None,
                    ).then_inc(sort_scattered, 16)
                pool.wait_ge(sort_scattered, TILES * 16)
                pool.sem_inc(sort_done, 1)

            def gathers(n, table, name):
                ring, turns, rest = RINGS[n], (GROUPS - 1) // RINGS[n], (GROUPS - 1) % RINGS[n] + 1
                pool.wait_ge(phase["sp"], STAGES.index(name) + 1)

                def indices(u, s):
                    for k in (s, s + 1):
                        pool.wait_ge(gathered[k], u * (16 * GROUP) + (uses(n, k) * 16 * GROUP))
                    nc.gpsimd.tensor_copy(
                        index_slot[:, s:s + 2].rearrange("p s g -> p (s g)"),
                        src_i[:, bass.ds(u * (ring * GROUP) + s * GROUP, 2 * GROUP)]).then_inc(pool_step, 1)

                def gather(u, s):
                    if s % 2 == 0:
                        pool.wait_ge(pool_step, u * (ring // 2) + (s // 2 + 1 + step.n))
                    elif isinstance(u, bass.RegisterHandle) or s + 1 < rest or u < turns:
                        indices(u + (s + 1) // ring, (s + 1) % ring)
                    pool.wait_ge(slot_used[s], u + (uses(n, s) + 1))
                    pool.sem_inc(slot_claimed, 1)
                    for g in range(GROUP):
                        nc.gpsimd.indirect_dma_start(
                            row_slots[s][:, g, :], None, table,
                            bass.IndirectOffsetOnAxis(ap=index_slot[:, s, g:g + 1], axis=0),
                        ).then_inc(gathered[s], 16)

                indices(0, 0)
                with nc.gpsimd.Fori(0, turns) as u:
                    for s in range(ring):
                        gather(u, s)
                for s in range(rest):
                    gather(turns, s)
                step.add(GROUPS // 2)

            gathers(0, tab_feat1, "node1")
            gathers(1, tab_feat2, "node2")
            gathers(2, tab_k, "node3")
            gathers(3, tab_v, "node3")

        @block.tensor
        def _(pe):
            def end():
                pe.sem_inc(phase["pe"], 1)

            pe.wait_ge(consts, 2)
            pe.wait_ge(order_dve, 1)
            nc.tensor.matmul(ps[0:1, 7, 0:1], order_col[:, 0:1], ones[:, 0:1], start=True, stop=True).then_inc(order_pe, 1)
            pe.wait_ge(edge_dve, 1)
            nc.tensor.matmul(ps[:, 0, 0:TCH], below[:], tile_s[:, 4, :], start=True, stop=True)
            nc.tensor.matmul(ps[:, 1, 0:TCH], ones[:], tile_s[:, 4, :], start=True, stop=True).then_inc(edge_pe, 1)
            pe.wait_ge(edge_dve, 2)
            for k in range(5):
                for c in range(TCH):
                    lhs = tiles_f[:, k, c, :] if k < 3 else ones[:]
                    rhs = bsel[:, c, :] if k == 3 else sel[:, c, :]
                    last = nc.tensor.matmul(ps[:, k, 0:ITEMS], lhs, rhs, start=c == 0, stop=c == TCH - 1)
            last.then_inc(edge_pe, 1)
            pe.wait_ge(edge_dve, 3)
            for k in range(4):
                w = item_f[:, k, :] if k != 1 else block_dst[:]
                for c in range(ICH):
                    m = P if c < ICH - 1 else LAST
                    last = nc.tensor.transpose(ps[0:m, k, c * P:(c + 1) * P], w[:, c * P:c * P + m], ident[:])
            last.then_inc(edge_pe, 1)
            pe.wait_ge(edge_pe, 3)
            end()

            begin(pe, "node1", ["dve", "act"])
            pe.wait_ge(weights_in[0], 5 * 16)
            pe.wait_ge(edge_dve, 5)

            def products_free(t, j, stage_no):
                if not early(t, j, 2):
                    pe.wait_ge(node_dve, nth_block(t, j, stage_no, -1))

            def terms(lhs, j):
                for k in range(2):
                    last = nc.tensor.matmul(ps[:, 3 + j, 256:272], lhs[:, j, k, :],
                                            w_el[:, k].rearrange("p a h -> p (a h)"), start=k == 0, stop=k == 1)
                return last

            def node1_products(t, j):
                pe.wait_ge(x_loaded[j], (t + 1) * 16)
                products_free(t, j, 0)
                for k in range(2):
                    nc.tensor.matmul(ps[:, product_bank(j), :], x_t[:, j, k, :], w_a[:, k, 0:2 * D],
                                     start=k == 0, stop=k == 1)
                terms(x_t, j).then_inc(node_mm, 1)

            pipeline(nc.tensor.Fori, [(0, node1_products)])
            pe.wait_ge(node_mm, BLOCKS)
            end()

            regs = [pe.alloc_register(f"pe_block{g}") for g in range(GROUP)]

            def blocks(u, s):
                pe.load(regs, block_i[0:1, bass.ds(u * STEP + s * GROUP, GROUP)])
                return [pe.snap(r, min_val=0, max_val=BLOCKS - 1) for r in regs]

            def gat_scores(layer, name, heads):
                begin(pe, name, ["dve", "act", "sp"])
                w = BLOCKS * heads
                er_blocks = er_parts[:, 0:3 * w].rearrange("p (b x) -> p b x", b=BLOCKS)
                with nc.tensor.Fori(0, TURNS) as u:
                    for s in range(SLOTS):
                        bs = blocks(u, s)
                        pe.wait_ge(onehot_made[s % 2], nth(u, s) + (layer * HALF + 2))
                        pe.wait_ge(score_read[s % 2], nth(u, s) + (layer * HALF + 1))
                        for g in range(GROUP):
                            bank, at = s % 2 * 4 + g // 2, g % 2 * D
                            e = slice(g * P, (g + 1) * P)
                            for k in range(3):
                                nc.tensor.matmul(ps[:, bank, at:at + w], onehot_t[:, s % 2, 0, e],
                                                 el_parts[:, k, 0:w], start=k == 0, stop=k == 2)
                            last = nc.tensor.matmul(ps[:, bank, at + w:at + w + 3 * heads], onehot_t[:, s % 2, 1, e],
                                                    er_blocks[:, bass.ds(bs[g], 1), :].rearrange("p a x -> p (a x)"),
                                                    start=True, stop=True)
                        last.then_inc(score_mm[s % 2], 1)
                for s in range(2):
                    pe.wait_ge(score_mm[s], (layer + 1) * HALF)
                end()

            def pair_scores(layer, name):
                begin(pe, name, ["dve", "act", "sp"])
                with nc.tensor.Fori(0, TURNS) as u:
                    for s in range(SLOTS):
                        bs = blocks(u, s)
                        pe.wait_ge(onehot_made[s % 2], nth(u, s) + (layer * HALF + 2))
                        for g in range(GROUP):
                            pe.wait_ge(pair_read, u * STEP + (s * GROUP + g + 1))
                            e = slice(g * P, (g + 1) * P)
                            for k in range(3):
                                part = query_parts[:, k, bass.ds(bs[g], 1), :].rearrange("p a d -> p (a d)")
                                nc.tensor.matmul(ps[:, g, 0:D], onehot_t[:, s % 2, 1, e], part,
                                                 start=k == 0, stop=k == 2)
                            for k in range(3):
                                last = nc.tensor.matmul(ps[:, g, D:D + R], onehot_t[0:R, s % 2, 0, e],
                                                        rel_parts[:, k, :], start=k == 0, stop=k == 2)
                            last.then_inc(pair_mm, 1)
                pe.wait_ge(pair_mm, ITEMS)
                end()

            def soft(n, name, heads, chunks):
                begin(pe, name, ["dve", "act"])
                each = ITEMS // chunks
                m = heads * chunks
                for j in range(each):
                    last = nc.tensor.transpose(ps[0:m, j // 4, j % 4 * P:(j % 4 + 1) * P],
                                               scores[:, j:ITEMS * heads:each], ident[:])
                last.then_inc(seg_t, 1)
                pe.wait_ge(seg_dve, 3 * n + 1)
                for k in range(4):
                    last = nc.tensor.matmul(ps[0:1, 0, k * P:k * P + m], chunk_col[0:m, k:k + 1], ident[0:m, 0:m],
                                            start=True, stop=True)
                last.then_inc(seg_small, 1)
                pe.wait_ge(seg_dve, 3 * n + 2)
                for k in range(2):
                    last = nc.tensor.matmul(ps[0:m, 1, k:k + 1], chunk_row[:, 8 + k, 0:m], ones[0:1, 0:1],
                                            start=True, stop=True)
                last.then_inc(seg_small, 1)
                pe.wait_ge(seg_exp, n + 1)
                for j in range(each):
                    last = nc.tensor.transpose(ps[:, j // 4, j % 4 * m:(j % 4 + 1) * m],
                                               seg[1][0:m, j * P:(j + 1) * P], ident[0:m, 0:m])
                last.then_inc(seg_back, 1)
                pe.wait_ge(seg_back, n + 1)
                end()

            def sums(n, name, heads, width):
                begin(pe, name, ["dve", "act"])
                with nc.tensor.Fori(0, TURNS) as u:
                    for s in range(SLOTS):
                        pe.wait_ge(weighted_made, u * SLOTS + (s + 1 + n * GROUPS))
                        for g in range(GROUP):
                            pe.wait_ge(sum_added, u * STEP + (s * GROUP + g + 1 + n * (ITEMS + GROUP)))
                            nc.tensor.matmul(ps[:, g, 0:width], onehot[:, s % 2, g, :], weighted[:, s % 2, g, 0:width],
                                             start=True, stop=True).then_inc(sum_mm, 1)
                pe.wait_ge(sum_mm, (n + 1) * ITEMS)
                end()

            def transposes(before):
                def go(t, j):
                    pe.wait_ge(h_made, nth_block(t, j, before, 1))
                    for k in range(2):
                        last = nc.tensor.transpose(ps[:, 3 + j, k * P:(k + 1) * P], h_n[:, j, k * P:(k + 1) * P], ident[:])
                    last.then_inc(t_made, 1)
                return go

            gat_scores(0, "score1", H1)
            soft(0, "soft1", H1, P // H1)
            sums(0, "sum1", H1, AW)

            begin(pe, "node2", ["dve", "act"])
            pe.wait_ge(weights_in[1], 7 * 16)
            pe.wait_ge(edge_dve, 6)

            def node2_products(t, j):
                bank = product_bank(j)
                pe.wait_ge(ht_copied, nth_block(t, j, 0, 1))
                pe.wait_ge(x_loaded[j], (t + (BTURNS + 1)) * 16)
                products_free(t, j, 1)
                for k in range(2):
                    nc.tensor.matmul(ps[:, bank, :], h_t[:, j, k, :], w_a[:, k, 0:2 * D], start=k == 0, stop=False)
                for k in range(2):
                    nc.tensor.matmul(ps[:, bank, D:2 * D], x_t[:, j, k, :], w_b[:, k, :], start=False, stop=k == 1)
                terms(h_t, j).then_inc(node_mm, 1)

            pipeline(nc.tensor.Fori, [(0, transposes(0)), (1, node2_products)])
            pe.wait_ge(node_mm, 2 * BLOCKS)
            end()

            gat_scores(1, "score2", H2)
            soft(1, "soft2", H2, ITEMS // 4)
            sums(1, "sum2", H2, D + H2)

            begin(pe, "node3", ["dve", "act"])
            pe.wait_ge(weights_in[2], 9 * 16)
            pe.wait_ge(bias_in, 3 * 16)

            def node3_products(t, j):
                pe.wait_ge(ht_copied, nth_block(t, j, 1, 1))
                products_free(t, j, 2)
                for at, w0, w1 in ((ps[:, product_bank(j), :], 0, 2 * D), (ps[:, 3 + j, D:2 * D], 2 * D, 3 * D)):
                    for k in range(2):
                        nc.tensor.matmul(at, h_t[:, j, k, :], w_a[:, k, w0:w1], start=k == 0, stop=False)
                    last = nc.tensor.matmul(at, ones_parts[:], bias_parts[:, w0:w1], start=False, stop=True)
                last.then_inc(node_mm, 1)

            pipeline(nc.tensor.Fori, [(0, transposes(1)), (1, node3_products)])
            pe.wait_ge(node_mm, 3 * BLOCKS)
            end()

            pair_scores(2, "score3")
            soft(2, "soft3", H3, P // H3)
            sums(2, "sum3", H3, D + H3)

            begin(pe, "final", ["dve", "act"])
            pe.wait_ge(weights_in[3], 4 * 16)
            pe.wait_ge(bias_in, 6 * 16)

            def final_products(t, j):
                at = ps[:, product_bank(j), 0:D]
                pe.wait_ge(ht_copied, nth_block(t, j, 2, 1))
                products_free(t, j, 3)
                for k in range(2):
                    nc.tensor.matmul(at, h_t[:, j, k, :], w_b[:, k, :], start=k == 0, stop=False)
                nc.tensor.matmul(at, ones_parts[:], bias_parts[:, 0:D], start=False, stop=True).then_inc(node_mm, 1)

            pipeline(nc.tensor.Fori, [(0, transposes(2)), (1, final_products)])

        @block.scalar
        def _(act):
            step = Count(act_step)

            def did(ins):
                ins.then_inc(act_step, 1)
                step.add()
                act.wait_ge(act_step, step.value())

            def end():
                act.sem_inc(phase["act"], 1)

            def idle(name):
                begin(act, name, ["act"])
                end()

            idle("items")

            def copy_transposes(before, bias=None, func=ACT.Identity, keep=False):
                def go(t, j):
                    act.wait_ge(t_made, nth_block(t, j, before, 1))
                    if keep:
                        nc.scalar.copy(block_of(base, t, j), h_n[:, j:j + 1])
                    if not early(t, j, UB):
                        act.wait_ge(node_mm, nth_block(t, j, before + 1, 1 - UB))
                    if bias is None:
                        last = nc.scalar.copy(h_t[:, j], ps[:, 3 + j, 0:D].rearrange("p (k n) -> p k n", k=2))
                    else:
                        for k in range(2):
                            last = nc.scalar.activation(h_t[:, j, k], ps[:, 3 + j, k * P:(k + 1) * P], func,
                                                        bias=bias[:, k:k + 1])
                    last.then_inc(ht_copied, 1)
                return go

            def gat_copies(stage_no, heads):
                def go(t, j):
                    act.wait_ge(node_mm, nth_block(t, j, stage_no, 1))
                    act.wait_ge(node_stored[j], t * 16 + 16 * stage_no * BTURNS)
                    nc.scalar.copy(stage[:, j, 0, :], ps[:, product_bank(j), 0:D])
                    got = ps[:, 3 + j, 256:272].rearrange("p (a h) -> p a h", a=2)
                    el_v = el[:, 0:BLOCKS * heads].rearrange("p (b h) -> p b h", h=heads)
                    nc.scalar.copy(block_of(el_v, t, j), got[:, 0:1, 0:heads])
                    nc.scalar.copy(block_of(er, t, j)[:, :, 0:heads], got[:, 1:2, 0:heads]).then_inc(node_act, 1)
                return go

            def soft(n, name, heads, chunks):
                begin(act, name, ["dve", "pe"])
                each, m = ITEMS // chunks, heads * chunks
                act.wait_ge(seg_t, n + 1)
                for bank in range(-(-each // 4)):
                    k = min(4, each - 4 * bank) * P
                    last = nc.scalar.copy(seg[1][0:m, 4 * bank * P:4 * bank * P + k], ps[0:m, bank, 0:k])
                last.then_inc(seg_copied, 1)
                act.wait_ge(seg_dve, 3 * n + 3)
                nc.scalar.activation(seg[1][0:m, 0:each * P], seg[1][0:m, 0:each * P], ACT.Exp).then_inc(seg_exp, 1)
                act.wait_ge(seg_back, n + 1)
                view = scores[:, 0:ITEMS * heads].rearrange("p (m j) -> p j m", j=each)
                for bank in range(-(-each // 4)):
                    k = min(4, each - 4 * bank)
                    last = nc.scalar.copy(view[:, 4 * bank:4 * bank + k],
                                          ps[:, bank, 0:k * m].rearrange("p (j m) -> p j m", j=k))
                did(last)
                end()

            def deviation(before, at):
                def go(t, j):
                    act.wait_ge(variance[at], nth_block(t, j, before, 1))
                    nc.scalar.activation(small[:, j, 16 * at + 8:16 * at + 9], small[:, j, 16 * at + 7:16 * at + 8],
                                         ACT.Sqrt, bias=eps_col[:]).then_inc(deviated[at], 1)
                return go

            begin(act, "node1", ["dve", "pe"])
            pipeline(nc.scalar.Fori, [(0, gat_copies(0, H1))])
            act.wait_ge(node_act, BLOCKS)
            end()
            idle("score1")
            soft(0, "soft1", H1, P // H1)
            idle("sum1")

            begin(act, "node2", ["dve", "pe"])
            act.wait_ge(weights_in[1], 7 * 16)
            pipeline(nc.scalar.Fori, [(0, copy_transposes(0, bias1_col, ACT.Relu)), (1, gat_copies(1, H2))])
            act.wait_ge(node_act, 2 * BLOCKS)
            end()
            idle("score2")
            soft(1, "soft2", H2, ITEMS // 4)
            idle("sum2")

            begin(act, "node3", ["dve", "pe"])
            act.wait_ge(weights_in[2], 9 * 16)
            did(nc.scalar.mul(query_col[:], query_col[:], 0.1))
            did(nc.scalar.mul(rel_sb[:], rel_sb[:], 0.2))

            def kv_copies(t, j):
                act.wait_ge(node_mm, nth_block(t, j, 2, 1))
                act.wait_ge(node_stored[j], t * 32 + 16 * 2 * BTURNS)
                nc.scalar.copy(stage[:, j, 0, :], ps[:, product_bank(j), D:2 * D])
                nc.scalar.copy(stage[:, j, 1, :], ps[:, 3 + j, D:2 * D]).then_inc(node_act, 1)

            pipeline(nc.scalar.Fori, [(0, deviation(0, 0)), (1, copy_transposes(1, query_col, keep=True)),
                                      (2, kv_copies)])
            act.wait_ge(node_act, 3 * BLOCKS)
            end()
            idle("score3")
            soft(2, "soft3", H3, P // H3)
            idle("sum3")

            begin(act, "final", ["dve", "pe"])
            pipeline(nc.scalar.Fori, [(0, copy_transposes(2)), (2, deviation(1, 0)), (3, deviation(0, 1))])

        @block.vector
        def _(dve):
            step = Count(dve_step)
            vec = nc.vector

            def did(ins):
                ins.then_inc(dve_step, 1)
                step.add()
                dve.wait_ge(dve_step, step.value())

            def then(ins):
                ins.then_inc(dve_step, 1)
                step.add()

            def all_but(k):
                dve.wait_ge(dve_step, step.value() - k)

            def end():
                dve.sem_inc(phase["dve"], 1)

            def signal(sem):
                dve.sem_inc(sem, 1)

            def sort_edges():
                inner = Count(sort_step)

                def then(ins):
                    ins.then_inc(sort_step, 1)
                    inner.add()
                    dve.wait_ge(sort_step, inner.value())

                then(vec.memset(sort_cols[:, 0, TILES - 1:TILES], 0))
                then(vec.memset(sort_cols[:, 1, TILES - 1:TILES], PAD_DST))
                then(vec.memset(sort_cols[:, 2, TILES - 1:TILES], 0))
                then(vec.memset(sort_rank, 0.0))
                signal(sort_done)
                dve.wait_ge(sort_cols_in, 6 * 16)
                then(vec.tensor_copy(sort_dst, sort_cols[:, 1, :]))
                then(vec.tensor_scalar(sort_level, sort_dst, 0.5, None, ALU.add))

                def rank_tile(t, k):
                    then(vec.tensor_copy(sort_row, sort_row_i[:, k]))
                    signal(sort_row_used[k])
                    level = sort_level[:, bass.ds(t, 1)]
                    then(vec.tensor_scalar(level, level, -0.5, None, ALU.add))
                    then(vec.tensor_tensor(sort_same, sort_row, sort_dst[:, bass.ds(t, 1)].broadcast_to([P, P]),
                                           ALU.is_equal))
                    then(vec.tensor_tensor(sort_same, sort_same, before_edge[:], ALU.mult))
                    then(vec.tensor_reduce(order_col[:, 1:2], sort_same, AX.X, ALU.add))
                    own = sort_rank[:, bass.ds(t, 1)]
                    then(vec.tensor_tensor(own, own, order_col[:, 1:2], ALU.add))
                    for p in range(0, TILES, PIECE):
                        then(vec.tensor_tensor(
                            sort_less, sort_row.unsqueeze(1).broadcast_to([P, PIECE, P]),
                            sort_level[:, p:p + PIECE].unsqueeze(2).broadcast_to([P, PIECE, P]), ALU.is_lt))
                        then(vec.tensor_reduce(sort_dst_sum, sort_less, AX.X, ALU.add))
                        then(vec.tensor_tensor(sort_rank[:, p:p + PIECE], sort_rank[:, p:p + PIECE],
                                               sort_dst_sum, ALU.add))

                each = 6 + 3 * (TILES // PIECE)
                with vec.Fori(0, TILES // 2) as t:
                    inner.enter(t, 2 * each)
                    for k in range(2):
                        dve.wait_ge(sort_row_in[k], (t + 1) * 16)
                        rank_tile(t * 2 + k, k)
                    inner.leave(TILES // 2)
                then(vec.memset(sort_row_i[:, 0], PAD_DST))
                signal(sort_done)
                dve.wait_ge(sort_row_in[0], (TILES // 2 + 1) * 16)
                rank_tile(TILES - 1, 0)
                then(vec.tensor_copy(sort_cols[:, 3, :], sort_rank))
                signal(sort_ranked)
                for c in range(TCH):
                    k = min(P, TILES - c * P)
                    dve.wait_ge(sort_back_in, (c + 1) * 16)
                    then(vec.tensor_copy(tiles_i[0:k, :, c, :], sort_back[0:k].rearrange("p (e k) -> p k e", k=ROW)[:, 0:3, :]))
                    signal(sort_back_used)

            dve.wait_ge(consts, 2)
            dve.wait_ge(edges_in, 12 * 16)
            did(vec.tensor_tensor(falls, next_i, tiles_i[:, 1], ALU.is_lt))
            did(vec.tensor_reduce(order_col[:, 0:1], falls, AX.XY, ALU.add))
            signal(order_dve)
            dve.wait_ge(order_pe, 1)
            did(vec.tensor_scalar(order_flag[:], ps[0:1, 7, 0:1], 1.0, None, ALU.min))
            signal(order_known)
            unsorted = dve.value_load(order_flag[0:1, 0:1], min_val=0, max_val=1)
            with dve.If(unsorted != 0):
                sort_edges()
            did(vec.tensor_copy(tiles_f, tiles_i))
            tile_si = tile_s.bitcast(I32)
            lo, hi, many, start, stop, shift, total = (tile_s[:, k, :] for k in range(2, 9))
            did(vec.tensor_scalar(tile_si[:, 0, :], tiles_i[:, 1, :, 0], 7, None, ALU.arith_shift_right))
            did(vec.tensor_scalar(tile_si[:, 1, :], tiles_i[:, 1, :, P - 1], 7, None, ALU.arith_shift_right))
            did(vec.tensor_copy(tile_s[:, 2:4, :], tile_si[:, 0:2, :]))
            did(vec.tensor_tensor(many, hi, lo, ALU.subtract))
            did(vec.tensor_scalar(many, many, 1.0, None, ALU.add))
            did(vec.scalar_tensor_tensor(many, tile_no[:], float(TILES), many, ALU.is_lt, ALU.mult))
            signal(edge_dve)
            dve.wait_ge(edge_pe, 1)
            did(vec.memset(total[:, 0:1], 0.0))
            for c in range(1, TCH):
                did(vec.tensor_tensor(total[:, c:c + 1], total[:, c - 1:c], ps[:, 1, c - 1:c], ALU.add))
            did(vec.tensor_tensor(start, total, ps[:, 0, 0:TCH], ALU.add))
            did(vec.tensor_tensor(stop, start, many, ALU.add))
            did(vec.tensor_tensor(shift, lo, start, ALU.subtract))
            for c in range(TCH):
                did(vec.tensor_scalar(item_tmp, iota_free[:], start[:, c:c + 1], None, ALU.is_ge))
                did(vec.scalar_tensor_tensor(sel[:, c, :], iota_free[:], stop[:, c:c + 1], item_tmp,
                                             ALU.is_lt, ALU.mult))
                did(vec.scalar_tensor_tensor(bsel[:, c, :], iota_free[:], shift[:, c:c + 1], sel[:, c, :],
                                             ALU.add, ALU.mult))
            signal(edge_dve)
            dve.wait_ge(edge_pe, 2)
            tmp_i = item_tmp.bitcast(I32)
            did(vec.tensor_copy(src_i[:], ps[:, 0, 0:ITEMS]))
            did(vec.tensor_copy(item_f[:, 0, :], ps[:, 1, 0:ITEMS]))
            did(vec.tensor_copy(item_f[:, 3, :], ps[:, 2, 0:ITEMS]))
            did(vec.tensor_copy(block_i[:], ps[:, 3, 0:ITEMS]))
            did(vec.scalar_tensor_tensor(block_dst[:], ps[:, 3, 0:ITEMS], -float(P), item_f[:, 0, :],
                                         ALU.mult, ALU.add))
            did(vec.tensor_tensor(block_dst[:], block_dst[:], ps[:, 4, 0:ITEMS], ALU.add))
            did(vec.tensor_scalar(block_dst[:], block_dst[:], -1.0, None, ALU.add))
            did(vec.tensor_scalar(tmp_i, src_i[:], 7, None, ALU.arith_shift_right))
            did(vec.tensor_copy(src_hi[:], tmp_i))
            did(vec.tensor_scalar(tmp_i, src_i[:], P - 1, None, ALU.bitwise_and))
            did(vec.tensor_copy(item_f[:, 2, :], tmp_i))
            signal(edge_dve)
            dve.wait_ge(edge_pe, 3)
            for k in range(4):
                did(vec.tensor_copy(rows_t[k][:, 0:ICH - 1, :],
                                    ps[:, k, 0:(ICH - 1) * P].rearrange("p (c e) -> p c e", e=P)))
                did(vec.tensor_copy(rows_t[k][0:LAST, ICH - 1, :], ps[0:LAST, k, (ICH - 1) * P:ICH * P]))
            signal(edge_dve)
            end()

            def attention_columns(k, count, heads):
                dve.wait_ge(weights_in[k], 16 * count)
                for side in range(2):
                    did(vec.tensor_tensor(tmp_n[:, 0:2, :], w_a[:, :, 0:D],
                                          attn[:, side:side + 1, :].broadcast_to([P, 2, D]), ALU.mult))
                    did(vec.tensor_reduce(w_el[:, :, side, 0:heads],
                                          tmp_n[:, 0:2, :].rearrange("p k (h d) -> p k h d", h=heads), AX.X, ALU.add))
                signal(edge_dve)

            begin(dve, "node1", ["pe", "act", "sp"])
            attention_columns(0, 5, H1)
            did(vec.memset(acc[:], 0.0))

            def residual(stage_no):
                def go(t, j):
                    dve.wait_ge(node_act, nth_block(t, j, stage_no, 1))
                    vec.tensor_tensor(block_of(base, t, j), ps[:, product_bank(j), D:2 * D].unsqueeze(1),
                                      bias_all[:, 1:2, :], ALU.add).then_inc(node_dve, 1)
                return go

            pipeline(vec.Fori, [(0, residual(0))])
            dve.wait_ge(node_dve, BLOCKS)
            end()

            def split(parts, value, rest, factor=1.0):
                did(vec.tensor_scalar(rest, value, factor, None, ALU.mult))
                for k in range(3):
                    did(vec.tensor_scalar(parts[k], rest, 1.0, None, ALU.mult))
                    if k < 2:
                        did(vec.tensor_tensor(rest, rest, parts[k], ALU.subtract))

            def onehots(layer, u, s):
                z = s % 2
                dve.wait_ge(bcast_in[z], nth(u, s) * 32 + 32 * (layer * HALF + 1))
                vec.tensor_scalar(onehot_t[:, z], bcast[:, z], part_no[:], None,
                                  ALU.is_equal).then_inc(onehot_made[z], 1)

            def gat_scores(layer, name, heads):
                begin(dve, name, ["pe", "act"])
                w = BLOCKS * heads
                split([el_parts[:, k, 0:w] for k in range(3)], el[:, 0:w], el[:, 0:w])
                er_v = er[:, :, 0:heads]
                er_blocks = er_parts[:, 0:3 * w].rearrange("p (b k h) -> p b k h", b=BLOCKS, k=3)
                split([er_blocks[:, :, k, :] for k in range(3)], er_v, er_v)
                onehots(layer, 0, 0)
                onehots(layer, 0, 1)
                did(vec.memset(hi_onehot[:, :, :, BLOCKS:PICKS], 1.0))

                def hot(u, s):
                    then(vec.tensor_tensor(
                        hi_onehot[:, s % 2, :, 0:BLOCKS],
                        iota_free[:, 0:BLOCKS].unsqueeze(1).broadcast_to([P, GROUP, BLOCKS]),
                        src_hi[:, bass.ds(u * STEP + s * GROUP, GROUP)].unsqueeze(2).broadcast_to([P, GROUP, BLOCKS]),
                        ALU.is_equal))

                def turn(u, ends):
                    for s in range(SLOTS):
                        z = s % 2
                        dve.wait_ge(score_mm[z], nth(u, s) + (layer * HALF + 1))
                        got = ps[:, z * 4:z * 4 + 4, :].rearrange("p q (i x) -> p (q i) x", i=2)[:, :, 0:PICKS * heads]
                        picked = product[:, z, :, 0:PICKS * heads].rearrange("p i (h b) -> p i h b", h=heads)
                        then(vec.tensor_tensor(picked, got.rearrange("p i (b h) -> p i h b", h=heads),
                                               hi_onehot[:, z, :, 0:PICKS].unsqueeze(2).broadcast_to(
                                                   [P, GROUP, heads, PICKS]), ALU.mult))
                        if ends and s == SLOTS - 1:
                            all_but(0)
                        else:
                            hot(u + (s + 1) // SLOTS, (s + 1) % SLOTS)
                            all_but(1)
                        signal(score_read[z])
                        source = product[:, z, :, PICKS * heads:PICKS * heads + heads]
                        then(vec.tensor_reduce(source, picked, AX.X, ALU.add))
                        if not (ends and s + 2 >= SLOTS):
                            onehots(layer, u + (s + 2) // SLOTS, (s + 2) % SLOTS)
                        all_but(0)
                        vec.scalar_tensor_tensor(by_item(heads)[:, bass.ds(u * STEP + s * GROUP, GROUP), :],
                                                 source, 0.2, source, ALU.mult, ALU.max)

                hot(0, 0)
                all_but(0)
                with vec.Fori(0, TURNS - 1) as u:
                    step.enter(u, SLOTS * 3)
                    turn(u, False)
                    step.leave(TURNS - 1)
                turn(TURNS - 1, True)
                did(vec.memset(chunk_col[:, 0:1], 0.0))
                end()

            def pair_scores(layer, name):
                begin(dve, name, ["pe", "act"])
                split([rel_parts[:, k] for k in range(3)], rel_sb[:], rel_sb[:])
                dve.sem_inc(pair_read, GROUP)
                onehots(layer, 0, 0)
                onehots(layer, 0, 1)

                def turn(u, ends):
                    for s in range(SLOTS):
                        z = s % 2
                        dve.wait_ge(gathered[s], u * (16 * GROUP) + ((uses(2, s) + 1) * 16 * GROUP))
                        for g in range(GROUP + 1):
                            if g < GROUP:
                                dve.wait_ge(pair_mm, u * STEP + (s * GROUP + g + 1))
                                key = product[:, z, g, 0:D].rearrange("p (h d) -> p h d", h=H3)
                                then(vec.tensor_tensor(key, rows[:, s, g, :].rearrange("p (h d) -> p h d", h=H3),
                                                       ps[:, g, D:D + R].unsqueeze(1).broadcast_to([P, H3, R]), ALU.add))
                            if g:
                                all_but(1 if g < GROUP else 0)
                                vec.tensor_tensor(product[:, z, g - 1, 0:D], product[:, z, g - 1, 0:D],
                                                  ps[:, g - 1, 0:D], ALU.mult).then_inc(pair_read, 1)
                        signal(slot_used[s])
                        if not (ends and s + 2 >= SLOTS):
                            onehots(layer, u + (s + 2) // SLOTS, (s + 2) % SLOTS)
                        dve.wait_ge(pair_read, u * STEP + (s + 2) * GROUP)
                        vec.tensor_reduce(by_item(H3)[:, bass.ds(u * STEP + s * GROUP, GROUP), :],
                                          product[:, z, :, 0:D].rearrange("p i (h d) -> p i h d", h=H3),
                                          AX.X, ALU.add)

                with vec.Fori(0, TURNS - 1) as u:
                    step.enter(u, SLOTS * GROUP)
                    turn(u, False)
                    step.leave(TURNS - 1)
                turn(TURNS - 1, True)
                did(vec.memset(chunk_col[:, 0:1], 0.0))
                end()

            def soft(n, name, heads, chunks, rows_before):
                begin(dve, name, ["pe", "act"])
                each, m = ITEMS // chunks, heads * chunks
                L = each * P
                dst, score, gap, top = (b[0:m] for b in seg)
                dve.wait_ge(seg_in, 16 * (rows_before + heads))
                did(vec.memset(gap[:, 0:1], -BIG))
                did(vec.memset(gap[:, L:L + 1], -BIG))
                did(vec.tensor_tensor(gap[:, 1:L], dst[:, 1:L], dst[:, 0:L - 1], ALU.not_equal))
                did(vec.tensor_scalar(gap[:, 1:L], gap[:, 1:L], -BIG, None, ALU.mult))
                dve.wait_ge(seg_copied, n + 1)
                did(vec.tensor_tensor_scan(top[:, 0:L], gap[:, 0:L], score[:, 0:L], -BIG, ALU.add, ALU.max))
                did(vec.tensor_tensor_scan(top[:, 0:L][:, ::-1], gap[:, 1:L + 1][:, ::-1], top[:, 0:L][:, ::-1],
                                           -BIG, ALU.add, ALU.max))
                for k, end_v in enumerate([top[:, 0:1], top[:, L - 1:L], dst[:, 0:1], dst[:, L - 1:L]]):
                    did(vec.tensor_copy(chunk_col[0:m, k:k + 1], end_v))
                signal(seg_dve)
                dve.wait_ge(seg_small, 2 * n + 1)
                did(vec.tensor_copy(chunk_row[:, 0:4, 0:m], ps[0:1, 0, :].rearrange("p (k c) -> p k c", k=4)[:, :, 0:m]))
                head_top, tail_top, head_dst, tail_dst, whole, joint, a0, b0, before, after, a1, b1 = (
                    chunk_row[:, k, 0:m] for k in range(12))
                did(vec.tensor_tensor(whole, head_dst, tail_dst, ALU.not_equal))
                did(vec.tensor_scalar(whole, whole, -BIG, None, ALU.mult))
                did(vec.tensor_tensor(joint[:, 1:m], head_dst[:, 1:m], tail_dst[:, 0:m - 1], ALU.not_equal))
                did(vec.tensor_scalar(joint[:, 1:m], joint[:, 1:m], -BIG, None, ALU.mult))
                did(vec.memset(joint.rearrange("p (h c) -> p h c", h=heads)[:, :, 0:1], -BIG))
                for row, col in ((a0, 0), (b0, 0), (a1, m - 1), (b1, m - 1)):
                    did(vec.memset(row[:, col:col + 1], -BIG))
                did(vec.tensor_tensor(a0[:, 1:m], whole[:, 0:m - 1], joint[:, 1:m], ALU.add))
                did(vec.tensor_tensor(b0[:, 1:m], tail_top[:, 0:m - 1], joint[:, 1:m], ALU.add))
                did(vec.tensor_tensor(a1[:, 0:m - 1], whole[:, 1:m], joint[:, 1:m], ALU.add))
                did(vec.tensor_tensor(b1[:, 0:m - 1], head_top[:, 1:m], joint[:, 1:m], ALU.add))
                did(vec.tensor_tensor_scan(before, a0, b0, -BIG, ALU.add, ALU.max))
                did(vec.tensor_tensor_scan(after[:, ::-1], a1[:, ::-1], b1[:, ::-1], -BIG, ALU.add, ALU.max))
                signal(seg_dve)
                dve.wait_ge(seg_small, 2 * n + 2)
                did(vec.tensor_copy(chunk_col[0:m, 0:2], ps[0:m, 1, 0:2]))
                for k in range(2):
                    did(vec.tensor_scalar(gap[:, 0:L], dst[:, 0:L], chunk_col[0:m, 2 + k:3 + k], -BIG,
                                          ALU.not_equal, ALU.mult))
                    did(vec.scalar_tensor_tensor(top[:, 0:L], gap[:, 0:L], chunk_col[0:m, k:k + 1], top[:, 0:L],
                                                 ALU.add, ALU.max))
                did(vec.tensor_tensor(score[:, 0:L], score[:, 0:L], top[:, 0:L], ALU.subtract))
                signal(seg_dve)
                end()

            regs = [dve.alloc_register(f"dve_block{g}") for g in range(GROUP)]

            def sums(n, name, heads, width, nth_pass):
                begin(dve, name, ["pe", "act"])
                ring, turns, rest = RINGS[nth_pass], (GROUPS - 1) // RINGS[nth_pass], (GROUPS - 1) % RINGS[nth_pass] + 1
                did(vec.memset(weighted[:, :, :, DEG:AW], 1.0))
                dve.sem_inc(sum_added, GROUP)

                def build(u, s, k, peeled=False):
                    z, i = s % 2, k % 4 * 2
                    first = u * (ring * GROUP) + s * GROUP
                    if k == 0:
                        dve.wait_ge(gathered[s], u * (16 * GROUP) + ((uses(nth_pass, s) + 1) * 16 * GROUP))
                        if not peeled:
                            dve.wait_ge(sum_mm, u * (ring * GROUP) + (s * GROUP - GROUP + n * ITEMS))
                    if k < 4:
                        vec.tensor_tensor(onehot[:, z, i:i + 2], iota_free[:, 0:P].unsqueeze(1).broadcast_to([P, 2, P]),
                                          block_dst[:, bass.ds(first + i, 2)].unsqueeze(2).broadcast_to([P, 2, P]),
                                          ALU.is_equal)
                        return
                    share = by_item(heads)[:, bass.ds(first + i, 2), :]
                    if k == 4:
                        vec.tensor_copy(weighted[:, z, :, D:D + heads], by_item(heads)[:, bass.ds(first, GROUP), :])
                    done = vec.tensor_tensor(weighted[:, z, i:i + 2, 0:D].rearrange("p i (h d) -> p i h d", h=heads),
                                             row_slots[s][:, i:i + 2].rearrange("p i (h d) -> p i h d", h=heads),
                                             share.unsqueeze(3).broadcast_to([P, 2, heads, D // heads]), ALU.mult)
                    if k == 7:
                        done.then_inc(weighted_made, 1)

                def add(u, s, then_build):
                    dve.wait_ge(weighted_made, u * ring + (s + 1 + n * GROUPS))
                    dve.sem_inc(slot_used[s], 1)
                    after = (u + (s + 1) // ring, (s + 1) % ring)
                    if then_build:
                        for k in range(3):
                            build(*after, k)
                    dve.load(regs, block_i[0:1, bass.ds(u * (ring * GROUP) + s * GROUP, GROUP)])
                    bs = [dve.snap(r, min_val=0, max_val=BLOCKS - 1) for r in regs]
                    for g in range(GROUP):
                        i = s * GROUP + g
                        dve.wait_ge(sum_mm, u * (ring * GROUP) + (i + 1 + n * ITEMS))
                        dve.wait_ge(sum_added, u * (ring * GROUP) + (i + GROUP + n * (ITEMS + GROUP)))
                        to = acc[:, bass.ds(bs[g], 1), 0:width].rearrange("p a d -> p (a d)")
                        vec.tensor_tensor(to, to, ps[:, g, 0:width], ALU.add).then_inc(sum_added, 1)
                        if then_build and g < 5:
                            build(*after, g + 3)

                for k in range(8):
                    build(0, 0, k, peeled=True)
                with vec.Fori(0, turns) as u:
                    for s in range(ring):
                        add(u, s, True)
                for s in range(rest):
                    add(turns, s, s + 1 < rest)
                dve.wait_ge(sum_added, (n + 1) * (ITEMS + GROUP))
                end()

            def inverses(heads):
                did(vec.tensor_scalar(inv_sum[:, :, 0:heads], acc[:, :, D:D + heads], 0.5, None, ALU.max))
                did(vec.reciprocal(inv_sum[:, :, 0:heads], inv_sum[:, :, 0:heads]))
                did(vec.tensor_scalar(inv_deg, deg[:], 1.0, None, ALU.max))
                did(vec.reciprocal(inv_deg, inv_deg))

            def mean_rows(t, j, heads):
                did(vec.tensor_tensor(h_n[:, j].rearrange("p (h d) -> p h d", h=heads),
                                      block_of(acc, t, j)[:, 0, 0:D].rearrange("p (h d) -> p h d", h=heads),
                                      block_of(inv_sum, t, j)[:, 0, 0:heads].unsqueeze(2).broadcast_to(
                                          [P, heads, D // heads]), ALU.mult))

            def slot_free(t, j, before):
                if not early(t, j, UB):
                    dve.wait_ge(t_made, nth_block(t, j, before, 1 - UB))

            def statistics(t, j, row, at):
                did(vec.bn_stats(small[:, j, 16 * at:16 * at + 6], row))
                signal(stats_made)
                vec.bn_aggr(small[:, j, 16 * at + 6:16 * at + 8], small[:, j, 16 * at:16 * at + 6]).then_inc(variance[at], 1)

            def inverse_deviation(t, j, before, at):
                dve.wait_ge(deviated[at], nth_block(t, j, before, 1))
                got = small[:, j, 16 * at + 9:16 * at + 10]
                did(vec.reciprocal(got, small[:, j, 16 * at + 8:16 * at + 9]))
                return small[:, j, 16 * at + 6:16 * at + 7], got

            gat_scores(0, "score1", H1)
            soft(0, "soft1", H1, P // H1, 0)
            sums(0, "sum1", H1, AW, 0)

            begin(dve, "node2", ["pe", "act"])
            attention_columns(1, 7, H2)
            did(vec.tensor_copy(deg[:].unsqueeze(2), acc[:, :, DEG:AW]))
            inverses(H1)

            def node2_rows(t, j):
                slot_free(t, j, 0)
                mean_rows(t, j, H1)
                vec.scalar_tensor_tensor(h_n[:, j], block_of(base, t, j)[:, 0], inv_deg[:, bass.ds(t * UB + j, 1)],
                                         h_n[:, j], ALU.mult, ALU.add).then_inc(h_made, 1)

            pipeline(vec.Fori, [(0, node2_rows), (2, residual(1))], step, 1)
            dve.wait_ge(node_dve, 2 * BLOCKS)
            did(vec.memset(acc[:], 0.0))
            end()

            gat_scores(1, "score2", H2)
            soft(1, "soft2", H2, ITEMS // 4, H1)
            sums(1, "sum2", H2, D + H2, 1)

            begin(dve, "node3", ["pe", "act"])
            dve.wait_ge(weights_in[2], 9 * 16)
            inverses(H2)
            split([bias_split[:, k] for k in range(3)], bias_row[:], bias_row[:])
            signal(bias_made)

            def node3_rows(t, j):
                slot_free(t, j, 1)
                dve.wait_ge(x_loaded[j], (t + (2 * BTURNS + 1)) * 16)
                row = h_n[:, j]
                did(vec.scalar_tensor_tensor(row, block_of(acc, t, j)[:, 0, 0:D], block_of(inv_sum, t, j)[:, 0, 0:1],
                                             x_n[:, j], ALU.mult, ALU.add))
                signal(x_used)
                did(vec.scalar_tensor_tensor(row, block_of(base, t, j)[:, 0], inv_deg[:, bass.ds(t * UB + j, 1)], row,
                                             ALU.mult, ALU.add))
                did(vec.tensor_tensor(row, row, bias_all[:, 0, :], ALU.add))
                statistics(t, j, row, 0)

            def node3_norm(t, j):
                mean, inv = inverse_deviation(t, j, 0, 0)
                vec.tensor_scalar(h_n[:, j], h_n[:, j], mean, inv, ALU.subtract, ALU.mult).then_inc(h_made, 1)

            def query_copies(t, j):
                dve.wait_ge(node_act, nth_block(t, j, 2, 1))
                factor = float(R) ** -0.5
                got, rest = ps[:, product_bank(j), 0:D], tmp_n[:, j]
                parts = [query_parts[:, k, bass.ds(t * UB + j, 1), :][:, 0] for k in range(3)]
                did(vec.tensor_scalar(parts[0], got, factor, None, ALU.mult))
                did(vec.scalar_tensor_tensor(rest, got, factor, parts[0], ALU.mult, ALU.subtract))
                signal(node_dve)
                did(vec.tensor_scalar(parts[1], rest, 1.0, None, ALU.mult))
                did(vec.tensor_tensor(parts[2], rest, parts[1], ALU.subtract))

            pipeline(vec.Fori, [(0, node3_rows), (1, node3_norm), (3, query_copies)], step, 4 + 1 + 4)
            dve.wait_ge(node_dve, 3 * BLOCKS)
            did(vec.memset(acc[:], 0.0))
            end()

            pair_scores(2, "score3")
            soft(2, "soft3", H3, P // H3, H1 + H2)
            sums(2, "sum3", H3, D + H3, 3)

            begin(dve, "final", ["pe", "act"])
            dve.wait_ge(weights_in[3], 4 * 16)
            inverses(H3)
            did(vec.tensor_scalar(inv_deg, deg[:], 0.5, None, ALU.is_lt))
            split([bias_split[:, k, 0:D] for k in range(3)], bias_row[:, 0:D], bias_row[:, 0:D])
            signal(bias_made)

            def final_rows(t, j):
                slot_free(t, j, 2)
                mean_rows(t, j, H3)
                dve.wait_ge(x_loaded[j], (t + (3 * BTURNS + 1)) * 16)
                vec.scalar_tensor_tensor(h_n[:, j], stage[:, j, 1, :], inv_deg[:, bass.ds(t * UB + j, 1)],
                                         h_n[:, j], ALU.mult, ALU.add).then_inc(h_made, 1)
                dve.wait_ge(h_made, nth_block(t, j, 2, 1))
                signal(x_used)

            def add_input(t, j):
                dve.wait_ge(node_mm, nth_block(t, j, 3, 1))
                did(vec.tensor_tensor(tmp_n[:, j:j + 1], ps[:, product_bank(j), 0:D].unsqueeze(1),
                                      block_of(base, t, j), ALU.add))
                signal(node_dve)
                statistics(t, j, tmp_n[:, j], 0)

            def inner_norm(t, j):
                mean, inv = inverse_deviation(t, j, 1, 0)
                row = tmp_n[:, j]
                did(vec.scalar_tensor_tensor(row, row, mean, bias_all[:, 0, :], ALU.subtract, ALU.mult))
                did(vec.scalar_tensor_tensor(row, row, inv, bias_all[:, 1, :], ALU.mult, ALU.add))
                did(vec.tensor_tensor(tmp_n[:, j:j + 1], tmp_n[:, j:j + 1], block_of(base, t, j), ALU.add))
                statistics(t, j, row, 1)

            def outer_norm(t, j):
                mean, inv = inverse_deviation(t, j, 0, 1)
                dve.wait_ge(node_stored[j], t * 16 + 16 * 4 * BTURNS)
                vec.tensor_scalar(stage[:, j, 0, :], tmp_n[:, j], mean, inv, ALU.subtract,
                                  ALU.mult).then_inc(out_made, 1)

            pipeline(vec.Fori, [(0, final_rows), (2, add_input), (3, inner_norm), (4, outer_norm)], step,
                     1 + 2 + 5 + 1)


def kernel(**inputs):
    import concourse.bacc as bacc
    from concourse.bass_utils import run_bass_kernel_spmd

    def rows_of(v):
        return np.ascontiguousarray(v).reshape(1, -1)

    x = np.zeros((NP, D), inputs["x"].dtype)
    x[0:N] = inputs["x"]
    arrays = {"x": x, "x_t": np.ascontiguousarray(x.T)}
    for k in ("src", "dst", "edge_type_64"):
        arrays[k] = np.ascontiguousarray(inputs[k])
    for k in ("fc1_w", "fc2_w", "wb0", "wb1"):
        arrays[k.replace("_w", "") + "_t"] = np.ascontiguousarray(np.transpose(inputs["L0_gnn_" + k]))
    arrays["bias1"] = np.ascontiguousarray(np.reshape(inputs["L0_gnn_bias1"], (2, P)).T)
    for k in ("attn_l1", "attn_r1", "attn_l2", "attn_r2", "bias2", "bb0", "bb1"):
        arrays[k] = rows_of(inputs["L0_gnn_" + k])
    for k in ("Wq", "Wk", "Wv", "Wo"):
        arrays[k.lower()] = np.ascontiguousarray(inputs["L1_gnn_" + k])
    for k in ("bq", "bk", "bv", "bo", "gamma", "beta"):
        arrays[k] = rows_of(inputs["L1_gnn_" + k])
    arrays["query"] = np.ascontiguousarray(np.reshape(inputs["L1_gnn_query_emb"], (2, P)).T)
    arrays["rel"] = np.ascontiguousarray(inputs["L1_gnn_rel_w"])

    nc = bacc.Bacc("TRN2", target_bir_lowering=False, num_devices=1)
    a = {k: nc.dram_tensor("in_" + k, v.shape, mybir.dt.from_np(v.dtype), kind="ExternalInput").ap()
         for k, v in arrays.items()}
    out = nc.dram_tensor("out", (N, D), F32, kind="ExternalOutput").ap()
    graph_layers(nc, a, out)
    r = run_bass_kernel_spmd(nc, [{"in_" + k: v for k, v in arrays.items()}], core_ids=[0])
    return r.results[0]["out"]
```

```python
import numpy as np
import concourse.bass as bass
from concourse import mybir
from contextlib import ExitStack

F32 = mybir.dt.float32
I32 = mybir.dt.int32
I16 = mybir.dt.int16
BF16 = mybir.dt.bfloat16
ALU = mybir.AluOpType
ACT = mybir.ActivationFunctionType
AX = mybir.AxisListType

P = 128
N, E, D, R = 3125, 50000, 256, 64
BLOCKS = -(-N // P)
NP = BLOCKS * P
TILES = -(-E // P)
TCH = -(-TILES // P)
GROUP = 8
SLOTS = 4
STEP = GROUP * SLOTS
ITEMS = -(-(TILES + BLOCKS - 1) // STEP) * STEP
GROUPS = ITEMS // GROUP
TURNS = ITEMS // STEP
ICH = -(-ITEMS // P)
LAST = ITEMS - (ICH - 1) * P
H1, H2, H3 = 8, 1, 4
UB = 5
PIECE = 23
ROW = 16
RINGS = [2 * SLOTS, 2 * SLOTS, SLOTS, SLOTS]
BTURNS = BLOCKS // UB
PICKS = BLOCKS + 3
BIG = 1.0e30
PAD_DST = NP - 1
DEG = D + H1
AW = DEG + 1
EPS = 1e-5


class Count:

    def __init__(self, sem):
        self.sem, self.n, self.turn, self.per, self.at = sem, 0, None, 0, 0

    def enter(self, turn, per):
        self.turn, self.per, self.at = turn, per, self.n

    def leave(self, turns):
        assert self.n - self.at == self.per, (self.n - self.at, self.per)
        self.n = self.at + self.per * turns
        self.turn = None

    def add(self, k=1):
        self.n += k

    def value(self):
        return self.n if self.turn is None else self.turn * self.per + self.n


def graph_layers(nc, a, out):
    ctx = ExitStack()
    with ctx:
        def sb(name, shape, dt=F32):
            return ctx.enter_context(nc.sbuf_tensor(name, shape, dt))

        def sem(name):
            return ctx.enter_context(nc.semaphore(name))

        def dram(name, shape, dt=F32):
            return nc.dram_tensor(name, shape, dt).ap()

        tab_feat1 = dram("tab_feat1", (NP, D))
        tab_feat2 = dram("tab_feat2", (NP, D))
        tab_k = dram("tab_k", (NP, D))
        tab_v = dram("tab_v", (NP, D))
        row_names = ["dst", "block_dst", "src_low", "type"]
        sorted_d = dram("sorted_edges", (TILES * P, ROW), I32)
        rows_d = {k: dram("rows_" + k, (ITEMS, P), I16 if k == "dst" else BF16) for k in row_names}

        ident = sb("ident", [P, P])
        below = sb("below", [P, P])
        before_edge = sb("before_edge", [P, P])
        ones = sb("ones", [P, P])
        iota_free = sb("iota_free", [P, ITEMS])
        part_no = sb("part_no", [P, 1])
        minus_part_no = sb("minus_part_no", [P, 1])
        tile_no = sb("tile_no", [P, TCH])
        eps_col = sb("eps_col", [P, 1])
        src_i = sb("src_i", [P, ITEMS], I32)
        src_hi = sb("src_hi", [P, ITEMS])
        block_dst = sb("block_dst", [P, ITEMS])
        block_i = sb("block_i", [P, ITEMS], I32)
        el = sb("el", [P, BLOCKS * H1])
        er = sb("er", [P, BLOCKS, H1])
        deg = sb("deg", [P, BLOCKS])
        acc = sb("acc", [P, BLOCKS, AW])
        base = sb("base", [P, BLOCKS, D])
        el_parts = sb("el_parts", [P, 3, BLOCKS * H1], BF16)
        er_parts = sb("er_parts", [P, BLOCKS * 3 * H1], BF16)
        rel_parts = sb("rel_parts", [R, 3, R], BF16)
        query_parts = sb("query_parts", [P, 3, BLOCKS, D], BF16)
        scores = sb("scores", [P, ITEMS * H1])

        def by_item(heads):
            return scores[:, 0:ITEMS * heads].rearrange("p (h i) -> p i h", h=heads)

        rows = sb("rows", [P, SLOTS, GROUP, D])
        bias_split = rows[0:1, 0].rearrange("p g d -> p (g d)").bitcast(BF16)[:, 0:3 * 3 * D].rearrange(
            "p (k d) -> p k d", k=3)
        more_rows = query_parts[:].rearrange("p k b d -> p (k b d)").bitcast(F32)[:, 0:SLOTS * GROUP * D].rearrange(
            "p (s g d) -> p s g d", s=SLOTS, g=GROUP)
        row_slots = [rows[:, s] for s in range(SLOTS)] + [more_rows[:, s] for s in range(SLOTS)]
        index_slot = sb("index_slot", [P, 2 * SLOTS, GROUP], I32)
        w_a = sb("w_a", [P, 2, 3 * D])
        w_b = sb("w_b", [P, 2, D])
        w_el = sb("w_el", [P, 2, 2, H1])
        bias_row = sb("bias_row", [1, 3 * D])
        bias_parts = sb("bias_parts", [3, 3 * D], BF16)
        ones_parts = sb("ones_parts", [3, P], BF16)
        bias_all = sb("bias_all", [P, 2, D])
        rel_sb = sb("rel_sb", [R, R])
        bias1_col = sb("bias1_col", [P, 2])
        query_col = sb("query_col", [P, 2])
        chunk_row = w_a[0:1].rearrange("p k n -> p (k n)").rearrange("p (r c) -> p r c", r=12)
        chunk_col = sb("chunk_col", [P, 4])

        ARENA = 10900
        arena = sb("arena", [P, ARENA])

        def views(*sizes):
            got, at = [], 0
            for n in sizes:
                got.append(arena[:, at:at + n])
                at += n
            assert at <= ARENA
            return got

        ps = ctx.enter_context(nc.psum_tensor("ps", [P, 8, 512], F32))

        v = views(3 * TCH * P, 3 * TCH * P, TCH * ITEMS, TCH * ITEMS, ITEMS, 4 * ITEMS, 4 * TCH * P, 12 * TCH)
        tiles_i = v[0].bitcast(I32).rearrange("p (a c e) -> p a c e", a=3, c=TCH)
        tiles_f = v[1].rearrange("p (a c e) -> p a c e", a=3, c=TCH)
        sel = v[2].rearrange("p (c i) -> p c i", c=TCH)
        bsel = v[3].rearrange("p (c i) -> p c i", c=TCH)
        item_tmp = v[4]
        item_f = v[5].rearrange("p (a i) -> p a i", a=4)
        rows_t = [v[6][:, k * TCH * P // 2:(k + 1) * TCH * P // 2].bitcast(I16 if k == 0 else BF16).rearrange(
            "p (c e) -> p c e", c=TCH) for k in range(4)]
        tile_s = v[7].rearrange("p (k c) -> p k c", k=12)
        v = views(3 * TCH * P, TCH * P, TCH * P, 4 * TILES, 3 * TILES, PIECE * P, 4 * P, ROW * P, ROW, 4 + PIECE)
        next_i = v[1].bitcast(I32).rearrange("p (c e) -> p c e", c=TCH)
        falls = v[2].rearrange("p (c e) -> p c e", c=TCH)
        sort_cols = v[3].bitcast(I32).rearrange("p (k t) -> p k t", k=4)
        sort_dst, sort_level, sort_rank = (v[4][:, k * TILES:(k + 1) * TILES] for k in range(3))
        sort_less = v[5].rearrange("p (t e) -> p t e", e=P)
        sort_row_i = v[6][:, 0:2 * P].bitcast(I32).rearrange("p (s e) -> p s e", s=2)
        sort_row, sort_same = v[6][:, 2 * P:3 * P], v[6][:, 3 * P:4 * P]
        sort_back = v[7].bitcast(I32)
        sort_record = v[8].bitcast(I32)
        order_col = v[9][:, 0:4]
        sort_dst_sum = v[9][:, 4:4 + PIECE]
        v = views(2 * GROUP * P, 2 * GROUP * P, 2 * GROUP * 32, 2 * GROUP * AW)
        bcast = v[0].bitcast(BF16).rearrange("p (s a e) -> p s a e", s=2, a=2)
        onehot_t = v[1].bitcast(BF16).rearrange("p (s a e) -> p s a e", s=2, a=2)
        hi_onehot = v[2].rearrange("p (s g d) -> p s g d", s=2, g=GROUP)
        product = v[3].rearrange("p (s g d) -> p s g d", s=2, g=GROUP)
        v = views(2 * GROUP * P, 2 * GROUP * AW)
        onehot = v[0].rearrange("p (s g d) -> p s g d", s=2, g=GROUP)
        weighted = v[1].rearrange("p (s g d) -> p s g d", s=2, g=GROUP)
        SEG = ITEMS * H1
        v = views(SEG // 2, SEG, SEG // 2 + 8, SEG)
        seg = [v[0].bitcast(I16), v[1], v[2].bitcast(BF16), v[3]]
        v = views(UB * 2 * P, UB * D, UB * 2 * P, UB * 2 * D, UB * D, UB * D, UB * 40, 2 * D, BLOCKS * H1, BLOCKS)
        x_t = v[0].rearrange("p (j k n) -> p j k n", j=UB, k=2)
        x_n = v[1].rearrange("p (j d) -> p j d", j=UB)
        h_t = v[2].rearrange("p (j k n) -> p j k n", j=UB, k=2)
        stage = v[3].rearrange("p (j a d) -> p j a d", j=UB, a=2)
        h_n = v[4].rearrange("p (j d) -> p j d", j=UB)
        tmp_n = v[5].rearrange("p (j d) -> p j d", j=UB)
        small = v[6].rearrange("p (j k) -> p j k", j=UB)
        inv_sum = v[8].rearrange("p (b h) -> p b h", b=BLOCKS)
        inv_deg = v[9]
        attn = v[7].rearrange("p (a d) -> p a d", a=2)

        edges_in = sem("edges_loaded")
        consts = sem("constants_made")
        weights_in = [sem(f"weights_loaded{k}") for k in range(4)]
        order_dve, order_pe, order_known = (
            sem("falls_counted"), sem("falls_summed"), sem("order_known"))
        order_flag = sb("order_flag", [1, 1], I32)
        sort_cols_in = sem("sort_columns_loaded")
        sort_row_in = [sem(f"sort_row_loaded{k}") for k in range(2)]
        sort_row_used = [sem(f"sort_row_used{k}") for k in range(2)]
        sort_ranked, sort_scattered, sort_back_in, sort_back_used, sort_done = (
            sem("sort_ranks_made"), sem("sort_records_stored"), sem("sorted_records_loaded"),
            sem("sorted_records_used"), sem("edges_sorted"))
        sort_step = sem("sort_step")
        sort_copied, sort_ready = sem("sort_record_copied"), sem("sort_record_ready")
        edge_pe = sem("edge_products")
        edge_dve = sem("edge_vectors")
        rows_stored = sem("item_rows_stored")
        phase = {k: sem("stage_done_" + k) for k in ["pe", "act", "dve", "sp"]}
        dve_step, act_step, pool_step = sem("dve_step"), sem("act_step"), sem("pool_step")
        x_loaded = [sem(f"node_inputs_loaded{j}") for j in range(UB)]
        h_made = sem("node_rows_made")
        t_made = sem("node_transposes_made")
        ht_copied = sem("node_transposes_copied")
        bias_made, bias_in = sem("bias_parts_made"), sem("bias_parts_loaded")
        x_used = sem("node_inputs_used")
        out_made = sem("output_rows_made")
        node_mm = sem("node_products_made")
        node_dve = sem("node_products_read_dve")
        node_act = sem("node_products_read_act")
        node_stored = [sem(f"node_rows_stored{j}") for j in range(UB)]
        variance = [sem(f"variance_made{k}") for k in range(2)]
        deviated = [sem(f"deviation_made{k}") for k in range(2)]
        gathered = [sem(f"rows_gathered{s}") for s in range(2 * SLOTS)]
        slot_claimed = sem("rows_slot_claimed")
        acc_cleared = sem("sums_cleared")
        parts_made = sem("attention_term_parts_made")
        stats_made = sem("row_statistics_made")
        slot_used = [sem(f"rows_used{s}") for s in range(2 * SLOTS)]
        bcast_in = [sem(f"item_rows_broadcast{s}") for s in range(2)]
        onehot_made = [sem(f"onehot_made{s}") for s in range(2)]
        score_mm = [sem(f"score_products_made{s}") for s in range(2)]
        score_read = [sem(f"score_products_read{s}") for s in range(2)]
        pair_mm = sem("pair_products_made")
        pair_read = sem("pair_products_read")
        seg_in = sem("segment_rows_loaded")
        seg_t = sem("score_transposes_made")
        seg_copied = sem("score_transposes_copied")
        seg_small = sem("chunk_rows_made")
        seg_dve = sem("chunk_rows_used")
        seg_exp = sem("numerators_made")
        seg_back = sem("numerators_transposed")
        weighted_made = sem("weighted_rows_made")
        sum_mm = sem("sums_made")
        sum_added = sem("sums_added")
        block = ctx.enter_context(nc.Block())

        STAGES = ["items", "node1", "score1", "soft1", "sum1", "node2", "score2", "soft2", "sum2",
                  "node3", "score3", "soft3", "sum3", "final"]

        def begin(eng, name, others):
            k = STAGES.index(name)
            for o in others:
                if k:
                    eng.wait_ge(phase[o], k)

        def pipeline(fori, steps, chain=None, per_block=0):
            lags = max(lag for lag, _ in steps)
            assert lags <= UB

            def iteration(t, j, fixed):
                for lag, work in steps:
                    b = t * UB + j - lag if fixed else None
                    if fixed and not 0 <= b < BLOCKS:
                        continue
                    if fixed:
                        work(b // UB, b % UB)
                    else:
                        work(t + (j - lag) // UB, (j - lag) % UB)

            for j in range(UB):
                iteration(0, j, True)
            with fori(0, BTURNS - 1) as t:
                if chain:
                    chain.enter(t, UB * per_block)
                for j in range(UB):
                    iteration(t + 1, j, False)
                if chain:
                    chain.leave(BTURNS - 1)
            for j in range(lags):
                iteration(BTURNS, j, True)

        def early(t, j, k):
            return isinstance(t, int) and t * UB + j < k

        def nth_block(t, j, stage_no, off):
            return t * UB + (j + off + stage_no * BLOCKS)

        def product_bank(j):
            return (0, 1, 2, 0, 1)[j]

        def block_of(buf, t, j):
            return buf[:, bass.ds(t * UB + j, 1)]

        def uses(n, s):
            return sum((GROUPS - 1 - s) // ring + 1 for ring in RINGS[0:n] if s < ring)

        x_t_d = a["x_t"].rearrange("(k p) n -> p k n", k=2)

        def halves(w):
            return w.rearrange("(k p) n -> p k n", k=2)

        def nth(u, s):
            return u * (SLOTS // 2) + s // 2

        HALF = GROUPS // 2

        @block.sync
        def _(sp):
            def end():
                sp.sem_inc(phase["sp"], 1)

            sp.wait_ge(consts, 1)
            full, tail = E // P, E % P
            for k, name in enumerate(["src", "dst", "edge_type_64"]):
                v = a[name]
                w = v[0:(TCH - 1) * P * P].rearrange("(c p e) -> p c e", c=TCH - 1, e=P)
                sp.dma_start(tiles_i[:, k, 0:TCH - 1, :], w).then_inc(edges_in, 16)
                m = full - (TCH - 1) * P
                w = v[(TCH - 1) * P * P:full * P].rearrange("(p e) -> p e", e=P)
                sp.dma_start(tiles_i[0:m, k, TCH - 1, :], w).then_inc(edges_in, 16)
                w = v[full * P:E].rearrange("(p e) -> p e", p=1)
                sp.dma_start(tiles_i[m:m + 1, k, TCH - 1, 0:tail], w).then_inc(edges_in, 16)
            after = a["dst"][1:E]
            m = full - (TCH - 1) * P
            w = after[0:(TCH - 1) * P * P].rearrange("(c p e) -> p c e", c=TCH - 1, e=P)
            sp.dma_start(next_i[:, 0:TCH - 1, :], w).then_inc(edges_in, 16)
            w = after[(TCH - 1) * P * P:full * P].rearrange("(p e) -> p e", e=P)
            sp.dma_start(next_i[0:m, TCH - 1, :], w).then_inc(edges_in, 16)
            w = after[full * P:E - 1].rearrange("(p e) -> p e", p=1)
            sp.dma_start(next_i[m:m + 1, TCH - 1, 0:tail - 1], w).then_inc(edges_in, 16)
            sp.wait_ge(order_known, 1)
            unsorted = sp.value_load(order_flag[0:1, 0:1], min_val=0, max_val=1)
            with sp.If(unsorted != 0):
                sp.wait_ge(sort_done, 1)
                with nc.allow_non_contiguous_dma(reason="only for edges out of order"):
                    for k, name in enumerate(["src", "dst", "edge_type_64"]):
                        w = a[name][0:full * P].rearrange("(t e) -> e t", e=P)
                        sp.dma_start(sort_cols[:, k, 0:full], w).then_inc(sort_cols_in, 16)
                        w = a[name][full * P:E].rearrange("(e t) -> e t", t=1)
                        sp.dma_start(sort_cols[0:tail, k, full:full + 1], w).then_inc(sort_cols_in, 16)
                with nc.sync.Fori(0, full // 2) as t:
                    for k in range(2):
                        sp.wait_ge(sort_row_used[k], t + 1)
                        row = a["dst"][bass.ds(t * (2 * P) + k * P, P)]
                        sp.dma_start(sort_row_i[:, k], row.partition_broadcast(P)).then_inc(sort_row_in[k], 16)
                sp.wait_ge(sort_done, 2)
                row = a["dst"][full * P:E]
                sp.dma_start(sort_row_i[:, 0, 0:tail], row.partition_broadcast(P)).then_inc(sort_row_in[0], 16)
                sp.wait_ge(sort_done, 3)
                for c in range(TCH):
                    k = min(P, TILES - c * P)
                    sp.wait_ge(sort_back_used, c)
                    w = sorted_d[c * P * P:(c * P + k) * P, :].rearrange("(p e) k -> p (e k)", e=P)
                    sp.dma_start(sort_back[0:k, :], w).then_inc(sort_back_in, 16)
                sp.wait_ge(sort_back_used, TCH)
            sp.dma_start(w_a[:, :, 0:D], halves(a["fc1_t"])).then_inc(weights_in[0], 16)
            sp.dma_start(w_a[:, :, D:2 * D], halves(a["wb0_t"])).then_inc(weights_in[0], 16)
            sp.dma_start(bias_all[:, 1, :], a["bb0"].broadcast_to([P, D])).then_inc(weights_in[0], 16)
            sp.wait_ge(edge_dve, 4)
            for k, name in enumerate(row_names):
                w = rows_d[name][0:(ICH - 1) * P, :].rearrange("(c p) e -> p c e", p=P)
                sp.dma_start(w, rows_t[k][:, 0:ICH - 1, :]).then_inc(rows_stored, 16)
                sp.dma_start(rows_d[name][(ICH - 1) * P:ITEMS, :],
                             rows_t[k][0:LAST, ICH - 1, :]).then_inc(rows_stored, 16)
            sp.wait_ge(rows_stored, 2 * 4 * 16)
            end()

            def load_xt(stage_no):
                def go(t, j):
                    if not early(t, j, UB):
                        sp.wait_ge(node_mm, nth_block(t, j, stage_no, 1 - UB))
                    sp.dma_start(x_t[:, j], x_t_d[:, :, bass.ds((t * UB + j) * P, P)]).then_inc(x_loaded[j], 16)
                return go

            def load_x(t, j):
                if not early(t, j, UB):
                    sp.wait_ge(x_used, nth_block(t, j, 0, 1 - UB))
                sp.dma_start(x_n[:, j], a["x"][bass.ds((t * UB + j) * P, P), :]).then_inc(x_loaded[j], 16)

            def load_v(t, j):
                if not early(t, j, UB):
                    sp.wait_ge(x_used, nth_block(t, j, 1, 1 - UB))
                sp.dma_start(stage[:, j, 1], tab_v[bass.ds((t * UB + j) * P, P), :]).then_inc(x_loaded[j], 16)

            def store(stage_no, *tables):
                def go(t, j):
                    sp.wait_ge(node_act, nth_block(t, j, stage_no, 1))
                    for k, table in enumerate(tables):
                        sp.dma_start(table[bass.ds((t * UB + j) * P, P), :], stage[:, j, k]).then_inc(node_stored[j], 16)
                return go

            def stored(count):
                for j in range(UB):
                    sp.wait_ge(node_stored[j], 16 * count)

            begin(sp, "node1", ["dve", "pe", "act"])
            for k, name in enumerate(["attn_l1", "attn_r1"]):
                sp.dma_start(attn[:, k, :], a[name].broadcast_to([P, D])).then_inc(weights_in[0], 16)
            pipeline(nc.sync.Fori, [(0, load_xt(0)), (4, store(0, tab_feat1))])
            stored(BTURNS)
            end()

            def score_rows(layer, name, first):
                begin(sp, name, ["dve", "pe", "act"])
                flat = [rows_d[x].rearrange("i e -> (i e)") for x in (first, "block_dst")]
                with nc.sync.Fori(0, TURNS) as u:
                    for s in range(SLOTS):
                        sp.wait_ge(onehot_made[s % 2], nth(u, s) + (layer * HALF + 1))
                        for k in range(2):
                            row = flat[k][bass.ds(u * (STEP * P) + s * GROUP * P, GROUP * P)]
                            sp.dma_start(bcast[:, s % 2, k], row.partition_broadcast(P)).then_inc(bcast_in[s % 2], 16)
                end()

            def seg_rows(name, heads, chunks):
                begin(sp, name, ["dve", "pe", "act"])
                n = ITEMS // chunks * P
                row = rows_d["dst"].rearrange("(c j) e -> c (j e)", c=chunks)
                for h in range(heads):
                    sp.dma_start(seg[0][h * chunks:(h + 1) * chunks, 0:n], row).then_inc(seg_in, 16)
                end()

            score_rows(0, "score1", "src_low")
            seg_rows("soft1", H1, P // H1)
            begin(sp, "sum1", ["dve", "pe", "act"])
            sp.dma_start(w_a[:, :, 0:D], halves(a["fc2_t"])).then_inc(weights_in[1], 16)
            sp.dma_start(w_a[:, :, D:2 * D], halves(a["wb1_t"][D:2 * D, :])).then_inc(weights_in[1], 16)
            sp.dma_start(w_b[:], halves(a["wb1_t"][0:D, :])).then_inc(weights_in[1], 16)
            sp.dma_start(bias_all[:, 1, :], a["bb1"].broadcast_to([P, D])).then_inc(weights_in[1], 16)
            sp.dma_start(bias1_col[:], a["bias1"]).then_inc(weights_in[1], 16)
            for k, name in enumerate(["attn_l2", "attn_r2"]):
                sp.dma_start(attn[:, k, :], a[name].broadcast_to([P, D])).then_inc(weights_in[1], 16)
            end()

            begin(sp, "node2", ["dve", "pe", "act"])
            pipeline(nc.sync.Fori, [(0, load_xt(1)), (4, store(1, tab_feat2))])
            stored(2 * BTURNS)
            end()
            score_rows(1, "score2", "src_low")
            seg_rows("soft2", H2, ITEMS // 4)
            begin(sp, "sum2", ["dve", "pe", "act"])
            for k, name in enumerate(["wq", "wk", "wv"]):
                sp.dma_start(w_a[:, :, k * D:(k + 1) * D], halves(a[name])).then_inc(weights_in[2], 16)
            for k, name in enumerate(["bq", "bk", "bv"]):
                sp.dma_start(bias_row[:, k * D:(k + 1) * D], a[name]).then_inc(weights_in[2], 16)
            sp.dma_start(bias_all[:, 0, :], a["bias2"].broadcast_to([P, D])).then_inc(weights_in[2], 16)
            sp.dma_start(query_col[:], a["query"]).then_inc(weights_in[2], 16)
            sp.dma_start(rel_sb[:], a["rel"]).then_inc(weights_in[2], 16)
            end()

            begin(sp, "node3", ["dve", "pe", "act"])
            sp.wait_ge(bias_made, 1)
            for k in range(3):
                sp.dma_start(bias_parts[k:k + 1, :], bias_split[:, k]).then_inc(bias_in, 16)
            pipeline(nc.sync.Fori, [(0, load_x), (4, store(2, tab_k, tab_v))])
            stored(4 * BTURNS)
            end()
            score_rows(2, "score3", "type")
            seg_rows("soft3", H3, P // H3)
            begin(sp, "sum3", ["dve", "pe", "act"])
            sp.dma_start(w_b[:], halves(a["wo"])).then_inc(weights_in[3], 16)
            sp.dma_start(bias_row[:, 0:D], a["bo"]).then_inc(weights_in[3], 16)
            for k, name in enumerate(["gamma", "beta"]):
                sp.dma_start(bias_all[:, k, :], a[name].broadcast_to([P, D])).then_inc(weights_in[3], 16)
            end()

            begin(sp, "final", ["dve", "pe", "act"])
            sp.wait_ge(bias_made, 2)
            for k in range(3):
                sp.dma_start(bias_parts[k:k + 1, 0:D], bias_split[:, k, 0:D]).then_inc(bias_in, 16)

            def store_out(t, j):
                sp.wait_ge(out_made, nth_block(t, j, 0, 1))
                last = isinstance(t, int) and t * UB + j == BLOCKS - 1
                m = N - (BLOCKS - 1) * P if last else P
                sp.dma_start(out[bass.ds((t * UB + j) * P, m), :], stage[0:m, j, 0]).then_inc(node_stored[j], 16)

            pipeline(nc.sync.Fori, [(0, load_v), (5, store_out)])
            stored(5 * BTURNS)

        @block.gpsimd
        def _(pool):
            step = Count(pool_step)

            def did(ins):
                ins.then_inc(pool_step, 1)
                step.add()
                pool.wait_ge(pool_step, step.value())

            did(nc.gpsimd.memset(tiles_i[:, :, TCH - 1, :], 0))
            did(nc.gpsimd.memset(tiles_i[:, 1, TCH - 1, :], PAD_DST))
            did(nc.gpsimd.memset(next_i[:, TCH - 1, :], PAD_DST))
            pool.sem_inc(consts, 1)
            for credit in slot_used + onehot_made + score_read + sort_row_used:
                pool.sem_inc(credit, 1)
            nc.gpsimd.memset(ones[:], 1.0)
            nc.gpsimd.memset(eps_col[:], EPS)
            nc.gpsimd.memset(ones_parts[:], 1.0)
            did(nc.gpsimd.memset(ident[:], 0.0))
            nc.gpsimd.affine_select(out=ident[:], in_=ident[:], compare_op=ALU.not_equal, fill=1.0, base=0,
                                    pattern=[[1, P]], channel_multiplier=-1)
            nc.gpsimd.affine_select(out=below[:], in_=ones[:], compare_op=ALU.is_gt, fill=0.0, base=0,
                                    pattern=[[1, P]], channel_multiplier=-1)
            nc.gpsimd.affine_select(out=before_edge[:], in_=ones[:], compare_op=ALU.is_gt, fill=0.0, base=0,
                                    pattern=[[-1, P]], channel_multiplier=1)
            nc.gpsimd.iota(iota_free[:], [[1, ITEMS]], base=0, channel_multiplier=0,
                           allow_small_or_imprecise_dtypes=True)
            nc.gpsimd.iota(part_no[:], [[0, 1]], base=0, channel_multiplier=1,
                           allow_small_or_imprecise_dtypes=True)
            did(nc.gpsimd.iota(tile_no[:], [[P, TCH]], base=0, channel_multiplier=1,
                               allow_small_or_imprecise_dtypes=True))
            did(nc.gpsimd.tensor_scalar(minus_part_no[:], part_no[:], -1.0, None, ALU.mult))
            pool.sem_inc(consts, 1)

            pool.wait_ge(order_known, 1)
            unsorted = pool.value_load(order_flag[0:1, 0:1], min_val=0, max_val=1)
            with pool.If(unsorted != 0):
                pool.wait_ge(sort_ranked, 1)
                nc.gpsimd.memset(sort_record, 0).then_inc(sort_copied, 1)
                pool.wait_ge(sort_copied, 1)
                with nc.gpsimd.Fori(0, TILES) as t:
                    pool.wait_ge(sort_scattered, t * 16)
                    nc.gpsimd.tensor_copy(sort_record[:, 0:4], sort_cols[:, :, bass.ds(t, 1)]).then_inc(sort_copied, 1)
                    pool.wait_ge(sort_copied, t + 2)
                    pool.sem_inc(sort_ready, 1)
                    nc.gpsimd.indirect_dma_start(
                        sorted_d, bass.IndirectOffsetOnAxis(ap=sort_record[:, 3:4], axis=0), sort_record, None,
                    ).then_inc(sort_scattered, 16)
                pool.wait_ge(sort_scattered, TILES * 16)
                pool.sem_inc(sort_done, 1)

            def gathers(n, table, name):
                ring, turns, rest = RINGS[n], (GROUPS - 1) // RINGS[n], (GROUPS - 1) % RINGS[n] + 1
                pool.wait_ge(phase["sp"], STAGES.index(name) + 1)

                def indices(u, s):
                    for k in (s, s + 1):
                        pool.wait_ge(gathered[k], u * (16 * GROUP) + (uses(n, k) * 16 * GROUP))
                    nc.gpsimd.tensor_copy(
                        index_slot[:, s:s + 2].rearrange("p s g -> p (s g)"),
                        src_i[:, bass.ds(u * (ring * GROUP) + s * GROUP, 2 * GROUP)]).then_inc(pool_step, 1)

                def gather(u, s, ends):
                    if s % 2 == 0:
                        pool.wait_ge(pool_step, u * (ring // 2) + (s // 2 + 1 + step.n))
                    elif not ends:
                        indices(u + (s + 1) // ring, (s + 1) % ring)
                    pool.wait_ge(slot_used[s], u + (uses(n, s) + 1))
                    pool.sem_inc(slot_claimed, 1)
                    for g in range(GROUP):
                        nc.gpsimd.indirect_dma_start(
                            row_slots[s][:, g, :], None, table,
                            bass.IndirectOffsetOnAxis(ap=index_slot[:, s, g:g + 1], axis=0),
                        ).then_inc(gathered[s], 16)

                indices(0, 0)
                with nc.gpsimd.Fori(0, turns) as u:
                    for s in range(ring):
                        gather(u, s, False)
                for s in range(rest):
                    gather(turns, s, s + 1 == rest)
                step.add(GROUPS // 2)

            def clear_sums(name):
                if name:
                    pool.wait_ge(phase["dve"], STAGES.index(name) + 1)
                nc.gpsimd.memset(acc[:], 0.0).then_inc(acc_cleared, 1)

            clear_sums(None)
            gathers(0, tab_feat1, "node1")
            clear_sums("node2")
            gathers(1, tab_feat2, "node2")
            gathers(2, tab_k, "node3")
            gathers(3, tab_v, "node3")

        @block.tensor
        def _(pe):
            def end():
                pe.sem_inc(phase["pe"], 1)

            pe.wait_ge(consts, 2)
            pe.wait_ge(order_dve, 1)
            nc.tensor.matmul(ps[0:1, 7, 0:1], order_col[:, 0:1], ones[:, 0:1], start=True, stop=True).then_inc(order_pe, 1)
            pe.wait_ge(edge_dve, 1)
            nc.tensor.matmul(ps[:, 0, 0:TCH], below[:], tile_s[:, 4, :], start=True, stop=True)
            nc.tensor.matmul(ps[:, 1, 0:TCH], ones[:], tile_s[:, 4, :], start=True, stop=True).then_inc(edge_pe, 1)
            pe.wait_ge(edge_dve, 2)
            for k in range(5):
                for c in range(TCH):
                    lhs = tiles_f[:, k, c, :] if k < 3 else ones[:]
                    rhs = bsel[:, c, :] if k == 3 else sel[:, c, :]
                    last = nc.tensor.matmul(ps[:, k, 0:ITEMS], lhs, rhs, start=c == 0, stop=c == TCH - 1)
            last.then_inc(edge_pe, 1)
            pe.wait_ge(edge_dve, 3)
            for k in range(4):
                w = item_f[:, k, :] if k != 1 else block_dst[:]
                for c in range(ICH):
                    m = P if c < ICH - 1 else LAST
                    last = nc.tensor.transpose(ps[0:m, k, c * P:(c + 1) * P], w[:, c * P:c * P + m], ident[:])
            last.then_inc(edge_pe, 1)
            pe.wait_ge(edge_pe, 3)
            end()

            begin(pe, "node1", ["dve", "act"])
            pe.wait_ge(weights_in[0], 5 * 16)
            pe.wait_ge(edge_dve, 5)

            def products_free(t, j, stage_no):
                if not early(t, j, 2):
                    pe.wait_ge(node_dve, nth_block(t, j, stage_no, -1))

            def terms(lhs, j):
                for k in range(2):
                    last = nc.tensor.matmul(ps[:, 3 + j, 256:272], lhs[:, j, k, :],
                                            w_el[:, k].rearrange("p a h -> p (a h)"), start=k == 0, stop=k == 1)
                return last

            def node1_products(t, j):
                pe.wait_ge(x_loaded[j], (t + 1) * 16)
                products_free(t, j, 0)
                for k in range(2):
                    nc.tensor.matmul(ps[:, product_bank(j), :], x_t[:, j, k, :], w_a[:, k, 0:2 * D],
                                     start=k == 0, stop=k == 1)
                terms(x_t, j).then_inc(node_mm, 1)

            pipeline(nc.tensor.Fori, [(0, node1_products)])
            pe.wait_ge(node_mm, BLOCKS)
            end()

            regs = [pe.alloc_register(f"pe_block{g}") for g in range(GROUP)]

            def blocks(u, s):
                pe.load(regs, block_i[0:1, bass.ds(u * STEP + s * GROUP, GROUP)])
                return [pe.snap(r, min_val=0, max_val=BLOCKS - 1) for r in regs]

            def gat_scores(layer, name, heads):
                begin(pe, name, ["dve", "act", "sp"])
                w = BLOCKS * heads
                er_blocks = er_parts[:, 0:3 * w].rearrange("p (b x) -> p b x", b=BLOCKS)
                pe.wait_ge(parts_made, layer + 1)
                with nc.tensor.Fori(0, TURNS) as u:
                    for s in range(SLOTS):
                        bs = blocks(u, s)
                        pe.wait_ge(onehot_made[s % 2], nth(u, s) + (layer * HALF + 2))
                        pe.wait_ge(score_read[s % 2], nth(u, s) + (layer * HALF + 1))
                        for g in range(GROUP):
                            bank, at = s % 2 * 4 + g // 2, g % 2 * D
                            e = slice(g * P, (g + 1) * P)
                            for k in range(3):
                                nc.tensor.matmul(ps[:, bank, at:at + w], onehot_t[:, s % 2, 0, e],
                                                 el_parts[:, k, 0:w], start=k == 0, stop=k == 2)
                            last = nc.tensor.matmul(ps[:, bank, at + w:at + w + 3 * heads], onehot_t[:, s % 2, 1, e],
                                                    er_blocks[:, bass.ds(bs[g], 1), :].rearrange("p a x -> p (a x)"),
                                                    start=True, stop=True)
                        last.then_inc(score_mm[s % 2], 1)
                for s in range(2):
                    pe.wait_ge(score_mm[s], (layer + 1) * HALF)
                end()

            def pair_scores(layer, name):
                begin(pe, name, ["dve", "act", "sp"])
                with nc.tensor.Fori(0, TURNS) as u:
                    for s in range(SLOTS):
                        bs = blocks(u, s)
                        pe.wait_ge(onehot_made[s % 2], nth(u, s) + (layer * HALF + 2))
                        for g in range(GROUP):
                            pe.wait_ge(pair_read, u * STEP + (s * GROUP + g + 1))
                            e = slice(g * P, (g + 1) * P)
                            for k in range(3):
                                part = query_parts[:, k, bass.ds(bs[g], 1), :].rearrange("p a d -> p (a d)")
                                nc.tensor.matmul(ps[:, g, 0:D], onehot_t[:, s % 2, 1, e], part,
                                                 start=k == 0, stop=k == 2)
                            for k in range(3):
                                last = nc.tensor.matmul(ps[:, g, D:D + R], onehot_t[0:R, s % 2, 0, e],
                                                        rel_parts[:, k, :], start=k == 0, stop=k == 2)
                            last.then_inc(pair_mm, 1)
                pe.wait_ge(pair_mm, ITEMS)
                end()

            def soft(n, name, heads, chunks):
                begin(pe, name, ["dve", "act"])
                each = ITEMS // chunks
                m = heads * chunks
                for j in range(each):
                    last = nc.tensor.transpose(ps[0:m, j // 4, j % 4 * P:(j % 4 + 1) * P],
                                               scores[:, j:ITEMS * heads:each], ident[:])
                last.then_inc(seg_t, 1)
                pe.wait_ge(seg_dve, 3 * n + 1)
                for k in range(4):
                    last = nc.tensor.matmul(ps[0:1, 0, k * P:k * P + m], chunk_col[0:m, k:k + 1], ident[0:m, 0:m],
                                            start=True, stop=True)
                last.then_inc(seg_small, 1)
                pe.wait_ge(seg_dve, 3 * n + 2)
                for k in range(2):
                    last = nc.tensor.matmul(ps[0:m, 1, k:k + 1], chunk_row[:, 8 + k, 0:m], ones[0:1, 0:1],
                                            start=True, stop=True)
                last.then_inc(seg_small, 1)
                pe.wait_ge(seg_exp, n + 1)
                for j in range(each):
                    last = nc.tensor.transpose(ps[:, j // 4, j % 4 * m:(j % 4 + 1) * m],
                                               seg[1][0:m, j * P:(j + 1) * P], ident[0:m, 0:m])
                last.then_inc(seg_back, 1)
                pe.wait_ge(seg_back, n + 1)
                end()

            def sums(n, name, heads, width):
                begin(pe, name, ["dve", "act"])
                with nc.tensor.Fori(0, TURNS) as u:
                    for s in range(SLOTS):
                        pe.wait_ge(weighted_made, u * SLOTS + (s + 1 + n * GROUPS))
                        for g in range(GROUP):
                            pe.wait_ge(sum_added, u * STEP + (s * GROUP + g + 1 + n * (ITEMS + GROUP)))
                            nc.tensor.matmul(ps[:, g, 0:width], onehot[:, s % 2, g, :], weighted[:, s % 2, g, 0:width],
                                             start=True, stop=True).then_inc(sum_mm, 1)
                pe.wait_ge(sum_mm, (n + 1) * ITEMS)
                end()

            def transposes(before):
                def go(t, j):
                    pe.wait_ge(h_made, nth_block(t, j, before, 1))
                    for k in range(2):
                        last = nc.tensor.transpose(ps[:, 3 + j, k * P:(k + 1) * P], h_n[:, j, k * P:(k + 1) * P], ident[:])
                    last.then_inc(t_made, 1)
                return go

            gat_scores(0, "score1", H1)
            soft(0, "soft1", H1, P // H1)
            sums(0, "sum1", H1, AW)

            begin(pe, "node2", ["dve", "act"])
            pe.wait_ge(weights_in[1], 7 * 16)
            pe.wait_ge(edge_dve, 6)

            def node2_products(t, j):
                bank = product_bank(j)
                pe.wait_ge(ht_copied, nth_block(t, j, 0, 1))
                pe.wait_ge(x_loaded[j], (t + (BTURNS + 1)) * 16)
                products_free(t, j, 1)
                for k in range(2):
                    nc.tensor.matmul(ps[:, bank, :], h_t[:, j, k, :], w_a[:, k, 0:2 * D], start=k == 0, stop=False)
                for k in range(2):
                    nc.tensor.matmul(ps[:, bank, D:2 * D], x_t[:, j, k, :], w_b[:, k, :], start=False, stop=k == 1)
                terms(h_t, j).then_inc(node_mm, 1)

            pipeline(nc.tensor.Fori, [(0, transposes(0)), (1, node2_products)])
            pe.wait_ge(node_mm, 2 * BLOCKS)
            end()

            gat_scores(1, "score2", H2)
            soft(1, "soft2", H2, ITEMS // 4)
            sums(1, "sum2", H2, D + H2)

            begin(pe, "node3", ["dve", "act"])
            pe.wait_ge(weights_in[2], 9 * 16)
            pe.wait_ge(bias_in, 3 * 16)

            def node3_products(t, j):
                pe.wait_ge(ht_copied, nth_block(t, j, 1, 1))
                products_free(t, j, 2)
                for at, w0, w1 in ((ps[:, product_bank(j), :], 0, 2 * D), (ps[:, 3 + j, D:2 * D], 2 * D, 3 * D)):
                    for k in range(2):
                        nc.tensor.matmul(at, h_t[:, j, k, :], w_a[:, k, w0:w1], start=k == 0, stop=False)
                    last = nc.tensor.matmul(at, ones_parts[:], bias_parts[:, w0:w1], start=False, stop=True)
                last.then_inc(node_mm, 1)

            pipeline(nc.tensor.Fori, [(0, transposes(1)), (1, node3_products)])
            pe.wait_ge(node_mm, 3 * BLOCKS)
            end()

            pair_scores(2, "score3")
            soft(2, "soft3", H3, P // H3)
            sums(2, "sum3", H3, D + H3)

            begin(pe, "final", ["dve", "act"])
            pe.wait_ge(weights_in[3], 4 * 16)
            pe.wait_ge(bias_in, 6 * 16)

            def final_products(t, j):
                at = ps[:, product_bank(j), 0:D]
                pe.wait_ge(ht_copied, nth_block(t, j, 2, 1))
                products_free(t, j, 3)
                for k in range(2):
                    nc.tensor.matmul(at, h_t[:, j, k, :], w_b[:, k, :], start=k == 0, stop=False)
                nc.tensor.matmul(at, ones_parts[:], bias_parts[:, 0:D], start=False, stop=True).then_inc(node_mm, 1)

            pipeline(nc.tensor.Fori, [(0, transposes(2)), (1, final_products)])

        @block.scalar
        def _(act):
            step = Count(act_step)

            def did(ins):
                ins.then_inc(act_step, 1)
                step.add()
                act.wait_ge(act_step, step.value())

            def end():
                act.sem_inc(phase["act"], 1)

            def idle(name):
                begin(act, name, ["act"])
                end()

            idle("items")

            def copy_transposes(before, bias=None, func=ACT.Identity, keep=False):
                def go(t, j):
                    act.wait_ge(t_made, nth_block(t, j, before, 1))
                    if keep:
                        nc.scalar.copy(block_of(base, t, j), h_n[:, j:j + 1])
                    if not early(t, j, UB):
                        act.wait_ge(node_mm, nth_block(t, j, before + 1, 1 - UB))
                    if bias is None:
                        last = nc.scalar.copy(h_t[:, j], ps[:, 3 + j, 0:D].rearrange("p (k n) -> p k n", k=2))
                    else:
                        for k in range(2):
                            last = nc.scalar.activation(h_t[:, j, k], ps[:, 3 + j, k * P:(k + 1) * P], func,
                                                        bias=bias[:, k:k + 1])
                    last.then_inc(ht_copied, 1)
                return go

            def gat_copies(stage_no, heads):
                def go(t, j):
                    act.wait_ge(node_mm, nth_block(t, j, stage_no, 1))
                    act.wait_ge(node_stored[j], t * 16 + 16 * stage_no * BTURNS)
                    nc.scalar.copy(stage[:, j, 0, :], ps[:, product_bank(j), 0:D])
                    got = ps[:, 3 + j, 256:272].rearrange("p (a h) -> p a h", a=2)
                    el_v = el[:, 0:BLOCKS * heads].rearrange("p (b h) -> p b h", h=heads)
                    nc.scalar.copy(block_of(el_v, t, j), got[:, 0:1, 0:heads])
                    nc.scalar.copy(block_of(er, t, j)[:, :, 0:heads], got[:, 1:2, 0:heads]).then_inc(node_act, 1)
                return go

            def soft(n, name, heads, chunks):
                begin(act, name, ["dve", "pe"])
                each, m = ITEMS // chunks, heads * chunks
                act.wait_ge(seg_t, n + 1)
                for bank in range(-(-each // 4)):
                    k = min(4, each - 4 * bank) * P
                    last = nc.scalar.copy(seg[1][0:m, 4 * bank * P:4 * bank * P + k], ps[0:m, bank, 0:k])
                last.then_inc(seg_copied, 1)
                act.wait_ge(seg_dve, 3 * n + 3)
                nc.scalar.activation(seg[1][0:m, 0:each * P], seg[1][0:m, 0:each * P], ACT.Exp).then_inc(seg_exp, 1)
                act.wait_ge(seg_back, n + 1)
                view = scores[:, 0:ITEMS * heads].rearrange("p (m j) -> p j m", j=each)
                for bank in range(-(-each // 4)):
                    k = min(4, each - 4 * bank)
                    last = nc.scalar.copy(view[:, 4 * bank:4 * bank + k],
                                          ps[:, bank, 0:k * m].rearrange("p (j m) -> p j m", j=k))
                did(last)
                end()

            def deviation(before, at):
                def go(t, j):
                    act.wait_ge(variance[at], nth_block(t, j, before, 1))
                    nc.scalar.activation(small[:, j, 16 * at + 8:16 * at + 9], small[:, j, 16 * at + 7:16 * at + 8],
                                         ACT.Sqrt, bias=eps_col[:]).then_inc(deviated[at], 1)
                return go

            begin(act, "node1", ["dve", "pe"])
            pipeline(nc.scalar.Fori, [(0, gat_copies(0, H1))])
            act.wait_ge(node_act, BLOCKS)
            end()

            begin(act, "score1", ["dve", "pe"])

            def onehots(u, s, first=False):
                z = s % 2
                act.wait_ge(bcast_in[z], nth(u, s) * 32 + 32)
                if not first:
                    act.wait_ge(score_mm[z], nth(u, s))
                did(nc.scalar.activation(onehot_t[:, z], bcast[:, z], ACT.Square, bias=minus_part_no[:]))
                nc.scalar.activation(onehot_t[:, z], onehot_t[:, z], ACT.Relu, scale=-1.0,
                                     bias=ones[:, 0:1]).then_inc(onehot_made[z], 1)

            for s in range(SLOTS):
                onehots(0, s, first=s < 2)
            with nc.scalar.Fori(0, TURNS - 1) as u:
                step.enter(u, SLOTS)
                for s in range(SLOTS):
                    onehots(u + 1, s)
                step.leave(TURNS - 1)
            act.wait_ge(onehot_made[1], HALF + 1)
            end()
            soft(0, "soft1", H1, P // H1)
            idle("sum1")

            begin(act, "node2", ["dve", "pe"])
            act.wait_ge(weights_in[1], 7 * 16)
            pipeline(nc.scalar.Fori, [(0, copy_transposes(0, bias1_col, ACT.Relu)), (1, gat_copies(1, H2))])
            act.wait_ge(node_act, 2 * BLOCKS)
            end()
            idle("score2")
            soft(1, "soft2", H2, ITEMS // 4)
            idle("sum2")

            begin(act, "node3", ["dve", "pe"])
            act.wait_ge(weights_in[2], 9 * 16)
            did(nc.scalar.mul(query_col[:], query_col[:], 0.1))
            did(nc.scalar.mul(rel_sb[:], rel_sb[:], 0.2))

            def kv_copies(t, j):
                act.wait_ge(node_mm, nth_block(t, j, 2, 1))
                act.wait_ge(node_stored[j], t * 32 + 16 * 2 * BTURNS)
                nc.scalar.copy(stage[:, j, 0, :], ps[:, product_bank(j), D:2 * D])
                nc.scalar.copy(stage[:, j, 1, :], ps[:, 3 + j, D:2 * D]).then_inc(node_act, 1)

            pipeline(nc.scalar.Fori, [(0, deviation(0, 0)), (1, copy_transposes(1, query_col, keep=True)),
                                      (2, kv_copies)])
            act.wait_ge(node_act, 3 * BLOCKS)
            end()
            idle("score3")
            soft(2, "soft3", H3, P // H3)
            idle("sum3")

            begin(act, "final", ["dve", "pe"])
            pipeline(nc.scalar.Fori, [(0, copy_transposes(2)), (2, deviation(1, 0)), (3, deviation(0, 1))])

        @block.vector
        def _(dve):
            step = Count(dve_step)
            vec = nc.vector

            def did(ins):
                ins.then_inc(dve_step, 1)
                step.add()
                dve.wait_ge(dve_step, step.value())

            def then(ins):
                ins.then_inc(dve_step, 1)
                step.add()

            def all_but(k):
                dve.wait_ge(dve_step, step.value() - k)

            def end():
                dve.sem_inc(phase["dve"], 1)

            def signal(sem):
                dve.sem_inc(sem, 1)

            def sort_edges():
                inner = Count(sort_step)

                def then(ins):
                    ins.then_inc(sort_step, 1)
                    inner.add()
                    dve.wait_ge(sort_step, inner.value())

                then(vec.memset(sort_cols[:, 0, TILES - 1:TILES], 0))
                then(vec.memset(sort_cols[:, 1, TILES - 1:TILES], PAD_DST))
                then(vec.memset(sort_cols[:, 2, TILES - 1:TILES], 0))
                then(vec.memset(sort_rank, 0.0))
                signal(sort_done)
                dve.wait_ge(sort_cols_in, 6 * 16)
                then(vec.tensor_copy(sort_dst, sort_cols[:, 1, :]))
                then(vec.tensor_scalar(sort_level, sort_dst, 0.5, None, ALU.add))

                def rank_tile(t, k):
                    then(vec.tensor_copy(sort_row, sort_row_i[:, k]))
                    signal(sort_row_used[k])
                    level = sort_level[:, bass.ds(t, 1)]
                    then(vec.tensor_scalar(level, level, -0.5, None, ALU.add))
                    then(vec.tensor_tensor(sort_same, sort_row, sort_dst[:, bass.ds(t, 1)].broadcast_to([P, P]),
                                           ALU.is_equal))
                    then(vec.tensor_tensor(sort_same, sort_same, before_edge[:], ALU.mult))
                    then(vec.tensor_reduce(order_col[:, 1:2], sort_same, AX.X, ALU.add))
                    own = sort_rank[:, bass.ds(t, 1)]
                    then(vec.tensor_tensor(own, own, order_col[:, 1:2], ALU.add))
                    for p in range(0, TILES, PIECE):
                        then(vec.tensor_tensor(
                            sort_less, sort_row.unsqueeze(1).broadcast_to([P, PIECE, P]),
                            sort_level[:, p:p + PIECE].unsqueeze(2).broadcast_to([P, PIECE, P]), ALU.is_lt))
                        then(vec.tensor_reduce(sort_dst_sum, sort_less, AX.X, ALU.add))
                        then(vec.tensor_tensor(sort_rank[:, p:p + PIECE], sort_rank[:, p:p + PIECE],
                                               sort_dst_sum, ALU.add))

                each = 6 + 3 * (TILES // PIECE)
                with vec.Fori(0, TILES // 2) as t:
                    inner.enter(t, 2 * each)
                    for k in range(2):
                        dve.wait_ge(sort_row_in[k], (t + 1) * 16)
                        rank_tile(t * 2 + k, k)
                    inner.leave(TILES // 2)
                then(vec.memset(sort_row_i[:, 0], PAD_DST))
                signal(sort_done)
                dve.wait_ge(sort_row_in[0], (TILES // 2 + 1) * 16)
                rank_tile(TILES - 1, 0)
                then(vec.tensor_copy(sort_cols[:, 3, :], sort_rank))
                signal(sort_ranked)
                for c in range(TCH):
                    k = min(P, TILES - c * P)
                    dve.wait_ge(sort_back_in, (c + 1) * 16)
                    then(vec.tensor_copy(tiles_i[0:k, :, c, :], sort_back[0:k].rearrange("p (e k) -> p k e", k=ROW)[:, 0:3, :]))
                    signal(sort_back_used)

            dve.wait_ge(consts, 2)
            dve.wait_ge(edges_in, 12 * 16)
            did(vec.tensor_tensor(falls, next_i, tiles_i[:, 1], ALU.is_lt))
            did(vec.tensor_reduce(order_col[:, 0:1], falls, AX.XY, ALU.add))
            signal(order_dve)
            dve.wait_ge(order_pe, 1)
            did(vec.tensor_scalar(order_flag[:], ps[0:1, 7, 0:1], 1.0, None, ALU.min))
            signal(order_known)
            unsorted = dve.value_load(order_flag[0:1, 0:1], min_val=0, max_val=1)
            with dve.If(unsorted != 0):
                sort_edges()
            did(vec.tensor_copy(tiles_f, tiles_i))
            tile_si = tile_s.bitcast(I32)
            lo, hi, many, start, stop, shift, total = (tile_s[:, k, :] for k in range(2, 9))
            did(vec.tensor_scalar(tile_si[:, 0, :], tiles_i[:, 1, :, 0], 7, None, ALU.arith_shift_right))
            did(vec.tensor_scalar(tile_si[:, 1, :], tiles_i[:, 1, :, P - 1], 7, None, ALU.arith_shift_right))
            did(vec.tensor_copy(tile_s[:, 2:4, :], tile_si[:, 0:2, :]))
            did(vec.tensor_tensor(many, hi, lo, ALU.subtract))
            did(vec.tensor_scalar(many, many, 1.0, None, ALU.add))
            did(vec.scalar_tensor_tensor(many, tile_no[:], float(TILES), many, ALU.is_lt, ALU.mult))
            signal(edge_dve)
            dve.wait_ge(edge_pe, 1)
            did(vec.memset(total[:, 0:1], 0.0))
            for c in range(1, TCH):
                did(vec.tensor_tensor(total[:, c:c + 1], total[:, c - 1:c], ps[:, 1, c - 1:c], ALU.add))
            did(vec.tensor_tensor(start, total, ps[:, 0, 0:TCH], ALU.add))
            did(vec.tensor_tensor(stop, start, many, ALU.add))
            did(vec.tensor_tensor(shift, lo, start, ALU.subtract))
            for c in range(TCH):
                did(vec.tensor_scalar(item_tmp, iota_free[:], start[:, c:c + 1], None, ALU.is_ge))
                did(vec.scalar_tensor_tensor(sel[:, c, :], iota_free[:], stop[:, c:c + 1], item_tmp,
                                             ALU.is_lt, ALU.mult))
                did(vec.scalar_tensor_tensor(bsel[:, c, :], iota_free[:], shift[:, c:c + 1], sel[:, c, :],
                                             ALU.add, ALU.mult))
            signal(edge_dve)
            dve.wait_ge(edge_pe, 2)
            tmp_i = item_tmp.bitcast(I32)
            did(vec.tensor_copy(src_i[:], ps[:, 0, 0:ITEMS]))
            did(vec.tensor_copy(item_f[:, 0, :], ps[:, 1, 0:ITEMS]))
            did(vec.tensor_copy(item_f[:, 3, :], ps[:, 2, 0:ITEMS]))
            did(vec.tensor_copy(block_i[:], ps[:, 3, 0:ITEMS]))
            did(vec.scalar_tensor_tensor(block_dst[:], ps[:, 3, 0:ITEMS], -float(P), item_f[:, 0, :],
                                         ALU.mult, ALU.add))
            did(vec.tensor_tensor(block_dst[:], block_dst[:], ps[:, 4, 0:ITEMS], ALU.add))
            did(vec.tensor_scalar(block_dst[:], block_dst[:], -1.0, None, ALU.add))
            did(vec.tensor_scalar(tmp_i, src_i[:], 7, None, ALU.arith_shift_right))
            did(vec.tensor_copy(src_hi[:], tmp_i))
            did(vec.tensor_scalar(tmp_i, src_i[:], P - 1, None, ALU.bitwise_and))
            did(vec.tensor_copy(item_f[:, 2, :], tmp_i))
            signal(edge_dve)
            dve.wait_ge(edge_pe, 3)
            for k in range(4):
                did(vec.tensor_copy(rows_t[k][:, 0:ICH - 1, :],
                                    ps[:, k, 0:(ICH - 1) * P].rearrange("p (c e) -> p c e", e=P)))
                did(vec.tensor_copy(rows_t[k][0:LAST, ICH - 1, :], ps[0:LAST, k, (ICH - 1) * P:ICH * P]))
            signal(edge_dve)
            end()

            def attention_columns(k, count, heads):
                dve.wait_ge(weights_in[k], 16 * count)
                for side in range(2):
                    did(vec.tensor_tensor(tmp_n[:, 0:2, :], w_a[:, :, 0:D],
                                          attn[:, side:side + 1, :].broadcast_to([P, 2, D]), ALU.mult))
                    did(vec.tensor_reduce(w_el[:, :, side, 0:heads],
                                          tmp_n[:, 0:2, :].rearrange("p k (h d) -> p k h d", h=heads), AX.X, ALU.add))
                signal(edge_dve)

            begin(dve, "node1", ["pe", "act", "sp"])
            attention_columns(0, 5, H1)

            def residual(stage_no):
                def go(t, j):
                    dve.wait_ge(node_act, nth_block(t, j, stage_no, 1))
                    vec.tensor_tensor(block_of(base, t, j), ps[:, product_bank(j), D:2 * D].unsqueeze(1),
                                      bias_all[:, 1:2, :], ALU.add).then_inc(node_dve, 1)
                return go

            pipeline(vec.Fori, [(0, residual(0))])
            dve.wait_ge(node_dve, BLOCKS)
            end()

            def split(parts, value, rest, factor=1.0):
                did(vec.tensor_scalar(rest, value, factor, None, ALU.mult))
                for k in range(3):
                    did(vec.tensor_scalar(parts[k], rest, 1.0, None, ALU.mult))
                    if k < 2:
                        did(vec.tensor_tensor(rest, rest, parts[k], ALU.subtract))

            def onehots(layer, u, s):
                z = s % 2
                dve.wait_ge(bcast_in[z], nth(u, s) * 32 + 32 * (layer * HALF + 1))
                vec.tensor_scalar(onehot_t[:, z], bcast[:, z], part_no[:], None,
                                  ALU.is_equal).then_inc(onehot_made[z], 1)

            def gat_scores(layer, name, heads, own_onehots):
                begin(dve, name, ["pe", "act"])
                w = BLOCKS * heads
                split([el_parts[:, k, 0:w] for k in range(3)], el[:, 0:w], el[:, 0:w])
                er_v = er[:, :, 0:heads]
                er_blocks = er_parts[:, 0:3 * w].rearrange("p (b k h) -> p b k h", b=BLOCKS, k=3)
                split([er_blocks[:, :, k, :] for k in range(3)], er_v, er_v)
                signal(parts_made)
                if own_onehots:
                    onehots(layer, 0, 0)
                    onehots(layer, 0, 1)
                else:
                    dve.wait_ge(bcast_in[0], 32)
                did(vec.memset(hi_onehot[:, :, :, BLOCKS:PICKS], 1.0))

                def hot(u, s):
                    then(vec.tensor_tensor(
                        hi_onehot[:, s % 2, :, 0:BLOCKS],
                        iota_free[:, 0:BLOCKS].unsqueeze(1).broadcast_to([P, GROUP, BLOCKS]),
                        src_hi[:, bass.ds(u * STEP + s * GROUP, GROUP)].unsqueeze(2).broadcast_to([P, GROUP, BLOCKS]),
                        ALU.is_equal))

                def turn(u, ends):
                    for s in range(SLOTS):
                        z = s % 2
                        dve.wait_ge(score_mm[z], nth(u, s) + (layer * HALF + 1))
                        all_but(0)
                        got = ps[:, z * 4:z * 4 + 4, :].rearrange("p q (i x) -> p (q i) x", i=2)[:, :, 0:PICKS * heads]
                        picked = product[:, z, :, 0:PICKS * heads].rearrange("p i (h b) -> p i h b", h=heads)
                        then(vec.tensor_tensor(picked, got.rearrange("p i (b h) -> p i h b", h=heads),
                                               hi_onehot[:, z, :, 0:PICKS].unsqueeze(2).broadcast_to(
                                                   [P, GROUP, heads, PICKS]), ALU.mult))
                        if ends and s == SLOTS - 1:
                            all_but(0)
                        else:
                            hot(u + (s + 1) // SLOTS, (s + 1) % SLOTS)
                            all_but(1)
                        signal(score_read[z])
                        vec.tensor_reduce(by_item(heads)[:, bass.ds(u * STEP + s * GROUP, GROUP), :], picked,
                                          AX.X, ALU.add)
                        if own_onehots and not (ends and s + 2 >= SLOTS):
                            onehots(layer, u + (s + 2) // SLOTS, (s + 2) % SLOTS)

                hot(0, 0)
                all_but(0)
                with vec.Fori(0, TURNS - 1) as u:
                    step.enter(u, SLOTS * 2)
                    turn(u, False)
                    step.leave(TURNS - 1)
                turn(TURNS - 1, True)
                did(vec.memset(chunk_col[:, 0:1], 0.0))
                e = scores[:, 0:ITEMS * heads]
                did(vec.scalar_tensor_tensor(e, e, 0.2, e, ALU.mult, ALU.max))
                end()

            def pair_scores(layer, name):
                begin(dve, name, ["pe", "act"])
                split([rel_parts[:, k] for k in range(3)], rel_sb[:], rel_sb[:])
                did(vec.memset(acc[:], 0.0))
                dve.sem_inc(pair_read, GROUP)
                onehots(layer, 0, 0)
                onehots(layer, 0, 1)

                def turn(u, ends):
                    for s in range(SLOTS):
                        z = s % 2
                        dve.wait_ge(gathered[s], u * (16 * GROUP) + ((uses(2, s) + 1) * 16 * GROUP))
                        for g in range(GROUP + 1):
                            if g < GROUP:
                                dve.wait_ge(pair_mm, u * STEP + (s * GROUP + g + 1))
                                key = product[:, z, g, 0:D].rearrange("p (h d) -> p h d", h=H3)
                                then(vec.tensor_tensor(key, rows[:, s, g, :].rearrange("p (h d) -> p h d", h=H3),
                                                       ps[:, g, D:D + R].unsqueeze(1).broadcast_to([P, H3, R]), ALU.add))
                            if g:
                                all_but(1 if g < GROUP else 0)
                                vec.tensor_tensor(product[:, z, g - 1, 0:D], product[:, z, g - 1, 0:D],
                                                  ps[:, g - 1, 0:D], ALU.mult).then_inc(pair_read, 1)
                        signal(slot_used[s])
                        if not (ends and s + 2 >= SLOTS):
                            onehots(layer, u + (s + 2) // SLOTS, (s + 2) % SLOTS)
                        dve.wait_ge(pair_read, u * STEP + (s + 2) * GROUP)
                        vec.tensor_reduce(by_item(H3)[:, bass.ds(u * STEP + s * GROUP, GROUP), :],
                                          product[:, z, :, 0:D].rearrange("p i (h d) -> p i h d", h=H3),
                                          AX.X, ALU.add)

                with vec.Fori(0, TURNS - 1) as u:
                    step.enter(u, SLOTS * GROUP)
                    turn(u, False)
                    step.leave(TURNS - 1)
                turn(TURNS - 1, True)
                did(vec.memset(chunk_col[:, 0:1], 0.0))
                end()

            def soft(n, name, heads, chunks, rows_before):
                begin(dve, name, ["pe", "act"])
                each, m = ITEMS // chunks, heads * chunks
                L = each * P
                dst, score, gap, top = (b[0:m] for b in seg)
                dve.wait_ge(seg_in, 16 * (rows_before + heads))
                did(vec.memset(gap[:, 0:1], -BIG))
                did(vec.memset(gap[:, L:L + 1], -BIG))
                did(vec.tensor_tensor(gap[:, 1:L], dst[:, 1:L], dst[:, 0:L - 1], ALU.not_equal))
                did(vec.tensor_scalar(gap[:, 1:L], gap[:, 1:L], -BIG, None, ALU.mult))
                dve.wait_ge(seg_copied, n + 1)
                did(vec.tensor_tensor_scan(top[:, 0:L], gap[:, 0:L], score[:, 0:L], -BIG, ALU.add, ALU.max))
                did(vec.tensor_tensor_scan(top[:, 0:L][:, ::-1], gap[:, 1:L + 1][:, ::-1], top[:, 0:L][:, ::-1],
                                           -BIG, ALU.add, ALU.max))
                for k, end_v in enumerate([top[:, 0:1], top[:, L - 1:L], dst[:, 0:1], dst[:, L - 1:L]]):
                    did(vec.tensor_copy(chunk_col[0:m, k:k + 1], end_v))
                signal(seg_dve)
                dve.wait_ge(seg_small, 2 * n + 1)
                did(vec.tensor_copy(chunk_row[:, 0:4, 0:m], ps[0:1, 0, :].rearrange("p (k c) -> p k c", k=4)[:, :, 0:m]))
                head_top, tail_top, head_dst, tail_dst, whole, joint, a0, b0, before, after, a1, b1 = (
                    chunk_row[:, k, 0:m] for k in range(12))
                did(vec.tensor_tensor(whole, head_dst, tail_dst, ALU.not_equal))
                did(vec.tensor_scalar(whole, whole, -BIG, None, ALU.mult))
                did(vec.tensor_tensor(joint[:, 1:m], head_dst[:, 1:m], tail_dst[:, 0:m - 1], ALU.not_equal))
                did(vec.tensor_scalar(joint[:, 1:m], joint[:, 1:m], -BIG, None, ALU.mult))
                did(vec.memset(joint.rearrange("p (h c) -> p h c", h=heads)[:, :, 0:1], -BIG))
                for row, col in ((a0, 0), (b0, 0), (a1, m - 1), (b1, m - 1)):
                    did(vec.memset(row[:, col:col + 1], -BIG))
                did(vec.tensor_tensor(a0[:, 1:m], whole[:, 0:m - 1], joint[:, 1:m], ALU.add))
                did(vec.tensor_tensor(b0[:, 1:m], tail_top[:, 0:m - 1], joint[:, 1:m], ALU.add))
                did(vec.tensor_tensor(a1[:, 0:m - 1], whole[:, 1:m], joint[:, 1:m], ALU.add))
                did(vec.tensor_tensor(b1[:, 0:m - 1], head_top[:, 1:m], joint[:, 1:m], ALU.add))
                did(vec.tensor_tensor_scan(before, a0, b0, -BIG, ALU.add, ALU.max))
                did(vec.tensor_tensor_scan(after[:, ::-1], a1[:, ::-1], b1[:, ::-1], -BIG, ALU.add, ALU.max))
                signal(seg_dve)
                dve.wait_ge(seg_small, 2 * n + 2)
                did(vec.tensor_copy(chunk_col[0:m, 0:2], ps[0:m, 1, 0:2]))
                for k in range(2):
                    did(vec.tensor_scalar(gap[:, 0:L], dst[:, 0:L], chunk_col[0:m, 2 + k:3 + k], -BIG,
                                          ALU.not_equal, ALU.mult))
                    did(vec.scalar_tensor_tensor(top[:, 0:L], gap[:, 0:L], chunk_col[0:m, k:k + 1], top[:, 0:L],
                                                 ALU.add, ALU.max))
                did(vec.tensor_tensor(score[:, 0:L], score[:, 0:L], top[:, 0:L], ALU.subtract))
                signal(seg_dve)
                end()

            regs = [dve.alloc_register(f"dve_block{g}") for g in range(GROUP)]

            def sums(n, name, heads, width, nth_pass):
                begin(dve, name, ["pe", "act"])
                ring, turns, rest = RINGS[nth_pass], (GROUPS - 1) // RINGS[nth_pass], (GROUPS - 1) % RINGS[nth_pass] + 1
                did(vec.memset(weighted[:, :, :, DEG:AW], 1.0))
                if n < 2:
                    dve.wait_ge(acc_cleared, n + 1)
                dve.sem_inc(sum_added, GROUP)

                def build(u, s, k, peeled=False):
                    z, i = s % 2, k % 4 * 2
                    first = u * (ring * GROUP) + s * GROUP
                    if k == 0:
                        dve.wait_ge(gathered[s], u * (16 * GROUP) + ((uses(nth_pass, s) + 1) * 16 * GROUP))
                        if not peeled:
                            dve.wait_ge(sum_mm, u * (ring * GROUP) + (s * GROUP - GROUP + n * ITEMS))
                    if k == 0:
                        vec.tensor_copy(weighted[:, z, :, D:D + heads], by_item(heads)[:, bass.ds(first, GROUP), :])
                    if k < 4:
                        share = by_item(heads)[:, bass.ds(first + i, 2), :]
                        done = vec.tensor_tensor(weighted[:, z, i:i + 2, 0:D].rearrange("p i (h d) -> p i h d", h=heads),
                                                 row_slots[s][:, i:i + 2].rearrange("p i (h d) -> p i h d", h=heads),
                                                 share.unsqueeze(3).broadcast_to([P, 2, heads, D // heads]), ALU.mult)
                    else:
                        done = vec.tensor_tensor(
                            onehot[:, z, i:i + 2], iota_free[:, 0:P].unsqueeze(1).broadcast_to([P, 2, P]),
                            block_dst[:, bass.ds(first + i, 2)].unsqueeze(2).broadcast_to([P, 2, P]), ALU.is_equal)
                    if k == 7:
                        done.then_inc(weighted_made, 1)

                def add(u, s, then_build):
                    dve.wait_ge(weighted_made, u * ring + (s + 1 + n * GROUPS))
                    dve.sem_inc(slot_used[s], 1)
                    after = (u + (s + 1) // ring, (s + 1) % ring)
                    if then_build:
                        for k in range(2):
                            build(*after, k)
                    dve.load(regs, block_i[0:1, bass.ds(u * (ring * GROUP) + s * GROUP, GROUP)])
                    bs = [dve.snap(r, min_val=0, max_val=BLOCKS - 1) for r in regs]
                    for g in range(GROUP):
                        i = s * GROUP + g
                        dve.wait_ge(sum_mm, u * (ring * GROUP) + (i + 1 + n * ITEMS))
                        dve.wait_ge(sum_added, u * (ring * GROUP) + (i + GROUP + n * (ITEMS + GROUP)))
                        to = acc[:, bass.ds(bs[g], 1), 0:width].rearrange("p a d -> p (a d)")
                        vec.tensor_tensor(to, to, ps[:, g, 0:width], ALU.add).then_inc(sum_added, 1)
                        if then_build and g < 6:
                            build(*after, g + 2)

                for k in range(8):
                    build(0, 0, k, peeled=True)
                with vec.Fori(0, turns) as u:
                    for s in range(ring):
                        add(u, s, True)
                for s in range(rest):
                    add(turns, s, s + 1 < rest)
                dve.wait_ge(sum_added, (n + 1) * (ITEMS + GROUP))
                end()

            def inverses(heads):
                did(vec.tensor_scalar(inv_sum[:, :, 0:heads], acc[:, :, D:D + heads], 0.5, None, ALU.max))
                did(vec.reciprocal(inv_sum[:, :, 0:heads], inv_sum[:, :, 0:heads]))
                did(vec.tensor_scalar(inv_deg, deg[:], 1.0, None, ALU.max))
                did(vec.reciprocal(inv_deg, inv_deg))

            def mean_rows(t, j, heads):
                did(vec.tensor_tensor(h_n[:, j].rearrange("p (h d) -> p h d", h=heads),
                                      block_of(acc, t, j)[:, 0, 0:D].rearrange("p (h d) -> p h d", h=heads),
                                      block_of(inv_sum, t, j)[:, 0, 0:heads].unsqueeze(2).broadcast_to(
                                          [P, heads, D // heads]), ALU.mult))

            def slot_free(t, j, before):
                if not early(t, j, UB):
                    dve.wait_ge(t_made, nth_block(t, j, before, 1 - UB))

            gat_scores(0, "score1", H1, own_onehots=False)
            soft(0, "soft1", H1, P // H1, 0)
            sums(0, "sum1", H1, AW, 0)

            begin(dve, "node2", ["pe", "act"])
            attention_columns(1, 7, H2)
            did(vec.tensor_copy(deg[:].unsqueeze(2), acc[:, :, DEG:AW]))
            inverses(H1)

            def node2_rows(t, j):
                slot_free(t, j, 0)
                mean_rows(t, j, H1)
                vec.scalar_tensor_tensor(h_n[:, j], block_of(base, t, j)[:, 0], inv_deg[:, bass.ds(t * UB + j, 1)],
                                         h_n[:, j], ALU.mult, ALU.add).then_inc(h_made, 1)

            pipeline(vec.Fori, [(0, node2_rows), (2, residual(1))], step, 1)
            dve.wait_ge(node_dve, 2 * BLOCKS)
            end()

            gat_scores(1, "score2", H2, own_onehots=True)
            soft(1, "soft2", H2, ITEMS // 4, H1)
            sums(1, "sum2", H2, D + H2, 1)

            begin(dve, "node3", ["pe", "act"])
            dve.wait_ge(weights_in[2], 9 * 16)
            inverses(H2)
            split([bias_split[:, k] for k in range(3)], bias_row[:], bias_row[:])
            signal(bias_made)

            def node3_rows(t, j, k):
                row, stats = h_n[:, j], small[:, j, 0:6]
                if k == 0:
                    slot_free(t, j, 1)
                    dve.wait_ge(x_loaded[j], (t + (2 * BTURNS + 1)) * 16)
                    return vec.scalar_tensor_tensor(row, block_of(acc, t, j)[:, 0, 0:D], block_of(inv_sum, t, j)[:, 0, 0:1],
                                                    x_n[:, j], ALU.mult, ALU.add)
                if k == 1:
                    signal(x_used)
                    return vec.scalar_tensor_tensor(row, block_of(base, t, j)[:, 0], inv_deg[:, bass.ds(t * UB + j, 1)],
                                                    row, ALU.mult, ALU.add)
                if k == 2:
                    return vec.tensor_tensor(row, row, bias_all[:, 0, :], ALU.add)
                if k == 3:
                    return vec.bn_stats(stats, row)
                signal(stats_made)
                return vec.bn_aggr(small[:, j, 6:8], stats).then_inc(variance[0], 1)

            def query_copies(t, j, k):
                factor = float(R) ** -0.5
                got, rest = ps[:, product_bank(j), 0:D], tmp_n[:, j]
                parts = [query_parts[:, i, bass.ds(t * UB + j, 1), :][:, 0] for i in range(3)]
                if k == 0:
                    dve.wait_ge(node_act, nth_block(t, j, 2, 1))
                    return vec.tensor_scalar(parts[0], got, factor, None, ALU.mult)
                if k == 1:
                    return vec.scalar_tensor_tensor(rest, got, factor, parts[0], ALU.mult, ALU.subtract)
                if k == 2:
                    signal(node_dve)
                    return vec.tensor_scalar(parts[1], rest, 1.0, None, ALU.mult)
                return vec.tensor_tensor(parts[2], rest, parts[1], ALU.subtract)

            def node3_iteration(t, j):
                edge = isinstance(t, int)
                i = t * UB + j if edge else None
                rows_too, norm_too, queries_too = (
                    not edge or 0 <= i - lag < BLOCKS for lag in (0, 1, 4))
                tn, jn, tq, jq = t + (j - 1) // UB, (j - 1) % UB, t + (j - 4) // UB, (j - 4) % UB
                inverse = small[:, jn, 9:10]

                def row_step(k, lag):
                    if rows_too:
                        if k:
                            all_but(0 if edge else lag)
                        ins = node3_rows(t, j, k)
                        if k < 4:
                            then(ins)

                def query_step(k):
                    if queries_too:
                        if k:
                            all_but(0 if edge else 1)
                        then(query_copies(tq, jq, k))

                row_step(0, 0)
                query_step(0)
                row_step(1, 1)
                query_step(1)
                if norm_too:
                    dve.wait_ge(deviated[0], nth_block(tn, jn, 0, 1))
                    then(vec.reciprocal(inverse, small[:, jn, 8:9]))
                row_step(2, 2)
                if norm_too:
                    all_but(0 if edge else 1)
                    vec.tensor_scalar(h_n[:, jn], h_n[:, jn], small[:, jn, 6:7], inverse, ALU.subtract,
                                      ALU.mult).then_inc(h_made, 1)
                query_step(2)
                row_step(3, 1)
                query_step(3)
                row_step(4, 1)

            for j in range(UB):
                node3_iteration(0, j)
            with vec.Fori(0, BTURNS - 1) as t:
                step.enter(t, UB * 9)
                for j in range(UB):
                    node3_iteration(t + 1, j)
                step.leave(BTURNS - 1)
            for j in range(4):
                node3_iteration(BTURNS, j)
            dve.wait_ge(node_dve, 3 * BLOCKS)
            end()

            pair_scores(2, "score3")
            soft(2, "soft3", H3, P // H3, H1 + H2)
            sums(2, "sum3", H3, D + H3, 3)

            begin(dve, "final", ["pe", "act"])
            dve.wait_ge(weights_in[3], 4 * 16)
            inverses(H3)
            did(vec.tensor_scalar(inv_deg, deg[:], 0.5, None, ALU.is_lt))
            split([bias_split[:, k, 0:D] for k in range(3)], bias_row[:, 0:D], bias_row[:, 0:D])
            signal(bias_made)

            def final_iteration(t, j):
                edge = isinstance(t, int)
                i = t * UB + j if edge else None
                rows_too, sums_too, inner_too, outer_too = (
                    not edge or 0 <= i - lag < BLOCKS for lag in (0, 2, 3, 4))
                (ta, ja), (tc, jc), (td, jd) = ((t + (j - lag) // UB, (j - lag) % UB) for lag in (2, 3, 4))
                row = tmp_n[:, jc]
                inner_inverse, outer_inverse = small[:, jc, 9:10], small[:, jd, 25:26]

                def after(lag):
                    all_but(0 if edge else lag)

                if rows_too:
                    slot_free(t, j, 2)
                    then(vec.tensor_tensor(h_n[:, j].rearrange("p (h d) -> p h d", h=H3),
                                           block_of(acc, t, j)[:, 0, 0:D].rearrange("p (h d) -> p h d", h=H3),
                                           block_of(inv_sum, t, j)[:, 0, 0:H3].unsqueeze(2).broadcast_to([P, H3, R]),
                                           ALU.mult))
                if sums_too:
                    dve.wait_ge(node_mm, nth_block(ta, ja, 3, 1))
                    then(vec.tensor_tensor(tmp_n[:, ja:ja + 1], ps[:, product_bank(ja), 0:D].unsqueeze(1),
                                           block_of(base, ta, ja), ALU.add))
                if inner_too:
                    dve.wait_ge(deviated[0], nth_block(tc, jc, 1, 1))
                    then(vec.reciprocal(inner_inverse, small[:, jc, 8:9]))
                if rows_too:
                    after(2)
                    dve.wait_ge(x_loaded[j], (t + (3 * BTURNS + 1)) * 16)
                    vec.scalar_tensor_tensor(h_n[:, j], stage[:, j, 1, :], inv_deg[:, bass.ds(t * UB + j, 1)],
                                             h_n[:, j], ALU.mult, ALU.add).then_inc(h_made, 1)
                if inner_too:
                    after(0)
                    then(vec.scalar_tensor_tensor(row, row, small[:, jc, 6:7], bias_all[:, 0, :],
                                                  ALU.subtract, ALU.mult))
                if sums_too:
                    after(1)
                    signal(node_dve)
                    then(vec.bn_stats(small[:, ja, 0:6], tmp_n[:, ja]))
                if inner_too:
                    after(1)
                    then(vec.scalar_tensor_tensor(row, row, inner_inverse, bias_all[:, 1, :], ALU.mult, ALU.add))
                if rows_too:
                    dve.wait_ge(h_made, nth_block(t, j, 2, 1))
                    signal(x_used)
                if sums_too:
                    after(1)
                    signal(stats_made)
                    vec.bn_aggr(small[:, ja, 6:8], small[:, ja, 0:6]).then_inc(variance[0], 1)
                if inner_too:
                    after(0)
                    then(vec.tensor_tensor(tmp_n[:, jc:jc + 1], tmp_n[:, jc:jc + 1], block_of(base, tc, jc), ALU.add))
                if outer_too:
                    dve.wait_ge(deviated[1], nth_block(td, jd, 0, 1))
                    then(vec.reciprocal(outer_inverse, small[:, jd, 24:25]))
                if inner_too:
                    after(1)
                    then(vec.bn_stats(small[:, jc, 16:22], row))
                if outer_too:
                    after(1)
                    dve.wait_ge(node_stored[jd], td * 16 + 16 * 4 * BTURNS)
                    vec.tensor_scalar(stage[:, jd, 0, :], tmp_n[:, jd], small[:, jd, 22:23], outer_inverse,
                                      ALU.subtract, ALU.mult).then_inc(out_made, 1)
                if inner_too:
                    after(0)
                    signal(stats_made)
                    vec.bn_aggr(small[:, jc, 22:24], small[:, jc, 16:22]).then_inc(variance[1], 1)

            for j in range(UB):
                final_iteration(0, j)
            with vec.Fori(0, BTURNS - 1) as t:
                step.enter(t, UB * 9)
                for j in range(UB):
                    final_iteration(t + 1, j)
                step.leave(BTURNS - 1)
            for j in range(4):
                final_iteration(BTURNS, j)


def kernel(**inputs):
    import concourse.bacc as bacc
    from concourse.bass_utils import run_bass_kernel_spmd

    def rows_of(v):
        return np.ascontiguousarray(v).reshape(1, -1)

    x = np.zeros((NP, D), inputs["x"].dtype)
    x[0:N] = inputs["x"]
    arrays = {"x": x, "x_t": np.ascontiguousarray(x.T)}
    for k in ("src", "dst", "edge_type_64"):
        arrays[k] = np.ascontiguousarray(inputs[k])
    for k in ("fc1_w", "fc2_w", "wb0", "wb1"):
        arrays[k.replace("_w", "") + "_t"] = np.ascontiguousarray(np.transpose(inputs["L0_gnn_" + k]))
    arrays["bias1"] = np.ascontiguousarray(np.reshape(inputs["L0_gnn_bias1"], (2, P)).T)
    for k in ("attn_l1", "attn_r1", "attn_l2", "attn_r2", "bias2", "bb0", "bb1"):
        arrays[k] = rows_of(inputs["L0_gnn_" + k])
    for k in ("Wq", "Wk", "Wv", "Wo"):
        arrays[k.lower()] = np.ascontiguousarray(inputs["L1_gnn_" + k])
    for k in ("bq", "bk", "bv", "bo", "gamma", "beta"):
        arrays[k] = rows_of(inputs["L1_gnn_" + k])
    arrays["query"] = np.ascontiguousarray(np.reshape(inputs["L1_gnn_query_emb"], (2, P)).T)
    arrays["rel"] = np.ascontiguousarray(inputs["L1_gnn_rel_w"])

    nc = bacc.Bacc("TRN2", target_bir_lowering=False, num_devices=1)
    a = {k: nc.dram_tensor("in_" + k, v.shape, mybir.dt.from_np(v.dtype), kind="ExternalInput").ap()
         for k, v in arrays.items()}
    out = nc.dram_tensor("out", (N, D), F32, kind="ExternalOutput").ap()
    graph_layers(nc, a, out)
    r = run_bass_kernel_spmd(nc, [{"in_" + k: v for k, v in arrays.items()}], core_ids=[0])
    return r.results[0]["out"]
```
